# Optimizing a Trainium2 kernel written in Bass

```python
import numpy as np
import jax
import jax.numpy as jnp

def _softmax(x, axis=-1):
    return jax.nn.softmax(x, axis=axis)

def _gelu(x):
    return jax.nn.gelu(x, approximate=True)

def _silu(x):
    return jax.nn.silu(x)

def _sigmoid(x):
    return jax.nn.sigmoid(x)

def _layernorm(x, axis=-1, eps=1e-05):
    m = jnp.mean(x, axis=axis, keepdims=True)
    v = jnp.var(x, axis=axis, keepdims=True)
    return (x - m) / jnp.sqrt(v + eps)

def _scatter_add(tgt, idx, src, axis=0):
    return tgt.at[idx].add(src)

def _segment_sum(src, seg, n):
    return jax.ops.segment_sum(src, seg, n)
kernel_name = 'mk_macaron_d2_jaxref_r8_52205c'

def setup_inputs(seed: int=0):
    np.random.seed(seed)
    _w = jnp.asarray

    def _L0_attn_setup():
        import jax, jax.numpy as jnp
        import numpy as np
        B, T, D = (2, 256, 512)
        H = 32
        HKV = 1
        HD = D // H
        key = jax.random.key(seed)
        ks = jax.random.split(key, 9)
        s = lambda fan_in: 1.0 / np.sqrt(fan_in)
        return {'x': jax.random.normal(ks[0], (B, T, D), dtype=jnp.float32), 'wq_w': jax.random.normal(ks[1], (H * HD, D), dtype=jnp.float32) * s(D), 'wq_b': jax.random.normal(ks[2], (H * HD,), dtype=jnp.float32) * 0.02, 'wk_w': jax.random.normal(ks[3], (HKV * HD, D), dtype=jnp.float32) * s(D), 'wk_b': jax.random.normal(ks[4], (HKV * HD,), dtype=jnp.float32) * 0.02, 'wv_w': jax.random.normal(ks[5], (HKV * HD, D), dtype=jnp.float32) * s(D), 'wv_b': jax.random.normal(ks[6], (HKV * HD,), dtype=jnp.float32) * 0.02, 'wo_w': jax.random.normal(ks[7], (D, H * HD), dtype=jnp.float32) * s(H * HD), 'wo_b': jax.random.normal(ks[8], (D,), dtype=jnp.float32) * 0.02}
    _L0_attn_in = _L0_attn_setup()

    def _L0_ffn_setup():
        import jax, jax.numpy as jnp
        import numpy as np
        BS = 128
        FP8_MAX = 448.0

        def act_quant(x):
            T, K = x.shape
            xb = x.reshape(T, K // BS, BS)
            amax = jnp.max(jnp.abs(xb), axis=-1)
            scale = amax / FP8_MAX + 1e-12
            xq = (xb / scale[:, :, None]).reshape(T, K)
            return (xq, scale)

        def linear_dsv3(x, wq, w_scale):
            T, K = x.shape
            N = wq.shape[0]
            xq, xs = act_quant(x)
            xdq = (xq.reshape(T, K // BS, BS) * xs[:, :, None]).reshape(T, K)
            wdq = (wq.reshape(N // BS, BS, K // BS, BS) * w_scale[:, None, :, None]).reshape(N, K)
            return xdq @ wdq.T
        key = jax.random.key(seed)
        ks = jax.random.split(key, 4)
        DIM, INTER = (512, 1792)

        def make_qweight(k, n, m):
            w = jax.random.normal(k, (n, m), dtype=jnp.float32) * 0.02
            wb = w.reshape(n // BS, BS, m // BS, BS)
            amax = jnp.max(jnp.abs(wb), axis=(1, 3))
            scale = amax / FP8_MAX + 1e-12
            wq = (wb / scale[:, None, :, None]).reshape(n, m)
            return (wq, scale)
        x = jax.random.normal(ks[0], (2, 128, DIM), dtype=jnp.float32)
        w1, w1_scale = make_qweight(ks[1], INTER, DIM)
        w3, w3_scale = make_qweight(ks[2], INTER, DIM)
        w2, w2_scale = make_qweight(ks[3], DIM, INTER)
        return {'x': x, 'w1': w1, 'w1_scale': w1_scale, 'w3': w3, 'w3_scale': w3_scale, 'w2': w2, 'w2_scale': w2_scale}
    _L0_ffn_in = _L0_ffn_setup()

    def _L1_attn_setup():
        import jax, jax.numpy as jnp
        import numpy as np
        import math
        HIDDEN = 512
        N_HEADS = 32
        N_KV_HEADS = 8
        HEAD_DIM = HIDDEN // N_HEADS
        GROUPS = N_HEADS // N_KV_HEADS
        ROPE_THETA = 10000.0
        TOKEN_BUDGET = 128
        INIT_BUDGET = 128
        RECENT_BUDGET = 128
        CHUNK = 16
        B, S = (1, 256)

        def _rotate_half(x):
            x1, x2 = jnp.split(x, 2, axis=-1)
            return jnp.concatenate([-x2, x1], axis=-1)

        def _rope(seq_len, dtype):
            inv_freq = 1.0 / ROPE_THETA ** (jnp.arange(0, HEAD_DIM, 2, dtype=jnp.float32) / HEAD_DIM)
            freqs = jnp.arange(seq_len, dtype=jnp.float32)[:, None] * inv_freq[None, :]
            emb = jnp.concatenate([freqs, freqs], axis=-1)
            return (jnp.cos(emb).astype(dtype), jnp.sin(emb).astype(dtype))
        key = jax.random.key(seed)
        ks = jax.random.split(key, 5)
        sc = 0.02
        return {'hidden_states': jax.random.normal(ks[0], (B, S, HIDDEN), dtype=jnp.float32), 'wq': jax.random.normal(ks[1], (N_HEADS * HEAD_DIM, HIDDEN), dtype=jnp.float32) * sc, 'wk': jax.random.normal(ks[2], (N_KV_HEADS * HEAD_DIM, HIDDEN), dtype=jnp.float32) * sc, 'wv': jax.random.normal(ks[3], (N_KV_HEADS * HEAD_DIM, HIDDEN), dtype=jnp.float32) * sc, 'wo': jax.random.normal(ks[4], (HIDDEN, N_HEADS * HEAD_DIM), dtype=jnp.float32) * sc}
    _L1_attn_in = _L1_attn_setup()

    def _L1_ffn_setup():
        import jax, jax.numpy as jnp
        import numpy as np
        BS = 128
        FP8_MAX = 448.0

        def act_quant(x):
            T, K = x.shape
            xb = x.reshape(T, K // BS, BS)
            amax = jnp.max(jnp.abs(xb), axis=-1)
            scale = amax / FP8_MAX + 1e-12
            xq = (xb / scale[:, :, None]).reshape(T, K)
            return (xq, scale)

        def linear_dsv3(x, wq, w_scale):
            T, K = x.shape
            N = wq.shape[0]
            xq, xs = act_quant(x)
            xdq = (xq.reshape(T, K // BS, BS) * xs[:, :, None]).reshape(T, K)
            wdq = (wq.reshape(N // BS, BS, K // BS, BS) * w_scale[:, None, :, None]).reshape(N, K)
            return xdq @ wdq.T
        key = jax.random.key(seed)
        ks = jax.random.split(key, 4)
        DIM, INTER = (512, 1792)

        def make_qweight(k, n, m):
            w = jax.random.normal(k, (n, m), dtype=jnp.float32) * 0.02
            wb = w.reshape(n // BS, BS, m // BS, BS)
            amax = jnp.max(jnp.abs(wb), axis=(1, 3))
            scale = amax / FP8_MAX + 1e-12
            wq = (wb / scale[:, None, :, None]).reshape(n, m)
            return (wq, scale)
        x = jax.random.normal(ks[0], (2, 128, DIM), dtype=jnp.float32)
        w1, w1_scale = make_qweight(ks[1], INTER, DIM)
        w3, w3_scale = make_qweight(ks[2], INTER, DIM)
        w2, w2_scale = make_qweight(ks[3], DIM, INTER)
        return {'x': x, 'w1': w1, 'w1_scale': w1_scale, 'w3': w3, 'w3_scale': w3_scale, 'w2': w2, 'w2_scale': w2_scale}
    _L1_ffn_in = _L1_ffn_setup()
    _d = {'L0_attn_x': _L0_attn_in['x'], 'L0_attn_wq_w': _L0_attn_in['wq_w'], 'L0_attn_wq_b': _L0_attn_in['wq_b'], 'L0_attn_wk_w': _L0_attn_in['wk_w'], 'L0_attn_wk_b': _L0_attn_in['wk_b'], 'L0_attn_wv_w': _L0_attn_in['wv_w'], 'L0_attn_wv_b': _L0_attn_in['wv_b'], 'L0_attn_wo_w': _L0_attn_in['wo_w'], 'L0_attn_wo_b': _L0_attn_in['wo_b'], 'L0_ffn_w1': _L0_ffn_in['w1'], 'L0_ffn_w1_scale': _L0_ffn_in['w1_scale'], 'L0_ffn_w3': _L0_ffn_in['w3'], 'L0_ffn_w3_scale': _L0_ffn_in['w3_scale'], 'L0_ffn_w2': _L0_ffn_in['w2'], 'L0_ffn_w2_scale': _L0_ffn_in['w2_scale'], 'L1_attn_wq': _L1_attn_in['wq'], 'L1_attn_wk': _L1_attn_in['wk'], 'L1_attn_wv': _L1_attn_in['wv'], 'L1_attn_wo': _L1_attn_in['wo'], 'L1_ffn_w1': _L1_ffn_in['w1'], 'L1_ffn_w1_scale': _L1_ffn_in['w1_scale'], 'L1_ffn_w3': _L1_ffn_in['w3'], 'L1_ffn_w3_scale': _L1_ffn_in['w3_scale'], 'L1_ffn_w2': _L1_ffn_in['w2'], 'L1_ffn_w2_scale': _L1_ffn_in['w2_scale']}
    _x0 = _d['L0_attn_x']
    _d['L0_attn_x'] = jax.random.normal(jax.random.fold_in(jax.random.key(seed), 1), (1, 1024, 512), dtype=_x0.dtype)
    del _x0
    return _d

def reference(L0_attn_x, L0_attn_wq_w, L0_attn_wq_b, L0_attn_wk_w, L0_attn_wk_b, L0_attn_wv_w, L0_attn_wv_b, L0_attn_wo_w, L0_attn_wo_b, L0_ffn_w1, L0_ffn_w1_scale, L0_ffn_w3, L0_ffn_w3_scale, L0_ffn_w2, L0_ffn_w2_scale, L1_attn_wq, L1_attn_wk, L1_attn_wv, L1_attn_wo, L1_ffn_w1, L1_ffn_w1_scale, L1_ffn_w3, L1_ffn_w3_scale, L1_ffn_w2, L1_ffn_w2_scale):

    def _L0_attn_ref(x, wq_w, wq_b, wk_w, wk_b, wv_w, wv_b, wo_w, wo_b):
        import jax, jax.numpy as jnp
        import numpy as np
        B, T, D = (2, 256, 512)
        H = 32
        HKV = 1
        HD = D // H
        b, t, d = x.shape
        q = (x @ wq_w.T + wq_b).reshape(b, t, H, HD)
        k = (x @ wk_w.T + wk_b).reshape(b, t, HKV, HD)
        v = (x @ wv_w.T + wv_b).reshape(b, t, HKV, HD)
        k1 = k[:, :, 0, :]
        v1 = v[:, :, 0, :]
        scores = jnp.einsum('bqhd,bkd->bhqk', q, k1) / jnp.sqrt(jnp.float32(HD))
        causal = jnp.tril(jnp.ones((t, t), dtype=bool))
        scores = jnp.where(causal, scores, -jnp.inf)
        weights = jax.nn.softmax(scores, axis=-1)
        attn = jnp.einsum('bhqk,bkd->bqhd', weights, v1)
        attn = attn.reshape(b, t, H * HD)
        return attn @ wo_w.T + wo_b

    def _L0_ffn_ref(x, w1, w1_scale, w3, w3_scale, w2, w2_scale):
        import jax, jax.numpy as jnp
        import numpy as np
        BS = 128
        FP8_MAX = 448.0

        def act_quant(x):
            T, K = x.shape
            xb = x.reshape(T, K // BS, BS)
            amax = jnp.max(jnp.abs(xb), axis=-1)
            scale = amax / FP8_MAX + 1e-12
            xq = (xb / scale[:, :, None]).reshape(T, K)
            return (xq, scale)

        def linear_dsv3(x, wq, w_scale):
            T, K = x.shape
            N = wq.shape[0]
            xq, xs = act_quant(x)
            xdq = (xq.reshape(T, K // BS, BS) * xs[:, :, None]).reshape(T, K)
            wdq = (wq.reshape(N // BS, BS, K // BS, BS) * w_scale[:, None, :, None]).reshape(N, K)
            return xdq @ wdq.T
        B, S, D = x.shape
        xf = x.reshape(-1, D)
        g = linear_dsv3(xf, w1, w1_scale)
        u = linear_dsv3(xf, w3, w3_scale)
        h = jax.nn.silu(g) * u
        y = linear_dsv3(h, w2, w2_scale)
        return y.reshape(B, S, D)

    def _L1_attn_ref(hidden_states, wq, wk, wv, wo):
        import jax, jax.numpy as jnp
        import numpy as np
        import math
        HIDDEN = 512
        N_HEADS = 32
        N_KV_HEADS = 8
        HEAD_DIM = HIDDEN // N_HEADS
        GROUPS = N_HEADS // N_KV_HEADS
        ROPE_THETA = 10000.0
        TOKEN_BUDGET = 128
        INIT_BUDGET = 128
        RECENT_BUDGET = 128
        CHUNK = 16
        B, S = (1, 256)

        def _rotate_half(x):
            x1, x2 = jnp.split(x, 2, axis=-1)
            return jnp.concatenate([-x2, x1], axis=-1)

        def _rope(seq_len, dtype):
            inv_freq = 1.0 / ROPE_THETA ** (jnp.arange(0, HEAD_DIM, 2, dtype=jnp.float32) / HEAD_DIM)
            freqs = jnp.arange(seq_len, dtype=jnp.float32)[:, None] * inv_freq[None, :]
            emb = jnp.concatenate([freqs, freqs], axis=-1)
            return (jnp.cos(emb).astype(dtype), jnp.sin(emb).astype(dtype))
        b, s, _ = hidden_states.shape
        dtype = hidden_states.dtype
        NEG = jnp.finfo(dtype).min
        q = (hidden_states @ wq.T).reshape(b, s, N_HEADS, HEAD_DIM).transpose(0, 2, 1, 3)
        k = (hidden_states @ wk.T).reshape(b, s, N_KV_HEADS, HEAD_DIM).transpose(0, 2, 1, 3)
        v = (hidden_states @ wv.T).reshape(b, s, N_KV_HEADS, HEAD_DIM).transpose(0, 2, 1, 3)
        cos, sin = _rope(s, dtype)
        q = q * cos[None, None] + _rotate_half(q) * sin[None, None]
        k = k * cos[None, None] + _rotate_half(k) * sin[None, None]
        k = jnp.repeat(k, GROUPS, axis=1)
        v = jnp.repeat(v, GROUPS, axis=1)
        scores = jnp.einsum('bhqd,bhkd->bhqk', q, k) / math.sqrt(HEAD_DIM)
        q_pos = jnp.arange(s)[:, None]
        k_pos = jnp.arange(s)[None, :]
        causal = k_pos <= q_pos
        masked = jnp.where(causal[None, None], scores, NEG)
        pad = -s % CHUNK
        padded = jnp.pad(masked, ((0, 0), (0, 0), (0, 0), (0, pad)), constant_values=NEG)
        n_chunks = (s + pad) // CHUNK
        chunk_max = padded.reshape(b, N_HEADS, s, n_chunks, CHUNK).max(axis=-1)
        k_top = min(max(3, TOKEN_BUDGET // CHUNK), n_chunks)
        _, topk_idx = jax.lax.top_k(chunk_max, k_top)
        chunk_mask = jnp.any(topk_idx[..., None] == jnp.arange(n_chunks), axis=-2)
        tok_mask = jnp.repeat(chunk_mask, CHUNK, axis=-1)[..., :s]
        init_mask = k_pos < INIT_BUDGET
        recent_mask = k_pos > q_pos - RECENT_BUDGET
        allowed = causal[None, None] & (tok_mask | init_mask[None, None] | recent_mask[None, None])
        final = jnp.where(allowed, scores, NEG)
        attn = jax.nn.softmax(final, axis=-1)
        out = jnp.einsum('bhqk,bhkd->bhqd', attn, v)
        out = out.transpose(0, 2, 1, 3).reshape(b, s, N_HEADS * HEAD_DIM)
        return out @ wo.T

    def _L1_ffn_ref(x, w1, w1_scale, w3, w3_scale, w2, w2_scale):
        import jax, jax.numpy as jnp
        import numpy as np
        BS = 128
        FP8_MAX = 448.0

        def act_quant(x):
            T, K = x.shape
            xb = x.reshape(T, K // BS, BS)
            amax = jnp.max(jnp.abs(xb), axis=-1)
            scale = amax / FP8_MAX + 1e-12
            xq = (xb / scale[:, :, None]).reshape(T, K)
            return (xq, scale)

        def linear_dsv3(x, wq, w_scale):
            T, K = x.shape
            N = wq.shape[0]
            xq, xs = act_quant(x)
            xdq = (xq.reshape(T, K // BS, BS) * xs[:, :, None]).reshape(T, K)
            wdq = (wq.reshape(N // BS, BS, K // BS, BS) * w_scale[:, None, :, None]).reshape(N, K)
            return xdq @ wdq.T
        B, S, D = x.shape
        xf = x.reshape(-1, D)
        g = linear_dsv3(xf, w1, w1_scale)
        u = linear_dsv3(xf, w3, w3_scale)
        h = jax.nn.silu(g) * u
        y = linear_dsv3(h, w2, w2_scale)
        return y.reshape(B, S, D)
    x = L0_attn_x
    x = x + 0.5 * _L0_ffn_ref(_layernorm(x, axis=-1), L0_ffn_w1, L0_ffn_w1_scale, L0_ffn_w3, L0_ffn_w3_scale, L0_ffn_w2, L0_ffn_w2_scale)
    x = x + _L0_attn_ref(_layernorm(x, axis=-1), L0_attn_wq_w, L0_attn_wq_b, L0_attn_wk_w, L0_attn_wk_b, L0_attn_wv_w, L0_attn_wv_b, L0_attn_wo_w, L0_attn_wo_b)
    x = x + 0.5 * _L0_ffn_ref(_layernorm(x, axis=-1), L0_ffn_w1, L0_ffn_w1_scale, L0_ffn_w3, L0_ffn_w3_scale, L0_ffn_w2, L0_ffn_w2_scale)
    x = x + 0.5 * _L1_ffn_ref(_layernorm(x, axis=-1), L1_ffn_w1, L1_ffn_w1_scale, L1_ffn_w3, L1_ffn_w3_scale, L1_ffn_w2, L1_ffn_w2_scale)
    x = x + _L1_attn_ref(_layernorm(x, axis=-1), L1_attn_wq, L1_attn_wk, L1_attn_wv, L1_attn_wo)
    x = x + 0.5 * _L1_ffn_ref(_layernorm(x, axis=-1), L1_ffn_w1, L1_ffn_w1_scale, L1_ffn_w3, L1_ffn_w3_scale, L1_ffn_w2, L1_ffn_w2_scale)
    return x

_drawn_inputs = setup_inputs


def setup_inputs(seed=0):
    import zlib

    import numpy as np

    out = dict(_drawn_inputs(seed))
    spreads = {}
    factors = {'L0_attn_wq_b': 64.0,
     'L0_attn_wk_b': 64.0,
     'L0_attn_wv_b': 23.608,
     'L0_attn_wo_b': 23.56,
     'L0_ffn_w1_scale': 6.923,
     'L0_ffn_w3_scale': 6.834,
     'L0_ffn_w2_scale': 8.0,
     'L1_attn_wq': 64.0,
     'L1_attn_wk': 64.0,
     'L1_ffn_w1_scale': 7.096,
     'L1_ffn_w3_scale': 7.003,
     'L1_ffn_w2_scale': 8.0,
     'L0_attn_wq_w': 8.0,
     'L0_attn_wk_w': 8.0,
     'L0_attn_wv_w': 7.321,
     'L0_attn_wo_w': 6.792,
     'L1_attn_wv': 8.0,
     'L1_attn_wo': 8.0}
    for name, (base, spread) in spreads.items():
        noise = np.random.default_rng([zlib.crc32(name.encode()), seed]).standard_normal(out[name].shape)
        drawn = base * np.exp(spread * noise) if base else spread * noise
        out[name] = jnp.asarray(drawn.astype(out[name].dtype))
    for name, factor in factors.items():
        out[name] = (out[name] * factor).astype(out[name].dtype)
    return out
```

```python
import concourse.bass as bass
from concourse import mybir
from contextlib import ExitStack

F32 = mybir.dt.float32
F32R = mybir.dt.float32r
I32 = mybir.dt.int32
BF16 = mybir.dt.bfloat16
ALU = mybir.AluOpType
ACT = mybir.ActivationFunctionType
AX = mybir.AxisListType

P = 128
T = 1024
D = 512
TT = T // P
KC = D // P
INTER = 1792
NJ = INTER // P
HALF = 512
NH = T // HALF
TH = HALF // P
EPS = 1e-5
H, HD = 32, 16
HKV1 = 8
G = 4
SR = 3 * HD
MR = 2 * SR
CHUNK = 16
NCH = T // CHUNK
MARK = 3e38
RSQRT_MAGIC = 1597463007.0


class Phase:

    def __init__(self, nc, name):
        self.nc, self.name, self.stack, self.sems = nc, name, ExitStack(), []

    def sb(self, name, shape, dt=F32):
        return self.stack.enter_context(self.nc.sbuf_tensor(f"{self.name}_{name}", shape, dt))

    def ps(self, name, shape, dt=F32):
        return self.stack.enter_context(self.nc.psum_tensor(f"{self.name}_{name}", shape, dt))

    def sem(self, name):
        self.sems.append(self.nc.alloc_semaphore(f"{self.name}_{name}"))
        return self.sems[-1]

    def close(self):
        self.nc.clear_and_free_semaphores(self.sems)
        self.nc.all_engine_barrier()
        self.stack.close()


class NormSems:

    def __init__(self, ph):
        self.stats = ph.sem("norm_stats")
        self.moments = ph.sem("norm_moments")
        self.rstd = ph.sem("norm_rstd")
        self.tile = ph.sem("norm_tile")
        self.turned = ph.sem("norm_turned")
        self.hi = ph.sem("norm_hi")
        self.lo = ph.sem("norm_lo")


def norm_vector(nc, dve, s, x, st, mv, rstd, xn, turn, xt_hi, xt_lo):
    y = rstd[:, 0, :]
    for t in range(TT):
        nc.vector.bn_stats(st[:, t, :], x[:, t, :]).then_inc(s.stats, 1)
    for t in range(TT):
        dve.wait_ge(s.stats, t + 1)
        nc.vector.bn_aggr(mv[:, t, :], st[:, t, :]).then_inc(s.moments, 1)
    dve.wait_ge(s.moments, TT)
    var, tmp = rstd[:, 1, :], rstd[:, 2, :]
    nc.vector.tensor_scalar(var, mv[:, :, 1], EPS, None, ALU.add).then_inc(s.rstd, 1)
    dve.wait_ge(s.rstd, 1)
    nc.vector.tensor_scalar(tmp.bitcast(I32), var.bitcast(I32), 1, None,
                            ALU.logical_shift_right).then_inc(s.rstd, 1)
    dve.wait_ge(s.rstd, 2)
    nc.vector.tensor_scalar(y.bitcast(I32), tmp.bitcast(I32), -1.0, RSQRT_MAGIC, ALU.mult, ALU.add).then_inc(s.rstd, 1)
    for n in range(3):
        dve.wait_ge(s.rstd, 3 + 3 * n)
        nc.vector.scalar_tensor_tensor(tmp, var, -0.5, y, ALU.mult, ALU.mult).then_inc(s.rstd, 1)
        dve.wait_ge(s.rstd, 4 + 3 * n)
        nc.vector.tensor_tensor(tmp, tmp, y, ALU.mult).then_inc(s.rstd, 1)
        dve.wait_ge(s.rstd, 5 + 3 * n)
        nc.vector.scalar_tensor_tensor(y, tmp, 1.5, y, ALU.add, ALU.mult).then_inc(s.rstd, 1)
    dve.wait_ge(s.rstd, 12)

    def lower(t):
        dve.wait_ge(s.hi, t + 1)
        nc.vector.tensor_tensor(xt_lo[:, :, t * P:(t + 1) * P], turn[t % 2][:, :, :],
                                xt_hi[:, :, t * P:(t + 1) * P].bitcast(F32), ALU.subtract).then_inc(s.lo, 1)

    for t in range(TT):
        if t >= 2:
            dve.wait_ge(s.turned, t - 1)
        nc.vector.tensor_scalar(xn[:, t % 2, :], x[:, t, :], mv[:, t, 0:1], rstd[:, 0, t:t + 1],
                                ALU.subtract, ALU.mult).then_inc(s.tile, 1)
        if t >= 1:
            lower(t - 1)
    lower(TT - 1)


def norm_scalar(nc, act, s, turn, xt_hi):
    for t in range(TT):
        act.wait_ge(s.turned, t + 1)
        nc.scalar.activation(xt_hi[:, :, t * P:(t + 1) * P], turn[t % 2][:, :, :], ACT.Copy).then_inc(s.hi, 1)


def norm_tensor(nc, pe, s, xn, ident, turn):
    for t in range(TT):
        pe.wait_ge(s.tile, t + 1)
        if t >= 2:
            pe.wait_ge(s.lo, t - 1)
        for c in range(KC):
            last = nc.tensor.transpose(turn[t % 2][:, c, :], xn[:, t % 2, c * P:(c + 1) * P], ident[:, :])
        last.then_inc(s.turned, 1)


def load_phase(nc, x, ident, ident_b, causal, x_dram):
    ph = Phase(nc, "load")
    loaded = ph.sem("loaded")
    made = ph.sem("made")
    with nc.Block() as block:
        @block.sync
        def _(sp):
            sp.dma_start(x[:, :, :], x_dram.rearrange("(t p) d -> p t d", p=P)).then_inc(loaded, 16)
            sp.wait_ge(loaded, 16)

        @block.gpsimd
        def _(pool):
            nc.gpsimd.memset(ident[:, :], 0.0).then_inc(made, 1)
            nc.gpsimd.memset(ident_b[:, :], 0.0).then_inc(made, 1)
            nc.gpsimd.memset(causal[:, :], 0.0).then_inc(made, 1)
            pool.wait_ge(made, 3)
            for m in (ident, ident_b):
                nc.gpsimd.affine_select(out=m[:, :], in_=m[:, :], compare_op=ALU.not_equal, fill=1.0,
                                        base=0, pattern=[[-1, P]], channel_multiplier=1).then_inc(made, 1)
            nc.gpsimd.affine_select(out=causal[:, :], in_=causal[:, :], compare_op=ALU.is_ge, fill=NEG,
                                    base=0, pattern=[[-1, P]], channel_multiplier=1).then_inc(made, 1)
            pool.wait_ge(made, 6)
    ph.close()


NEG = -1e36


def ffn_phase(nc, name, x, ident, w13_dram, w2_dram, scale_dram):
    ph = Phase(nc, name)
    sc = ph.sb("scales", [P, NJ, 12])
    st = ph.sb("stats", [P, TT, 6])
    mv = ph.sb("moments", [P, TT, 2])
    rstd = ph.sb("rstd", [P, 3, TT])
    xn = ph.sb("xn", [P, 2, D])
    xt_hi = ph.sb("xt_hi", [P, KC, T], F32R)
    xt_lo = ph.sb("xt_lo", [P, KC, T], F32R)
    raw13 = [ph.sb(f"raw13_{b}", [P, 8, P]) for b in range(2)]
    w13_hi = [ph.sb(f"w13_hi{b}", [P, 8, P], F32R) for b in range(2)]
    w13_lo = [ph.sb(f"w13_lo{b}", [P, 8, P], F32R) for b in range(2)]
    raw2 = [ph.sb(f"raw2_{b}", [P, 4, P]) for b in range(2)]
    w2_hi = ph.sb("w2_hi", [P, NJ, D], F32R)
    w2_lo = ph.sb("w2_lo", [P, NJ, D], F32R)
    h = ph.sb("h", [P, NJ, T])
    silu = [ph.sb(f"silu{b}", [P, HALF]) for b in range(2)]
    hs_hi = [ph.sb(f"hs_hi{b}", [P, HALF], F32R) for b in range(2)]
    hs_lo = [ph.sb(f"hs_lo{b}", [P, HALF], F32R) for b in range(2)]
    bank = [ph.ps(f"bank{b}", [P, 4, P]) for b in range(8)]
    turn = bank[4:6]
    flat = [b[:, :, :].rearrange("p a b -> p (a b)") for b in bank]
    gate, up = flat[0:2], flat[2:4]
    y = [flat[4:8], flat[0:4]]

    s = NormSems(ph)
    scales_in = ph.sem("scales_in")
    w13_in = [ph.sem(f"w13_in{b}") for b in range(2)]
    w2_in = [ph.sem(f"w2_in{b}") for b in range(2)]
    w13_scaled, w2_scaled = ph.sem("w13_scaled"), ph.sem("w2_scaled")
    w13_hi_done, w2_hi_done = ph.sem("w13_hi_done"), ph.sem("w2_hi_done")
    w13_lo_done, w2_lo_done = ph.sem("w13_lo_done"), ph.sem("w2_lo_done")
    gate_done, up_done = ph.sem("gate_done"), ph.sem("up_done")
    silu_done, h_done = ph.sem("silu_done"), ph.sem("h_done")
    hs_hi_done, hs_lo_done, hs_used = ph.sem("hs_hi_done"), ph.sem("hs_lo_done"), ph.sem("hs_used")
    y_done, x_done = ph.sem("y_done"), ph.sem("x_done")

    def over_blocks(eng, step):
        for b in range(2):
            step(0, b, True, False)
        with eng.Fori(1, NJ // 2 - 1) as i:
            for b in range(2):
                step(i, b, False, False)
        for b in range(2):
            step(NJ // 2 - 1, b, False, True)

    def part_free(eng, hf, i, b, first):
        if not first:
            eng.wait_ge(hs_used, (NJ - 1) * hf + 2 * i + b - 1)
        elif hf > 0:
            if b == 0:
                eng.wait_ge(hs_used, (NJ - 1) * hf)
            else:
                eng.wait_ge(y_done, TH * hf)

    with nc.Block() as block:
        @block.sync
        def _(sp):
            sp.dma_start(sc[:, :, :], scale_dram.to_broadcast((P, NJ, 12))).then_inc(scales_in, 16)

            def load(i, b, first, last):
                j = 2 * i + b
                if not first:
                    sp.wait_ge(w13_lo_done, j - 1)
                sp.dma_start(raw13[b][:, :, :], w13_dram[j, :, :, :]).then_inc(w13_in[b], 16)
                if not first:
                    sp.wait_ge(w2_lo_done, j - 1)
                sp.dma_start(raw2[b][:, :, :], w2_dram[j, :, :, :]).then_inc(w2_in[b], 16)
            over_blocks(sp, load)

        @block.gpsimd
        def _(pool):
            pool.wait_ge(scales_in, 16)

            def dequantise(i, b, first, last):
                j = 2 * i + b
                pool.wait_ge(w13_in[b], 16 * i + 16)
                nc.gpsimd.tensor_tensor(raw13[b][:, :, :], raw13[b][:, :, :],
                                        sc[:, j, 0:8].unsqueeze(2).to_broadcast((P, 8, P)),
                                        ALU.mult).then_inc(w13_scaled, 1)
                pool.wait_ge(w2_in[b], 16 * i + 16)
                nc.gpsimd.tensor_tensor(raw2[b][:, :, :], raw2[b][:, :, :],
                                        sc[:, j, 8:12].unsqueeze(2).to_broadcast((P, 4, P)),
                                        ALU.mult).then_inc(w2_scaled, 1)
            over_blocks(pool, dequantise)

        @block.scalar
        def _(act):
            def upper(j, b, first):
                act.wait_ge(w13_scaled, j + 1)
                if not first:
                    act.wait_ge(up_done, 2 * j - 2)
                nc.scalar.activation(w13_hi[b][:, :, :], raw13[b][:, :, :], ACT.Copy).then_inc(w13_hi_done, 1)

            def inner(i, b, first, last):
                j = 2 * i + b
                if not (last and b == 1):
                    upper(j + 1, 1 - b, first and b == 0)
                act.wait_ge(w2_scaled, j + 1)
                nc.scalar.activation(w2_hi[:, j, :], raw2[b][:, :, :].rearrange("p a b -> p (a b)"),
                                     ACT.Copy).then_inc(w2_hi_done, 1)
                for hf in range(NH):
                    act.wait_ge(gate_done, 2 * j + hf + 1)
                    if not (first and b == 0):
                        act.wait_ge(h_done, 2 * j + hf - 1)
                    nc.scalar.activation(silu[hf][:, :], gate[hf], ACT.Silu).then_inc(silu_done, 1)

            def split(hf):
                def step(i, b, first, last):
                    part_free(act, hf, i, b, first)
                    nc.scalar.activation(hs_hi[b][:, :], h[:, 2 * i + b, hf * HALF:(hf + 1) * HALF],
                                         ACT.Copy).then_inc(hs_hi_done, 1)
                return step
            upper(0, 0, True)
            norm_scalar(nc, act, s, turn, xt_hi)
            over_blocks(act, inner)
            act.wait_ge(h_done, NH * NJ)
            for hf in range(NH):
                over_blocks(act, split(hf))

        @block.vector
        def _(dve):
            norm_vector(nc, dve, s, x, st, mv, rstd, xn, turn, xt_hi, xt_lo)

            def lower(j, b, first):
                dve.wait_ge(w13_hi_done, j + 1)
                if not first:
                    dve.wait_ge(up_done, 2 * j - 2)
                nc.vector.tensor_tensor(w13_lo[b][:, :, :], raw13[b][:, :, :], w13_hi[b][:, :, :].bitcast(F32),
                                        ALU.subtract).then_inc(w13_lo_done, 1)

            def inner(i, b, first, last):
                j = 2 * i + b
                if not (last and b == 1):
                    lower(j + 1, 1 - b, first and b == 0)
                dve.wait_ge(w2_hi_done, j + 1)
                nc.vector.tensor_tensor(w2_lo[:, j, :], raw2[b][:, :, :].rearrange("p a b -> p (a b)"),
                                        w2_hi[:, j, :].bitcast(F32), ALU.subtract).then_inc(w2_lo_done, 1)
                for hf in range(NH):
                    dve.wait_ge(up_done, 2 * j + hf + 1)
                    dve.wait_ge(silu_done, 2 * j + hf + 1)
                    nc.vector.tensor_tensor(h[:, j, hf * HALF:(hf + 1) * HALF], up[hf], silu[hf][:, :],
                                            ALU.mult).then_inc(h_done, 1)

            def split(hf):
                def step(i, b, first, last):
                    n = hf * NJ + 2 * i + b
                    part_free(dve, hf, i, b, first)
                    dve.wait_ge(hs_hi_done, n + 1)
                    nc.vector.tensor_tensor(hs_lo[b][:, :], h[:, 2 * i + b, hf * HALF:(hf + 1) * HALF],
                                            hs_hi[b][:, :].bitcast(F32), ALU.subtract).then_inc(hs_lo_done, 1)
                    if hf == 1 and first and b == 1:
                        add(0)
                return step

            def add(hf):
                for t in range(TH):
                    dve.wait_ge(y_done, TH * hf + t + 1)
                    xs = x[:, TH * hf + t, :]
                    nc.vector.scalar_tensor_tensor(xs, y[hf][t], 0.5, xs, ALU.mult, ALU.add).then_inc(x_done, 1)
            lower(0, 0, True)
            over_blocks(dve, inner)
            dve.wait_ge(h_done, NH * NJ)
            for hf in range(NH):
                over_blocks(dve, split(hf))
            add(1)

        @block.tensor
        def _(pe):
            norm_tensor(nc, pe, s, xn, ident, turn)
            pe.wait_ge(s.lo, TT)

            def inner(i, b, first, last):
                j = 2 * i + b
                pe.wait_ge(w13_lo_done, j + 1)
                for hf in range(NH):
                    if not (first and b == 0):
                        pe.wait_ge(h_done, 2 * j + hf - 1)
                    cols = slice(hf * HALF, (hf + 1) * HALF)
                    for w, out, done in ((0, gate[hf], gate_done), (1, up[hf], up_done)):
                        for c in range(KC):
                            k = 4 * w + c
                            nc.tensor.matmul(out, w13_hi[b][:, k, :], xt_hi[:, c, cols], start=c == 0, stop=False)
                            nc.tensor.matmul(out, w13_hi[b][:, k, :], xt_lo[:, c, cols], start=False, stop=False)
                            mm = nc.tensor.matmul(out, w13_lo[b][:, k, :], xt_hi[:, c, cols], start=False,
                                                  stop=c == KC - 1)
                        mm.then_inc(done, 1)

            def outer(hf):
                def step(i, b, first, last):
                    n = hf * NJ + 2 * i + b
                    j = 2 * i + b
                    pe.wait_ge(hs_lo_done, n + 1)
                    begin, end = first and b == 0, last and b == 1
                    for t in range(TH):
                        tok = slice(t * P, (t + 1) * P)
                        nc.tensor.matmul(y[hf][t], hs_hi[b][:, tok], w2_hi[:, j, :], start=begin, stop=False)
                        nc.tensor.matmul(y[hf][t], hs_hi[b][:, tok], w2_lo[:, j, :], start=False, stop=False)
                        mm = nc.tensor.matmul(y[hf][t], hs_lo[b][:, tok], w2_hi[:, j, :], start=False, stop=end)
                        if end:
                            mm.then_inc(y_done, 1)
                    if not end:
                        mm.then_inc(hs_used, 1)
                return step
            over_blocks(pe, inner)
            pe.wait_ge(w2_lo_done, NJ)
            pe.wait_ge(h_done, NH * NJ)
            for hf in range(NH):
                over_blocks(pe, outer(hf))
    ph.close()


class TurnSems:

    def __init__(self, ph):
        self.turned = ph.sem("turned")
        self.hi = ph.sem("turned_hi")
        self.lo = ph.sem("turned_lo")


def project_phase(nc, name, x, ident, q_nat, kv_nat, w_dram, bias_dram, rope_dram):
    kvw = kv_nat.shape[2]
    nw = D + kvw
    ph = Phase(nc, name)
    st = ph.sb("stats", [P, TT, 6])
    mv = ph.sb("moments", [P, TT, 2])
    rstd = ph.sb("rstd", [P, 3, TT])
    xn = ph.sb("xn", [P, 2, D])
    xt_hi = ph.sb("xt_hi", [P, KC, T], F32R)
    xt_lo = ph.sb("xt_lo", [P, KC, T], F32R)
    raw = ph.sb("raw", [P, KC, nw])
    w_hi = ph.sb("w_hi", [P, KC, nw], F32R)
    w_lo = ph.sb("w_lo", [P, KC, nw], F32R)
    bank = [ph.ps(f"bank{b}", [P, 4, P]) for b in range(6)]
    flat = [b[:, :, :].rearrange("p a b -> p (a b)") for b in bank]
    turn, q_ps, kv_ps = bank[0:2], flat[2:4], flat[4:6]
    s = NormSems(ph)
    w_in, w_hi_done, w_lo_done = ph.sem("w_in"), ph.sem("w_hi_done"), ph.sem("w_lo_done")
    extra_in = ph.sem("extra_in")
    q_done, kv_done, taken = ph.sem("q_done"), ph.sem("kv_done"), ph.sem("taken")
    if bias_dram is not None:
        bias = ph.sb("bias", [P, nw])
    else:
        rope = ph.sb("rope", [P, TT, 2, HD])
        swap = ph.sb("swap", [P, H + HKV1, HD])
        rot_done, half_done = ph.sem("rot_done"), ph.sem("half_done")

    with nc.Block() as block:
        @block.sync
        def _(sp):
            sp.dma_start(raw[:, :, :], w_dram).then_inc(w_in, 16)
            if bias_dram is not None:
                sp.dma_start(bias[:, :], bias_dram.to_broadcast((P, nw))).then_inc(extra_in, 16)
            else:
                sp.dma_start(rope[:, :, :, :], rope_dram).then_inc(extra_in, 16)

        @block.scalar
        def _(act):
            act.wait_ge(w_in, 16)
            nc.scalar.activation(w_hi[:, :, :], raw[:, :, :], ACT.Copy).then_inc(w_hi_done, 1)
            norm_scalar(nc, act, s, turn, xt_hi)

        @block.vector
        def _(dve):
            norm_vector(nc, dve, s, x, st, mv, rstd, xn, turn, xt_hi, xt_lo)
            dve.wait_ge(w_hi_done, 1)
            nc.vector.tensor_tensor(w_lo[:, :, :], raw[:, :, :], w_hi[:, :, :].bitcast(F32),
                                    ALU.subtract).then_inc(w_lo_done, 1)
            dve.wait_ge(extra_in, 16)
            for t in range(TT):
                dve.wait_ge(q_done, t + 1)
                dve.wait_ge(kv_done, t + 1)
                if bias_dram is not None:
                    nc.vector.tensor_tensor(q_nat[:, t, :], q_ps[t % 2], bias[:, 0:D], ALU.add).then_inc(taken, 1)
                    nc.vector.tensor_tensor(kv_nat[:, t, :], kv_ps[t % 2][:, 0:kvw], bias[:, D:nw],
                                            ALU.add).then_inc(taken, 1)
                    continue
                kw = kvw // 2
                qh = q_ps[t % 2].rearrange("p (h d) -> p h d", d=HD)
                kh = kv_ps[t % 2][:, 0:kw].rearrange("p (h d) -> p h d", d=HD)
                qo = q_nat[:, t, :].rearrange("p (h d) -> p h d", d=HD)
                ko = kv_nat[:, t, 0:kw].rearrange("p (h d) -> p h d", d=HD)
                half = HD // 2
                if t >= 1:
                    dve.wait_ge(rot_done, 2 * t)
                for src, out, lo, n in ((qh, qo, 0, H), (kh, ko, H, HKV1)):
                    def table(which, a, b):
                        return rope[:, t, which, a:b].unsqueeze(1).to_broadcast((P, n, b - a))
                    nc.vector.tensor_tensor(out, src, table(0, 0, HD), ALU.mult).then_inc(half_done, 1)
                    for a in (0, half):
                        b = half - a
                        nc.vector.tensor_tensor(swap[:, lo:lo + n, a:a + half], src[:, :, b:b + half],
                                                table(1, a, a + half), ALU.mult).then_inc(half_done, 1)
                nc.vector.tensor_copy(kv_nat[:, t, kw:kvw], kv_ps[t % 2][:, kw:kvw]).then_inc(taken, 1)
                dve.wait_ge(half_done, 6 * (t + 1))
                nc.vector.tensor_tensor(qo, qo, swap[:, 0:H, :], ALU.add).then_inc(rot_done, 1)
                nc.vector.tensor_tensor(ko, ko, swap[:, H:, :], ALU.add).then_inc(rot_done, 1)

        @block.tensor
        def _(pe):
            norm_tensor(nc, pe, s, xn, ident, turn)
            pe.wait_ge(w_lo_done, 1)
            taken_per_tile = 2 if bias_dram is not None else 1
            for t in range(TT):
                tok = slice(t * P, (t + 1) * P)
                pe.wait_ge(s.lo, t + 1)
                if t >= 2:
                    pe.wait_ge(taken, taken_per_tile * (t - 1))
                for out, cols, done in ((q_ps[t % 2], slice(0, D), q_done),
                                        (kv_ps[t % 2][:, 0:kvw], slice(D, nw), kv_done)):
                    for c in range(KC):
                        nc.tensor.matmul(out, xt_hi[:, c, tok], w_hi[:, c, cols], start=c == 0, stop=False)
                        nc.tensor.matmul(out, xt_hi[:, c, tok], w_lo[:, c, cols], start=False, stop=False)
                        mm = nc.tensor.matmul(out, xt_lo[:, c, tok], w_hi[:, c, cols], start=False,
                                              stop=c == KC - 1)
                    mm.then_inc(done, 1)
    ph.close()


def output_phase(nc, name, x, ident, ao, w_dram, bias_dram):
    ph = Phase(nc, name)
    at_hi = ph.sb("at_hi", [P, KC, T], F32R)
    at_lo = ph.sb("at_lo", [P, KC, T], F32R)
    raw = ph.sb("raw", [P, KC, D])
    w_hi = ph.sb("w_hi", [P, KC, D], F32R)
    w_lo = ph.sb("w_lo", [P, KC, D], F32R)
    bank = [ph.ps(f"bank{b}", [P, 4, P]) for b in range(4)]
    turn = bank[0:2]
    out = [b[:, :, :].rearrange("p a b -> p (a b)") for b in bank[2:4]]
    s = TurnSems(ph)
    w_in, w_hi_done, w_lo_done = ph.sem("w_in"), ph.sem("w_hi_done"), ph.sem("w_lo_done")
    bias_in, biased = ph.sem("bias_in"), ph.sem("biased")
    y_done, x_done = ph.sem("y_done"), ph.sem("x_done")
    if bias_dram is not None:
        bias = ph.sb("bias", [P, D])

    with nc.Block() as block:
        @block.sync
        def _(sp):
            sp.dma_start(raw[:, :, :], w_dram).then_inc(w_in, 16)
            if bias_dram is not None:
                sp.dma_start(bias[:, :], bias_dram.to_broadcast((P, D))).then_inc(bias_in, 16)

        @block.scalar
        def _(act):
            act.wait_ge(w_in, 16)
            nc.scalar.activation(w_hi[:, :, :], raw[:, :, :], ACT.Copy).then_inc(w_hi_done, 1)
            for t in range(TT):
                act.wait_ge(s.turned, t + 1)
                nc.scalar.activation(at_hi[:, :, t * P:(t + 1) * P], turn[t % 2][:, :, :],
                                     ACT.Copy).then_inc(s.hi, 1)

        @block.vector
        def _(dve):
            dve.wait_ge(w_hi_done, 1)
            nc.vector.tensor_tensor(w_lo[:, :, :], raw[:, :, :], w_hi[:, :, :].bitcast(F32),
                                    ALU.subtract).then_inc(w_lo_done, 1)
            if bias_dram is not None:
                dve.wait_ge(bias_in, 16)
                for t in range(TT):
                    nc.vector.tensor_tensor(x[:, t, :], x[:, t, :], bias[:, :], ALU.add).then_inc(biased, 1)
                dve.wait_ge(biased, TT)
            for t in range(TT + 1):
                if t < TT:
                    dve.wait_ge(s.hi, t + 1)
                    nc.vector.tensor_tensor(at_lo[:, :, t * P:(t + 1) * P], turn[t % 2][:, :, :],
                                            at_hi[:, :, t * P:(t + 1) * P].bitcast(F32),
                                            ALU.subtract).then_inc(s.lo, 1)
                if t >= 1:
                    dve.wait_ge(y_done, t)
                    nc.vector.tensor_tensor(x[:, t - 1, :], x[:, t - 1, :], out[(t - 1) % 2],
                                            ALU.add).then_inc(x_done, 1)

        @block.tensor
        def _(pe):
            def turn_tile(t):
                if t >= 2:
                    pe.wait_ge(s.lo, t - 1)
                for c in range(KC):
                    last = nc.tensor.transpose(turn[t % 2][:, c, :], ao[:, t, c * P:(c + 1) * P], ident[:, :])
                last.then_inc(s.turned, 1)
            turn_tile(0)
            for t in range(TT):
                if t + 1 < TT:
                    turn_tile(t + 1)
                if t == 0:
                    pe.wait_ge(w_lo_done, 1)
                if t >= 2:
                    pe.wait_ge(x_done, t - 1)
                pe.wait_ge(s.lo, t + 1)
                tok = slice(t * P, (t + 1) * P)
                for c in range(KC):
                    nc.tensor.matmul(out[t % 2], at_hi[:, c, tok], w_hi[:, c, :], start=c == 0, stop=False)
                    nc.tensor.matmul(out[t % 2], at_hi[:, c, tok], w_lo[:, c, :], start=False, stop=False)
                    mm = nc.tensor.matmul(out[t % 2], at_lo[:, c, tok], w_hi[:, c, :], start=False,
                                          stop=c == KC - 1)
                mm.then_inc(y_done, 1)
    ph.close()


def attend_phase(nc, name, ident, ident_b, causal, q_nat, kv_nat, ao, sparse):
    ph = Phase(nc, name)
    kvw = kv_nat.shape[2]
    KSET = 2 if sparse else 1
    qx = [ph.sb(f"qx{p}", [P, TT, 2, 2 * SR]) for p in range(2)]
    kx = ph.sb("kx", [P, TT, 3 * SR])
    qs = [[ph.sb(f"qs{p}{i}", [MR + 4, T], F32R) for i in range(2)] for p in range(2)]
    ks = [[ph.sb(f"ks{p}{e}", [MR + 4, T], F32R) for e in range(2)] for p in range(KSET)]
    v1 = [ph.sb(f"v1{p}", [P, TT, 32]) for p in range(KSET)]
    sel = ph.sb("sel", [P, 2])
    mx = [ph.sb(f"mx{p}", [P, TT, G, 8]) for p in range(2)]
    nm = [ph.sb(f"nm{p}", [P, TT, G, 2]) for p in range(2)]
    pt = [[ph.sb(f"pt{s}{a}", [P, HALF]) for a in range(G)] for s in range(2)]
    ot_sb = ph.sb("ot_sb", [P, HALF])
    rden = ph.sb("rden", [P, TH, G])
    if sparse:
        cm = [ph.sb(f"cm{r}", [P, NCH]) for r in range(4)]
        cr = [ph.sb(f"cr{r}", [P, NCH]) for r in range(4)]
        drop = [ph.sb(f"drop{r}", [P, NCH], BF16) for r in range(2)]
        mark = ph.sb("mark", [P, 1])
        idle = ph.sb("idle", [P, 1])
        settled = ph.sem("settled")
        spare = ph.sb("spare", [P, 1])
        spared = ph.sem("spared")
        price = ph.sb("price", [P, (TT - 2) * P], BF16)
        mk = [[[ph.sb(f"mk{p}{a}{t}", [P, (t - 1) * P], BF16) for t in range(2, TT)] for a in range(G)]
              for p in range(2)]
        cm_done, top_done, cr_done = ph.sem("cm_done"), ph.sem("top_done"), ph.sem("cr_done")
        drop_done, mk_done = ph.sem("drop_done"), ph.sem("mk_done")

    sa = [ph.ps(f"sa{r}", [P, T]) for r in range(2)]
    sb = [ph.ps(f"sb{r}", [P, HALF]) for r in range(2)]
    ot = ph.ps("ot", [P, HALF])
    tr = ph.ps("tr", [P, TH, P])

    const_done = ph.sem("const_done")
    qx_done = ph.sem("qx_done")
    tr_done, tr_free = ph.sem("tr_done"), ph.sem("tr_free")
    sa_done, max_done = ph.sem("sa_done"), ph.sem("max_done")
    nm_done = ph.sem("nm_done")
    sb_done, exp_done, av_done = ph.sem("sb_done"), ph.sem("exp_done"), ph.sem("av_done")
    ot_out, rden_done, ao_done = ph.sem("ot_out"), ph.sem("rden_done"), ph.sem("ao_done")

    NSTEP = sum(4 * g + 4 for g in range(NH))
    STEPS = [(g, kb) for g in range(NH) for kb in range(4 * g + 4)]
    NA = TT * G
    NB = NSTEP * G
    KT = 4
    TPG = 4 + 4 + NH + (KT if sparse else 0)
    TRK0 = 0 if sparse else KT
    QXG = 9 if sparse else 4
    QX0 = 0 if sparse else 5
    LATE = [(t, a) for t in range(2, TT) for a in range(G)]

    def over_groups(eng, step):
        for p in range(2):
            step(p, p, True)
        with eng.Fori(1, H // G // 2) as i:
            for p in range(2):
                step(2 * i + p, p, False)

    with nc.Block() as block:
        @block.gpsimd
        def _(pool):
            def step_k(n, base, p):
                k_src = kv_nat[:, :, bass.ds(HD * n, HD)] if sparse else kv_nat[:, :, 0:HD]
                v_src = kv_nat[:, :, bass.ds(kvw // 2 + HD * n, HD)] if sparse else kv_nat[:, :, HD:2 * HD]
                hi, second, lo = (kx[:, :, SR + HD * c:SR + HD * (c + 1)] for c in range(3))
                nc.gpsimd.tensor_copy(hi.bitcast(F32R), k_src).then_inc(qx_done, 1)
                nc.gpsimd.tensor_copy(second.bitcast(F32R), k_src).then_inc(qx_done, 1)
                nc.gpsimd.tensor_copy(lo, k_src).then_inc(qx_done, 1)
                pool.wait_ge(qx_done, base + 3)
                nc.gpsimd.tensor_tensor(lo.bitcast(F32R), lo, hi, ALU.subtract).then_inc(qx_done, 1)
                nc.gpsimd.tensor_copy(v1[p][:, :, 0:HD], v_src).then_inc(qx_done, 1)

            def prep(n, p, first):
                base = QX0 + QXG * n
                if not first:
                    pool.wait_ge(av_done, NSTEP * (n - 1))
                src = q_nat[:, :, bass.ds(G * HD * n, G * HD)].rearrange("p t (s w) -> p t s w", w=HD)
                v = qx[p][:, :, :, :].rearrange("p t i (e w) -> p t (i e) w", w=SR)
                hi, lo, third = (v[:, :, :, HD * c:HD * (c + 1)] for c in range(3))
                nc.gpsimd.tensor_copy(hi.bitcast(F32R), src).then_inc(qx_done, 1)
                nc.gpsimd.tensor_copy(third, src).then_inc(qx_done, 1)
                pool.wait_ge(qx_done, base + 2)
                nc.gpsimd.tensor_tensor(lo.bitcast(F32R), third, hi, ALU.subtract).then_inc(qx_done, 1)
                pool.wait_ge(qx_done, base + 3)
                nc.gpsimd.tensor_tensor(third.bitcast(F32R), third, lo, ALU.subtract).then_inc(qx_done, 1)
                if sparse:
                    if not (first and p == 0):
                        pool.wait_ge(tr_done, TPG * (n - 1) + 4 + KT)
                    step_k(n, base + 4, p)

            def masks(n, p, first):
                if not first:
                    pool.wait_ge(av_done, NSTEP * (n - 1))
                    pool.wait_ge(mk_done, len(LATE) * n)
                base = len(LATE) * n
                for u in range(len(LATE) + 1):
                    if u < len(LATE):
                        pool.wait_ge(cr_done, base + u + 1)
                    if u >= 2:
                        pool.wait_ge(mk_done, base + u - 1)
                    if u == 0:
                        nc.gpsimd.tensor_tensor(spare[:, :], mark[:, :], mark[:, :], ALU.subtract).then_inc(spared, 1)
                    else:
                        t, a = LATE[u - 1]
                        nch = 8 * t
                        pool.wait_ge(drop_done, base + u)
                        nc.gpsimd.tensor_tensor(
                            mk[p][a][t - 2][:, :].rearrange("p (c w) -> p c w", w=CHUNK),
                            drop[(u - 1) % 2][:, 8:nch].unsqueeze(2).to_broadcast((P, nch - 8, CHUNK)),
                            price[:, (TT - 1 - t) * P:].rearrange("p (c w) -> p c w", w=CHUNK),
                            ALU.mult).then_inc(mk_done, 1)
                    if u < len(LATE):
                        nch = 8 * LATE[u][0]
                        nc.gpsimd.tensor_scalar(drop[u % 2][:, 8:nch], cr[u % 4][:, 8:nch], MARK, None,
                                                ALU.is_lt).then_inc(drop_done, 1)

            nc.gpsimd.memset(kx[:, :, :], 0.0).then_inc(const_done, 1)
            for v in v1:
                nc.gpsimd.memset(v[:, :, :], 0.0).then_inc(const_done, 1)
            pool.wait_ge(const_done, 1 + KSET)
            for v in v1:
                nc.gpsimd.memset(v[:, :, HD:HD + 1], 1.0).then_inc(const_done, 1)
            for e in range(2):
                nc.gpsimd.tensor_tensor(sel[:, e:e + 1], ident[:, MR + 2 * e:MR + 2 * e + 1],
                                        ident[:, MR + 2 * e + 1:MR + 2 * e + 2], ALU.add).then_inc(const_done, 1)
            pool.wait_ge(const_done, 3 + 2 * KSET)
            for pair in ks:
                for e, k in enumerate(pair):
                    nc.gpsimd.tensor_copy(k[MR:MR + 4, :], sel[MR:MR + 4, e:e + 1].to_broadcast((4, T))).then_inc(const_done, 1)
            pool.wait_ge(const_done, 3 + 4 * KSET)
            if sparse:
                nc.gpsimd.memset(mark[:, :], MARK).then_inc(const_done, 1)
                nc.gpsimd.memset(price[:, :], NEG).then_inc(const_done, 1)
                pool.wait_ge(const_done, 5 + 4 * KSET)
                nc.gpsimd.affine_select(out=price[:, -P:], in_=price[:, -P:], compare_op=ALU.is_ge, fill=0.0,
                                        base=0, pattern=[[-1, P]], channel_multiplier=1).then_inc(const_done, 1)
                pool.wait_ge(const_done, 6 + 4 * KSET)
            else:
                step_k(0, 0, 0)

            def group(n, p, first):
                prep(n, p, first)
                if sparse:
                    masks(n, p, first)
            over_groups(pool, group)

        @block.tensor
        def _(pe):
            pe.wait_ge(const_done, 3 + 4 * KSET + (3 if sparse else 0))

            def use_tr(u, first):
                if not first:
                    pe.wait_ge(tr_free, u)

            def turn_k(u, first):
                for e in range(2):
                    for g in range(NH):
                        use_tr(u + 2 * e + g, first and e + g == 0)
                        for t in range(TH):
                            mm = nc.tensor.transpose(tr[0:MR, t, :], kx[:, TH * g + t, SR * (1 - e):SR * (3 - e)],
                                                     ident[:, :])
                        mm.then_inc(tr_done, 1)

            def group(n, p, first):
                fst = first and p == 0
                u = TRK0 + TPG * n
                pe.wait_ge(qx_done, QX0 + QXG * (n + 1))
                for i in range(2):
                    for g in range(NH):
                        use_tr(u + 2 * i + g, fst and sparse and i + g == 0)
                        for t in range(TH):
                            mm = nc.tensor.transpose(tr[0:MR, t, :], qx[p][:, TH * g + t, i, :], ident[:, :])
                        mm.then_inc(tr_done, 1)
                u = u + 4
                if sparse:
                    turn_k(u, False)
                    u = u + KT
                pe.wait_ge(tr_free, u)
                k = ks[p if sparse else 0]
                for t in range(TT):
                    for a in range(G):
                        unit = NA * n + G * t + a
                        if not (fst and t == 0 and a < 2):
                            pe.wait_ge(max_done, unit - 1)
                        q, out, w = qs[p][a // 2][0:MR, t * P:(t + 1) * P], sa[a % 2], (t + 1) * P
                        for c0 in range(0, w, HALF):
                            c1 = min(c0 + HALF, w)
                            nc.tensor.matmul(out[:, c0:c1], q, k[a % 2][0:MR, c0:c1], start=True, stop=c1 < w,
                                             skip_group_check=True)
                        nc.tensor.matmul(out[:, w - P:w], ident_b[:, :], causal[:, :], start=False, stop=True,
                                         skip_group_check=True).then_inc(sa_done, 1)
                for g in range(NH):
                    pe.wait_ge(nm_done, NH * n + g + 1)
                    for i in range(2):
                        use_tr(u, False)
                        for t in range(TH):
                            mm = nc.tensor.transpose(
                                tr[0:4, t, :], nm[p][:, TH * g + t, 2 * i:2 * i + 2, :].rearrange("p a b -> p (a b)"),
                                ident[:, :])
                        mm.then_inc(tr_done, 1)
                        u = u + 1
                pe.wait_ge(tr_free, u)
                if sparse:
                    pe.wait_ge(mk_done, len(LATE) * (n + 1))

                def weigh(s):
                    g, kb = STEPS[s]
                    c0 = max(0, (kb - 4 * g) * P)
                    pe.wait_ge(exp_done, NB * n + G * (s + 1))
                    if kb == 0 and not (fst and g == 0):
                        pe.wait_ge(ot_out, NH * n + g)
                    for a in range(G):
                        mm = nc.tensor.matmul(ot[32 * a:32 * a + 32, c0:HALF], v1[p if sparse else 0][:, kb, :],
                                              pt[s % 2][a][:, c0:HALF], start=kb == 0, stop=kb == 4 * g + 3,
                                              skip_group_check=True)
                    mm.then_inc(av_done, 1)

                def finish(g, u):
                    pe.wait_ge(ot_out, NH * n + g + 1)
                    use_tr(u, False)
                    for t in range(TH):
                        mm = nc.tensor.transpose(tr[:, t, :], ot_sb[:, t * P:(t + 1) * P], ident[:, :])
                    mm.then_inc(tr_done, 1)

                for s, (g, kb) in enumerate(STEPS):
                    c0 = max(0, (kb - 4 * g) * P)
                    for a in range(G):
                        unit = NB * n + G * s + a
                        if not (fst and s == 0 and a < 2):
                            pe.wait_ge(exp_done, unit - 1)
                        late = [t for t in range(TH * g, TH * (g + 1)) if sparse and t >= 2 and 1 <= kb <= t - 1]
                        diag = kb >= 4 * g
                        mm = nc.tensor.matmul(sb[a % 2][:, c0:HALF], k[a % 2][:, kb * P:(kb + 1) * P],
                                         qs[p][a // 2][:, HALF * g + c0:HALF * (g + 1)], start=True,
                                         stop=not (late or diag), skip_group_check=True)
                        adds = [(causal[:, :], kb)] if diag else []
                        adds += [(mk[p][a][t - 2][:, (kb - 1) * P:kb * P], t) for t in late]
                        for x_, (m, t) in enumerate(adds):
                            c = t * P - HALF * g
                            mm = nc.tensor.matmul(sb[a % 2][:, c:c + P], m, ident_b[:, :], start=False,
                                                  stop=x_ == len(adds) - 1, skip_group_check=True)
                        mm.then_inc(sb_done, 1)
                    if s:
                        weigh(s - 1)
                    if s == 6:
                        finish(0, u)
                weigh(NSTEP - 1)
                finish(1, u + 1)

            if not sparse:
                pe.wait_ge(qx_done, QX0)
                turn_k(0, True)
            over_groups(pe, group)

        @block.scalar
        def _(act):
            def rows(dst, src, u):
                act.wait_ge(tr_done, u + 1)
                nc.scalar.activation(dst, src, ACT.Copy).then_inc(tr_free, 1)

            def stack_k(k, u):
                for e in range(2):
                    for g in range(NH):
                        rows(k[e][0:MR, g * HALF:(g + 1) * HALF].rearrange("p (t w) -> p t w", w=P),
                             tr[0:MR, :, :], u + 2 * e + g)

            def group(n, p, first):
                fst = first and p == 0
                u = TRK0 + TPG * n
                for i in range(2):
                    for g in range(NH):
                        rows(qs[p][i][0:MR, g * HALF:(g + 1) * HALF].rearrange("p (t w) -> p t w", w=P),
                             tr[0:MR, :, :], u + 2 * i + g)
                u = u + 4
                if sparse:
                    stack_k(ks[p], u)
                    u = u + KT
                for g in range(NH):
                    for i in range(2):
                        rows(qs[p][i][MR:MR + 4, g * HALF:(g + 1) * HALF].rearrange("p (t w) -> p t w", w=P),
                             tr[0:4, :, :], u + 2 * g + i)
                for s, (g, kb) in enumerate(STEPS):
                    c0 = max(0, (kb - 4 * g) * P)
                    for a in range(G):
                        act.wait_ge(sb_done, NB * n + G * s + a + 1)
                        if a == 0 and not (fst and s < 2):
                            act.wait_ge(av_done, NSTEP * n + s - 1)
                        nc.scalar.activation(pt[s % 2][a][:, c0:HALF], sb[a % 2][:, c0:HALF], ACT.Exp,
                                             scale=HD ** -0.5).then_inc(exp_done, 1)

            if not sparse:
                stack_k(ks[0], 0)
            over_groups(act, group)

        @block.vector
        def _(dve):
            if sparse:
                dve.wait_ge(const_done, 6 + 4 * KSET)
            units = [(t, a) for t in range(TT) for a in range(G)]

            def chunk_maxima(n, p, fst, v):
                t, a = units[v]
                unit = NA * n + v
                if not (fst and v == 0):
                    dve.wait_ge(max_done, unit)
                if not (fst and v < 2):
                    dve.wait_ge(top_done, unit - 1)
                if v >= 2 and units[v - 2] in LATE and not (fst and LATE.index(units[v - 2]) < 4):
                    dve.wait_ge(drop_done, len(LATE) * n + LATE.index(units[v - 2]) - 3)
                if v >= 4 and units[v - 4] in LATE:
                    dve.wait_ge(cr_done, len(LATE) * n + LATE.index(units[v - 4]) + 1)
                dve.wait_ge(sa_done, unit + 1)
                nc.vector.tensor_reduce(cm[v % 4][:, 0:8 * t + 8],
                                        sa[a % 2][:, 0:(t + 1) * P].rearrange("p (c w) -> p c w", w=CHUNK),
                                        AX.X, ALU.max).then_inc(max_done, 1)

            def largest(p, v):
                t, a = units[v]
                nc.vector.max(mx[p][:, t, a, :], cm[v % 4][:, 0:8 * t + 8]).then_inc(top_done, 1)

            def match(p, v):
                t, a = units[v]
                if (t, a) in LATE:
                    nc.vector.match_replace(out=cr[LATE.index((t, a)) % 4][:, 0:8 * t + 8],
                                            in_to_replace=mx[p][:, t, a, :], in_values=cm[v % 4][:, 0:8 * t + 8],
                                            imm_value=MARK).then_inc(cr_done, 1)

            def settle(n, v):
                dve.wait_ge(max_done, NA * n + NA)
                dve.wait_ge(top_done, NA * n + v - 1)
                dve.wait_ge(drop_done, len(LATE) * n + LATE.index(units[v - 2]) - 3)
                nc.vector.tensor_copy(idle[:, :], mark[:, :]).then_inc(settled, 1)

            def split_maxima(n, p, g):
                m = mx[p][:, TH * g:TH * (g + 1), :, 0]
                out = nm[p][:, TH * g:TH * (g + 1), :, :]
                dve.wait_ge(top_done if sparse else max_done, NA * n + G * TH * (g + 1))
                nc.vector.tensor_scalar(out[:, :, :, 0].bitcast(F32R), m, -1.0, None, ALU.mult).then_inc(rden_done, 1)
                dve.wait_ge(rden_done, 4 * n + g + 1)
                nc.vector.scalar_tensor_tensor(out[:, :, :, 1].bitcast(F32R), m, -1.0, out[:, :, :, 0],
                                               ALU.mult, ALU.subtract).then_inc(nm_done, 1)

            def group(n, p, first):
                fst = first and p == 0
                for v, (t, a) in enumerate(units):
                    if sparse:
                        chunk_maxima(n, p, fst, v)
                        if v >= 1:
                            largest(p, v - 1)
                        if v >= 2:
                            match(p, v - 2)
                        if v == G * TH + 1:
                            split_maxima(n, p, 0)
                    else:
                        dve.wait_ge(sa_done, NA * n + v + 1)
                        nc.vector.tensor_reduce(mx[p][:, t, a, 0:1], sa[a % 2][:, 0:(t + 1) * P], AX.X,
                                                ALU.max).then_inc(max_done, 1)
                        if v == G * TH - 1:
                            split_maxima(n, p, 0)
                if sparse:
                    settle(n, NA)
                    largest(p, NA - 1)
                    match(p, NA - 2)
                    settle(n, NA + 1)
                    match(p, NA - 1)
                split_maxima(n, p, 1)
                u = TRK0 + TPG * n + TPG - NH
                for g in range(NH):
                    dve.wait_ge(av_done, NSTEP * n + 4 + 8 * g)
                    dve.wait_ge(tr_done, u + g)
                    nc.vector.tensor_copy(ot_sb[:, :], ot[:, :]).then_inc(ot_out, 1)
                    dve.wait_ge(tr_done, u + g + 1)
                    heads = tr[:, :, :].rearrange("p t (a w) -> p t a w", w=32)
                    nc.vector.reciprocal(rden[:, :, :], heads[:, :, :, HD]).then_inc(rden_done, 1)
                    dve.wait_ge(rden_done, 4 * n + 3 + g)
                    nc.vector.tensor_tensor(
                        ao[:, TH * g:TH * (g + 1), bass.ds(G * HD * n, G * HD)].rearrange("p t (a w) -> p t a w", w=HD),
                        heads[:, :, :, 0:HD], rden[:, :, :].unsqueeze(3).to_broadcast((P, TH, G, HD)),
                        ALU.mult).then_inc(tr_free, 1)
            over_groups(dve, group)
    ph.close()


def store_phase(nc, x, out_dram):
    ph = Phase(nc, "store")
    stored = ph.sem("stored")
    with nc.Block() as block:
        @block.sync
        def _(sp):
            sp.dma_start(out_dram.rearrange("(t p) d -> p t d", p=P), x[:, :, :]).then_inc(stored, 16)
            sp.wait_ge(stored, 16)
    ph.close()


def attention(nc, name, x, ident, ident_b, causal, t, layer, kvw):
    with ExitStack() as keep:
        q_nat = keep.enter_context(nc.sbuf_tensor(f"{name}_q", [P, TT, D], F32))
        kv_nat = keep.enter_context(nc.sbuf_tensor(f"{name}_kv", [P, TT, kvw], F32))
        ao = keep.enter_context(nc.sbuf_tensor(f"{name}_ao", [P, TT, D], F32))
        project_phase(nc, f"{name}p", x, ident, q_nat, kv_nat, t[f"{layer}_wqkv"], t.get(f"{layer}_bqkv"),
                      t.get("rope"))
        attend_phase(nc, f"{name}s", ident, ident_b, causal, q_nat, kv_nat, ao, sparse=layer == "L1")
        output_phase(nc, f"{name}o", x, ident, ao, t[f"{layer}_wo"], t.get(f"{layer}_bo"))


def program(nc, t):
    with ExitStack() as keep:
        x = keep.enter_context(nc.sbuf_tensor("x", [P, TT, D], F32))
        ident = keep.enter_context(nc.sbuf_tensor("ident", [P, P], F32))
        ident_b = keep.enter_context(nc.sbuf_tensor("ident_b", [P, P], BF16))
        causal = keep.enter_context(nc.sbuf_tensor("causal", [P, P], BF16))
        load_phase(nc, x, ident, ident_b, causal, t["x"])
        ffn_phase(nc, "ffn0a", x, ident, t["L0_w13"], t["L0_w2"], t["L0_scale"])
        attention(nc, "att0", x, ident, ident_b, causal, t, "L0", 2 * HD)
        ffn_phase(nc, "ffn0b", x, ident, t["L0_w13"], t["L0_w2"], t["L0_scale"])
        ffn_phase(nc, "ffn1a", x, ident, t["L1_w13"], t["L1_w2"], t["L1_scale"])
        attention(nc, "att1", x, ident, ident_b, causal, t, "L1", 2 * HKV1 * HD)
        ffn_phase(nc, "ffn1b", x, ident, t["L1_w13"], t["L1_w2"], t["L1_scale"])
        store_phase(nc, x, t["out"])


def kernel(**inputs):
    import numpy as np
    import concourse.bacc as bacc
    from concourse.bass_utils import run_bass_kernel_spmd

    arrays = {"x": np.ascontiguousarray(inputs["L0_attn_x"].reshape(T, D))}
    for layer in ("L0", "L1"):
        def in_blocks(w):
            return w.reshape(NJ, P, KC, P).transpose(0, 3, 2, 1)
        w1, w3, w2 = (inputs[f"{layer}_ffn_w{n}"] for n in (1, 3, 2))
        s1, s3, s2 = (inputs[f"{layer}_ffn_w{n}_scale"] for n in (1, 3, 2))
        arrays[f"{layer}_w13"] = np.ascontiguousarray(np.concatenate([in_blocks(w1), in_blocks(w3)], axis=2))
        arrays[f"{layer}_w2"] = np.ascontiguousarray(w2.T.reshape(NJ, P, KC, P))
        arrays[f"{layer}_scale"] = np.ascontiguousarray(np.concatenate([s1, s3, s2.T], axis=1))[None]
    def in_chunks(w):
        return np.ascontiguousarray(w.T.reshape(KC, P, -1).transpose(1, 0, 2))
    arrays["L0_wqkv"] = in_chunks(np.concatenate([inputs[f"L0_attn_w{n}_w"] for n in "qkv"]))
    arrays["L0_bqkv"] = np.concatenate([inputs[f"L0_attn_w{n}_b"] for n in "qkv"])[None]
    arrays["L0_wo"] = in_chunks(inputs["L0_attn_wo_w"])
    arrays["L0_bo"] = np.ascontiguousarray(inputs["L0_attn_wo_b"][None])
    arrays["L1_wqkv"] = in_chunks(np.concatenate([inputs[f"L1_attn_w{n}"] for n in "qkv"]))
    arrays["L1_wo"] = in_chunks(inputs["L1_attn_wo"])
    freq = (np.float32(1.0) / np.float32(10000.0) ** (np.arange(0, HD, 2, dtype=np.float32) / np.float32(HD)))
    angle = np.arange(T, dtype=np.float32)[:, None] * freq[None, :].astype(np.float32)
    cos, sin = np.cos(angle), np.sin(angle)
    rope = np.stack([np.concatenate([cos, cos], 1), np.concatenate([-sin, sin], 1)], 1)
    arrays["rope"] = np.ascontiguousarray(rope.reshape(TT, P, 2, HD).transpose(1, 0, 2, 3).astype(np.float32))
    nc = bacc.Bacc("TRN2", target_bir_lowering=False, num_devices=1)
    aps = {n: nc.dram_tensor(f"in_{n}", a.shape, mybir.dt.from_np(a.dtype), kind="ExternalInput").ap()
           for n, a in arrays.items()}
    aps["out"] = nc.dram_tensor("result", (T, D), F32, kind="ExternalOutput").ap()
    program(nc, aps)
    r = run_bass_kernel_spmd(nc, [{f"in_{n}": a for n, a in arrays.items()}], core_ids=[0])
    return r.results[0]["result"].reshape(1, T, D)
```

```python
import concourse.bass as bass
from concourse import mybir
from contextlib import ExitStack

F32 = mybir.dt.float32
F32R = mybir.dt.float32r
I32 = mybir.dt.int32
BF16 = mybir.dt.bfloat16
ALU = mybir.AluOpType
ACT = mybir.ActivationFunctionType
AX = mybir.AxisListType

P = 128
T = 1024
D = 512
TT = T // P
KC = D // P
INTER = 1792
NJ = INTER // P
HALF = 512
NH = T // HALF
TH = HALF // P
EPS = 1e-5
H, HD = 32, 16
HKV1 = 8
G = 4
SR = 3 * HD
MR = 2 * SR
CHUNK = 16
NCH = T // CHUNK
MARK = 3e38
RSQRT_MAGIC = 1597463007.0


class Phase:

    def __init__(self, nc, name):
        self.nc, self.name, self.stack, self.sems = nc, name, ExitStack(), []

    def sb(self, name, shape, dt=F32):
        return self.stack.enter_context(self.nc.sbuf_tensor(f"{self.name}_{name}", shape, dt))

    def ps(self, name, shape, dt=F32):
        return self.stack.enter_context(self.nc.psum_tensor(f"{self.name}_{name}", shape, dt))

    def sem(self, name):
        self.sems.append(self.nc.alloc_semaphore(f"{self.name}_{name}"))
        return self.sems[-1]

    def close(self):
        self.nc.clear_and_free_semaphores(self.sems)
        self.nc.all_engine_barrier()
        self.stack.close()


class NormSems:

    def __init__(self, ph):
        self.stats = ph.sem("norm_stats")
        self.moments = ph.sem("norm_moments")
        self.rstd = ph.sem("norm_rstd")
        self.tile = ph.sem("norm_tile")
        self.turned = ph.sem("norm_turned")
        self.hi = ph.sem("norm_hi")
        self.lo = ph.sem("norm_lo")


def norm_vector(nc, dve, s, x, st, mv, rstd, xn, turn, xt_hi, xt_lo):
    y = rstd[:, 0, :]
    for t in range(TT):
        nc.vector.bn_stats(st[:, t, :], x[:, t, :]).then_inc(s.stats, 1)
    for t in range(TT):
        dve.wait_ge(s.stats, t + 1)
        nc.vector.bn_aggr(mv[:, t, :], st[:, t, :]).then_inc(s.moments, 1)
    dve.wait_ge(s.moments, TT)
    var, tmp = rstd[:, 1, :], rstd[:, 2, :]
    nc.vector.tensor_scalar(var, mv[:, :, 1], EPS, None, ALU.add).then_inc(s.rstd, 1)
    dve.wait_ge(s.rstd, 1)
    nc.vector.tensor_scalar(tmp.bitcast(I32), var.bitcast(I32), 1, None,
                            ALU.logical_shift_right).then_inc(s.rstd, 1)
    dve.wait_ge(s.rstd, 2)
    nc.vector.tensor_scalar(y.bitcast(I32), tmp.bitcast(I32), -1.0, RSQRT_MAGIC, ALU.mult, ALU.add).then_inc(s.rstd, 1)
    for n in range(3):
        dve.wait_ge(s.rstd, 3 + 3 * n)
        nc.vector.scalar_tensor_tensor(tmp, var, -0.5, y, ALU.mult, ALU.mult).then_inc(s.rstd, 1)
        dve.wait_ge(s.rstd, 4 + 3 * n)
        nc.vector.tensor_tensor(tmp, tmp, y, ALU.mult).then_inc(s.rstd, 1)
        dve.wait_ge(s.rstd, 5 + 3 * n)
        nc.vector.scalar_tensor_tensor(y, tmp, 1.5, y, ALU.add, ALU.mult).then_inc(s.rstd, 1)
    dve.wait_ge(s.rstd, 12)

    def lower(t):
        dve.wait_ge(s.hi, t + 1)
        nc.vector.tensor_tensor(xt_lo[:, :, t * P:(t + 1) * P], turn[t % 2][:, :, :],
                                xt_hi[:, :, t * P:(t + 1) * P].bitcast(F32), ALU.subtract).then_inc(s.lo, 1)

    for t in range(TT):
        if t >= 2:
            dve.wait_ge(s.turned, t - 1)
        nc.vector.tensor_scalar(xn[:, t % 2, :], x[:, t, :], mv[:, t, 0:1], rstd[:, 0, t:t + 1],
                                ALU.subtract, ALU.mult).then_inc(s.tile, 1)
        if t >= 1:
            lower(t - 1)
    lower(TT - 1)


def norm_scalar(nc, act, s, turn, xt_hi):
    for t in range(TT):
        act.wait_ge(s.turned, t + 1)
        nc.scalar.activation(xt_hi[:, :, t * P:(t + 1) * P], turn[t % 2][:, :, :], ACT.Copy).then_inc(s.hi, 1)


def norm_tensor(nc, pe, s, xn, ident, turn):
    for t in range(TT):
        pe.wait_ge(s.tile, t + 1)
        if t >= 2:
            pe.wait_ge(s.lo, t - 1)
        for c in range(KC):
            last = nc.tensor.transpose(turn[t % 2][:, c, :], xn[:, t % 2, c * P:(c + 1) * P], ident[:, :])
        last.then_inc(s.turned, 1)


def load_phase(nc, x, ident, ident_b, causal, x_dram):
    ph = Phase(nc, "load")
    loaded = ph.sem("loaded")
    made = ph.sem("made")
    with nc.Block() as block:
        @block.sync
        def _(sp):
            sp.dma_start(x[:, :, :], x_dram.rearrange("(t p) d -> p t d", p=P)).then_inc(loaded, 16)
            sp.wait_ge(loaded, 16)

        @block.gpsimd
        def _(pool):
            nc.gpsimd.memset(ident[:, :], 0.0).then_inc(made, 1)
            nc.gpsimd.memset(ident_b[:, :], 0.0).then_inc(made, 1)
            nc.gpsimd.memset(causal[:, :], 0.0).then_inc(made, 1)
            pool.wait_ge(made, 3)
            for m in (ident, ident_b):
                nc.gpsimd.affine_select(out=m[:, :], in_=m[:, :], compare_op=ALU.not_equal, fill=1.0,
                                        base=0, pattern=[[-1, P]], channel_multiplier=1).then_inc(made, 1)
            nc.gpsimd.affine_select(out=causal[:, :], in_=causal[:, :], compare_op=ALU.is_ge, fill=NEG,
                                    base=0, pattern=[[-1, P]], channel_multiplier=1).then_inc(made, 1)
            pool.wait_ge(made, 6)
    ph.close()


NEG = -1e36


def ffn_phase(nc, name, x, ident, w13_dram, w2_dram, scale_dram):
    ph = Phase(nc, name)
    sc = ph.sb("scales", [P, NJ, 12])
    st = ph.sb("stats", [P, TT, 6])
    mv = ph.sb("moments", [P, TT, 2])
    rstd = ph.sb("rstd", [P, 3, TT])
    xn = ph.sb("xn", [P, 2, D])
    xt_hi = ph.sb("xt_hi", [P, KC, T], F32R)
    xt_lo = ph.sb("xt_lo", [P, KC, T], F32R)
    raw13 = [ph.sb(f"raw13_{b}", [P, 8, P]) for b in range(2)]
    w13_hi = [ph.sb(f"w13_hi{b}", [P, 8, P], F32R) for b in range(2)]
    w13_lo = [ph.sb(f"w13_lo{b}", [P, 8, P], F32R) for b in range(2)]
    raw2 = [ph.sb(f"raw2_{b}", [P, 4, P]) for b in range(2)]
    w2_hi = ph.sb("w2_hi", [P, NJ, D], F32R)
    w2_lo = ph.sb("w2_lo", [P, NJ, D], F32R)
    h = ph.sb("h", [P, NJ, T])
    silu = [ph.sb(f"silu{b}", [P, HALF]) for b in range(2)]
    hs_hi = [ph.sb(f"hs_hi{b}", [P, HALF], F32R) for b in range(2)]
    hs_lo = [ph.sb(f"hs_lo{b}", [P, HALF], F32R) for b in range(2)]
    bank = [ph.ps(f"bank{b}", [P, 4, P]) for b in range(8)]
    turn = bank[4:6]
    flat = [b[:, :, :].rearrange("p a b -> p (a b)") for b in bank]
    gate, up = flat[0:2], flat[2:4]
    y = [flat[4:8], flat[0:4]]

    s = NormSems(ph)
    scales_in = ph.sem("scales_in")
    w13_in = [ph.sem(f"w13_in{b}") for b in range(2)]
    w2_in = [ph.sem(f"w2_in{b}") for b in range(2)]
    w13_scaled, w2_scaled = ph.sem("w13_scaled"), ph.sem("w2_scaled")
    w13_hi_done, w2_hi_done = ph.sem("w13_hi_done"), ph.sem("w2_hi_done")
    w13_lo_done, w2_lo_done = ph.sem("w13_lo_done"), ph.sem("w2_lo_done")
    gate_done, up_done = ph.sem("gate_done"), ph.sem("up_done")
    silu_done, h_done = ph.sem("silu_done"), ph.sem("h_done")
    hs_hi_done, hs_lo_done, hs_used = ph.sem("hs_hi_done"), ph.sem("hs_lo_done"), ph.sem("hs_used")
    y_done, x_done = ph.sem("y_done"), ph.sem("x_done")

    def over_blocks(eng, step):
        for b in range(2):
            step(0, b, True, False)
        with eng.Fori(1, NJ // 2 - 1) as i:
            for b in range(2):
                step(i, b, False, False)
        for b in range(2):
            step(NJ // 2 - 1, b, False, True)

    def part_free(eng, hf, i, b, first):
        if not first:
            eng.wait_ge(hs_used, (NJ - 1) * hf + 2 * i + b - 1)
        elif hf > 0:
            if b == 0:
                eng.wait_ge(hs_used, (NJ - 1) * hf)
            else:
                eng.wait_ge(y_done, TH * hf)

    with nc.Block() as block:
        @block.sync
        def _(sp):
            sp.dma_start(sc[:, :, :], scale_dram.to_broadcast((P, NJ, 12))).then_inc(scales_in, 16)

            def load(i, b, first, last):
                j = 2 * i + b
                if not first:
                    sp.wait_ge(w13_lo_done, j - 1)
                sp.dma_start(raw13[b][:, :, :], w13_dram[j, :, :, :]).then_inc(w13_in[b], 16)
                if not first:
                    sp.wait_ge(w2_lo_done, j - 1)
                sp.dma_start(raw2[b][:, :, :], w2_dram[j, :, :, :]).then_inc(w2_in[b], 16)
            over_blocks(sp, load)

        @block.gpsimd
        def _(pool):
            pool.wait_ge(scales_in, 16)

            def dequantise(i, b, first, last):
                j = 2 * i + b
                pool.wait_ge(w13_in[b], 16 * i + 16)
                nc.gpsimd.tensor_tensor(raw13[b][:, :, :], raw13[b][:, :, :],
                                        sc[:, j, 0:8].unsqueeze(2).to_broadcast((P, 8, P)),
                                        ALU.mult).then_inc(w13_scaled, 1)
                pool.wait_ge(w2_in[b], 16 * i + 16)
                nc.gpsimd.tensor_tensor(raw2[b][:, :, :], raw2[b][:, :, :],
                                        sc[:, j, 8:12].unsqueeze(2).to_broadcast((P, 4, P)),
                                        ALU.mult).then_inc(w2_scaled, 1)
            over_blocks(pool, dequantise)

        @block.scalar
        def _(act):
            def upper(j, b, first):
                act.wait_ge(w13_scaled, j + 1)
                if not first:
                    act.wait_ge(up_done, 2 * j - 2)
                nc.scalar.activation(w13_hi[b][:, :, :], raw13[b][:, :, :], ACT.Copy).then_inc(w13_hi_done, 1)

            def inner(i, b, first, last):
                j = 2 * i + b
                if not (last and b == 1):
                    upper(j + 1, 1 - b, first and b == 0)
                act.wait_ge(w2_scaled, j + 1)
                nc.scalar.activation(w2_hi[:, j, :], raw2[b][:, :, :].rearrange("p a b -> p (a b)"),
                                     ACT.Copy).then_inc(w2_hi_done, 1)
                for hf in range(NH):
                    act.wait_ge(gate_done, 2 * j + hf + 1)
                    if not (first and b == 0):
                        act.wait_ge(h_done, 2 * j + hf - 1)
                    nc.scalar.activation(silu[hf][:, :], gate[hf], ACT.Silu).then_inc(silu_done, 1)

            def split(hf):
                def step(i, b, first, last):
                    part_free(act, hf, i, b, first)
                    nc.scalar.activation(hs_hi[b][:, :], h[:, 2 * i + b, hf * HALF:(hf + 1) * HALF],
                                         ACT.Copy).then_inc(hs_hi_done, 1)
                return step
            upper(0, 0, True)
            norm_scalar(nc, act, s, turn, xt_hi)
            over_blocks(act, inner)
            act.wait_ge(h_done, NH * NJ)
            for hf in range(NH):
                over_blocks(act, split(hf))

        @block.vector
        def _(dve):
            norm_vector(nc, dve, s, x, st, mv, rstd, xn, turn, xt_hi, xt_lo)

            def lower(j, b, first):
                dve.wait_ge(w13_hi_done, j + 1)
                if not first:
                    dve.wait_ge(up_done, 2 * j - 2)
                nc.vector.tensor_tensor(w13_lo[b][:, :, :], raw13[b][:, :, :], w13_hi[b][:, :, :].bitcast(F32),
                                        ALU.subtract).then_inc(w13_lo_done, 1)

            def inner(i, b, first, last):
                j = 2 * i + b
                if not (last and b == 1):
                    lower(j + 1, 1 - b, first and b == 0)
                dve.wait_ge(w2_hi_done, j + 1)
                nc.vector.tensor_tensor(w2_lo[:, j, :], raw2[b][:, :, :].rearrange("p a b -> p (a b)"),
                                        w2_hi[:, j, :].bitcast(F32), ALU.subtract).then_inc(w2_lo_done, 1)
                for hf in range(NH):
                    dve.wait_ge(up_done, 2 * j + hf + 1)
                    dve.wait_ge(silu_done, 2 * j + hf + 1)
                    nc.vector.tensor_tensor(h[:, j, hf * HALF:(hf + 1) * HALF], up[hf], silu[hf][:, :],
                                            ALU.mult).then_inc(h_done, 1)

            def split(hf):
                def step(i, b, first, last):
                    n = hf * NJ + 2 * i + b
                    part_free(dve, hf, i, b, first)
                    dve.wait_ge(hs_hi_done, n + 1)
                    nc.vector.tensor_tensor(hs_lo[b][:, :], h[:, 2 * i + b, hf * HALF:(hf + 1) * HALF],
                                            hs_hi[b][:, :].bitcast(F32), ALU.subtract).then_inc(hs_lo_done, 1)
                    if hf == 1 and first and b == 1:
                        add(0)
                return step

            def add(hf):
                for t in range(TH):
                    dve.wait_ge(y_done, TH * hf + t + 1)
                    xs = x[:, TH * hf + t, :]
                    nc.vector.scalar_tensor_tensor(xs, y[hf][t], 0.5, xs, ALU.mult, ALU.add).then_inc(x_done, 1)
            lower(0, 0, True)
            over_blocks(dve, inner)
            dve.wait_ge(h_done, NH * NJ)
            for hf in range(NH):
                over_blocks(dve, split(hf))
            add(1)

        @block.tensor
        def _(pe):
            norm_tensor(nc, pe, s, xn, ident, turn)
            pe.wait_ge(s.lo, TT)

            def inner(i, b, first, last):
                j = 2 * i + b
                pe.wait_ge(w13_lo_done, j + 1)
                for hf in range(NH):
                    if not (first and b == 0):
                        pe.wait_ge(h_done, 2 * j + hf - 1)
                    cols = slice(hf * HALF, (hf + 1) * HALF)
                    for w, out, done in ((0, gate[hf], gate_done), (1, up[hf], up_done)):
                        for c in range(KC):
                            k = 4 * w + c
                            nc.tensor.matmul(out, w13_hi[b][:, k, :], xt_hi[:, c, cols], start=c == 0, stop=False)
                            nc.tensor.matmul(out, w13_hi[b][:, k, :], xt_lo[:, c, cols], start=False, stop=False)
                            mm = nc.tensor.matmul(out, w13_lo[b][:, k, :], xt_hi[:, c, cols], start=False,
                                                  stop=c == KC - 1)
                        mm.then_inc(done, 1)

            def outer(hf):
                def step(i, b, first, last):
                    n = hf * NJ + 2 * i + b
                    j = 2 * i + b
                    pe.wait_ge(hs_lo_done, n + 1)
                    begin, end = first and b == 0, last and b == 1
                    for t in range(TH):
                        tok = slice(t * P, (t + 1) * P)
                        nc.tensor.matmul(y[hf][t], hs_hi[b][:, tok], w2_hi[:, j, :], start=begin, stop=False)
                        nc.tensor.matmul(y[hf][t], hs_hi[b][:, tok], w2_lo[:, j, :], start=False, stop=False)
                        mm = nc.tensor.matmul(y[hf][t], hs_lo[b][:, tok], w2_hi[:, j, :], start=False, stop=end)
                        if end:
                            mm.then_inc(y_done, 1)
                    if not end:
                        mm.then_inc(hs_used, 1)
                return step
            over_blocks(pe, inner)
            pe.wait_ge(w2_lo_done, NJ)
            pe.wait_ge(h_done, NH * NJ)
            for hf in range(NH):
                over_blocks(pe, outer(hf))
    ph.close()


class TurnSems:

    def __init__(self, ph):
        self.turned = ph.sem("turned")
        self.hi = ph.sem("turned_hi")
        self.lo = ph.sem("turned_lo")


def project_phase(nc, name, x, ident, q_nat, kv_nat, w_dram, bias_dram, rope_dram):
    kvw = kv_nat.shape[2]
    nw = D + kvw
    ph = Phase(nc, name)
    st = ph.sb("stats", [P, TT, 6])
    mv = ph.sb("moments", [P, TT, 2])
    rstd = ph.sb("rstd", [P, 3, TT])
    xn = ph.sb("xn", [P, 2, D])
    xt_hi = ph.sb("xt_hi", [P, KC, T], F32R)
    xt_lo = ph.sb("xt_lo", [P, KC, T], F32R)
    raw = ph.sb("raw", [P, KC, nw])
    w_hi = ph.sb("w_hi", [P, KC, nw], F32R)
    w_lo = ph.sb("w_lo", [P, KC, nw], F32R)
    bank = [ph.ps(f"bank{b}", [P, 4, P]) for b in range(6)]
    flat = [b[:, :, :].rearrange("p a b -> p (a b)") for b in bank]
    turn, q_ps, kv_ps = bank[0:2], flat[2:4], flat[4:6]
    s = NormSems(ph)
    w_in, w_hi_done, w_lo_done = ph.sem("w_in"), ph.sem("w_hi_done"), ph.sem("w_lo_done")
    extra_in = ph.sem("extra_in")
    q_done, kv_done, taken = ph.sem("q_done"), ph.sem("kv_done"), ph.sem("taken")
    if bias_dram is not None:
        bias = ph.sb("bias", [P, nw])
    else:
        rope = ph.sb("rope", [P, TT, 2, HD])
        swap = ph.sb("swap", [P, H + HKV1, HD])
        rot_done, half_done = ph.sem("rot_done"), ph.sem("half_done")

    with nc.Block() as block:
        @block.sync
        def _(sp):
            sp.dma_start(raw[:, :, :], w_dram).then_inc(w_in, 16)
            if bias_dram is not None:
                sp.dma_start(bias[:, :], bias_dram.to_broadcast((P, nw))).then_inc(extra_in, 16)
            else:
                sp.dma_start(rope[:, :, :, :], rope_dram).then_inc(extra_in, 16)

        @block.scalar
        def _(act):
            act.wait_ge(w_in, 16)
            nc.scalar.activation(w_hi[:, :, :], raw[:, :, :], ACT.Copy).then_inc(w_hi_done, 1)
            norm_scalar(nc, act, s, turn, xt_hi)

        @block.vector
        def _(dve):
            norm_vector(nc, dve, s, x, st, mv, rstd, xn, turn, xt_hi, xt_lo)
            dve.wait_ge(w_hi_done, 1)
            nc.vector.tensor_tensor(w_lo[:, :, :], raw[:, :, :], w_hi[:, :, :].bitcast(F32),
                                    ALU.subtract).then_inc(w_lo_done, 1)
            dve.wait_ge(extra_in, 16)
            for t in range(TT):
                dve.wait_ge(q_done, t + 1)
                dve.wait_ge(kv_done, t + 1)
                if bias_dram is not None:
                    nc.vector.tensor_tensor(q_nat[:, t, :], q_ps[t % 2], bias[:, 0:D], ALU.add).then_inc(taken, 1)
                    nc.vector.tensor_tensor(kv_nat[:, t, :], kv_ps[t % 2][:, 0:kvw], bias[:, D:nw],
                                            ALU.add).then_inc(taken, 1)
                    continue
                kw = kvw // 2
                qh = q_ps[t % 2].rearrange("p (h d) -> p h d", d=HD)
                kh = kv_ps[t % 2][:, 0:kw].rearrange("p (h d) -> p h d", d=HD)
                qo = q_nat[:, t, :].rearrange("p (h d) -> p h d", d=HD)
                ko = kv_nat[:, t, 0:kw].rearrange("p (h d) -> p h d", d=HD)
                half = HD // 2
                if t >= 1:
                    dve.wait_ge(rot_done, 2 * t)
                for src, out, lo, n in ((qh, qo, 0, H), (kh, ko, H, HKV1)):
                    def table(which, a, b):
                        return rope[:, t, which, a:b].unsqueeze(1).to_broadcast((P, n, b - a))
                    nc.vector.tensor_tensor(out, src, table(0, 0, HD), ALU.mult).then_inc(half_done, 1)
                    for a in (0, half):
                        b = half - a
                        nc.vector.tensor_tensor(swap[:, lo:lo + n, a:a + half], src[:, :, b:b + half],
                                                table(1, a, a + half), ALU.mult).then_inc(half_done, 1)
                nc.vector.tensor_copy(kv_nat[:, t, kw:kvw], kv_ps[t % 2][:, kw:kvw]).then_inc(taken, 1)
                dve.wait_ge(half_done, 6 * (t + 1))
                nc.vector.tensor_tensor(qo, qo, swap[:, 0:H, :], ALU.add).then_inc(rot_done, 1)
                nc.vector.tensor_tensor(ko, ko, swap[:, H:, :], ALU.add).then_inc(rot_done, 1)

        @block.tensor
        def _(pe):
            norm_tensor(nc, pe, s, xn, ident, turn)
            pe.wait_ge(w_lo_done, 1)
            taken_per_tile = 2 if bias_dram is not None else 1
            for t in range(TT):
                tok = slice(t * P, (t + 1) * P)
                pe.wait_ge(s.lo, t + 1)
                if t >= 2:
                    pe.wait_ge(taken, taken_per_tile * (t - 1))
                for out, cols, done in ((q_ps[t % 2], slice(0, D), q_done),
                                        (kv_ps[t % 2][:, 0:kvw], slice(D, nw), kv_done)):
                    for c in range(KC):
                        nc.tensor.matmul(out, xt_hi[:, c, tok], w_hi[:, c, cols], start=c == 0, stop=False)
                        nc.tensor.matmul(out, xt_hi[:, c, tok], w_lo[:, c, cols], start=False, stop=False)
                        mm = nc.tensor.matmul(out, xt_lo[:, c, tok], w_hi[:, c, cols], start=False,
                                              stop=c == KC - 1)
                    mm.then_inc(done, 1)
    ph.close()


def output_phase(nc, name, x, ident, ao, w_dram, bias_dram):
    ph = Phase(nc, name)
    at_hi = ph.sb("at_hi", [P, KC, T], F32R)
    at_lo = ph.sb("at_lo", [P, KC, T], F32R)
    raw = ph.sb("raw", [P, KC, D])
    w_hi = ph.sb("w_hi", [P, KC, D], F32R)
    w_lo = ph.sb("w_lo", [P, KC, D], F32R)
    bank = [ph.ps(f"bank{b}", [P, 4, P]) for b in range(4)]
    turn = bank[0:2]
    out = [b[:, :, :].rearrange("p a b -> p (a b)") for b in bank[2:4]]
    s = TurnSems(ph)
    w_in, w_hi_done, w_lo_done = ph.sem("w_in"), ph.sem("w_hi_done"), ph.sem("w_lo_done")
    bias_in, biased = ph.sem("bias_in"), ph.sem("biased")
    y_done, x_done = ph.sem("y_done"), ph.sem("x_done")
    if bias_dram is not None:
        bias = ph.sb("bias", [P, D])

    with nc.Block() as block:
        @block.sync
        def _(sp):
            sp.dma_start(raw[:, :, :], w_dram).then_inc(w_in, 16)
            if bias_dram is not None:
                sp.dma_start(bias[:, :], bias_dram.to_broadcast((P, D))).then_inc(bias_in, 16)

        @block.scalar
        def _(act):
            act.wait_ge(w_in, 16)
            nc.scalar.activation(w_hi[:, :, :], raw[:, :, :], ACT.Copy).then_inc(w_hi_done, 1)
            for t in range(TT):
                act.wait_ge(s.turned, t + 1)
                nc.scalar.activation(at_hi[:, :, t * P:(t + 1) * P], turn[t % 2][:, :, :],
                                     ACT.Copy).then_inc(s.hi, 1)

        @block.vector
        def _(dve):
            dve.wait_ge(w_hi_done, 1)
            nc.vector.tensor_tensor(w_lo[:, :, :], raw[:, :, :], w_hi[:, :, :].bitcast(F32),
                                    ALU.subtract).then_inc(w_lo_done, 1)
            if bias_dram is not None:
                dve.wait_ge(bias_in, 16)
                for t in range(TT):
                    nc.vector.tensor_tensor(x[:, t, :], x[:, t, :], bias[:, :], ALU.add).then_inc(biased, 1)
                dve.wait_ge(biased, TT)
            for t in range(TT + 1):
                if t < TT:
                    dve.wait_ge(s.hi, t + 1)
                    nc.vector.tensor_tensor(at_lo[:, :, t * P:(t + 1) * P], turn[t % 2][:, :, :],
                                            at_hi[:, :, t * P:(t + 1) * P].bitcast(F32),
                                            ALU.subtract).then_inc(s.lo, 1)
                if t >= 1:
                    dve.wait_ge(y_done, t)
                    nc.vector.tensor_tensor(x[:, t - 1, :], x[:, t - 1, :], out[(t - 1) % 2],
                                            ALU.add).then_inc(x_done, 1)

        @block.tensor
        def _(pe):
            def turn_tile(t):
                if t >= 2:
                    pe.wait_ge(s.lo, t - 1)
                for c in range(KC):
                    last = nc.tensor.transpose(turn[t % 2][:, c, :], ao[:, t, c * P:(c + 1) * P], ident[:, :])
                last.then_inc(s.turned, 1)
            turn_tile(0)
            for t in range(TT):
                if t + 1 < TT:
                    turn_tile(t + 1)
                if t == 0:
                    pe.wait_ge(w_lo_done, 1)
                if t >= 2:
                    pe.wait_ge(x_done, t - 1)
                pe.wait_ge(s.lo, t + 1)
                tok = slice(t * P, (t + 1) * P)
                for c in range(KC):
                    nc.tensor.matmul(out[t % 2], at_hi[:, c, tok], w_hi[:, c, :], start=c == 0, stop=False)
                    nc.tensor.matmul(out[t % 2], at_hi[:, c, tok], w_lo[:, c, :], start=False, stop=False)
                    mm = nc.tensor.matmul(out[t % 2], at_lo[:, c, tok], w_hi[:, c, :], start=False,
                                          stop=c == KC - 1)
                mm.then_inc(y_done, 1)
    ph.close()


def attend_phase(nc, name, ident, ident_b, causal, q_nat, kv_nat, ao, sparse):
    ph = Phase(nc, name)
    kvw = kv_nat.shape[2]
    KSET = 2 if sparse else 1
    qx = [ph.sb(f"qx{p}", [P, TT, 2, 2 * SR]) for p in range(2)]
    kx = ph.sb("kx", [P, TT, 3 * SR])
    qs = [[ph.sb(f"qs{p}{i}", [MR + 4, T], F32R) for i in range(2)] for p in range(2)]
    ks = [[ph.sb(f"ks{p}{e}", [MR + 4, T], F32R) for e in range(2)] for p in range(KSET)]
    v1 = [ph.sb(f"v1{p}", [P, TT, 32]) for p in range(KSET)]
    sel = ph.sb("sel", [P, 2])
    mx = [ph.sb(f"mx{p}", [P, TT, G, 8]) for p in range(2)]
    nm = [ph.sb(f"nm{p}", [P, TT, G, 2]) for p in range(2)]
    pt = [[ph.sb(f"pt{s}{a}", [P, HALF]) for a in range(G)] for s in range(2)]
    ot_sb = ph.sb("ot_sb", [P, HALF])
    rden = ph.sb("rden", [P, TH, G])
    if sparse:
        cm = [ph.sb(f"cm{r}", [P, NCH]) for r in range(4)]
        cr = [ph.sb(f"cr{r}", [P, NCH]) for r in range(4)]
        drop = [ph.sb(f"drop{r}", [P, NCH], BF16) for r in range(2)]
        mark = ph.sb("mark", [P, 1])
        idle = ph.sb("idle", [P, 1])
        settled = ph.sem("settled")
        spare = ph.sb("spare", [P, 1])
        spared = ph.sem("spared")
        price = ph.sb("price", [P, (TT - 2) * P], BF16)
        mk = [[[ph.sb(f"mk{p}{a}{t}", [P, (t - 1) * P], BF16) for t in range(2, TT)] for a in range(G)]
              for p in range(2)]
        cm_done, top_done, cr_done = ph.sem("cm_done"), ph.sem("top_done"), ph.sem("cr_done")
        drop_done, mk_done = ph.sem("drop_done"), ph.sem("mk_done")

    sa = [ph.ps(f"sa{r}", [P, T]) for r in range(2)]
    sb = [ph.ps(f"sb{r}", [P, HALF]) for r in range(2)]
    ot = ph.ps("ot", [P, HALF])
    tr = ph.ps("tr", [P, TH, P])

    const_done = ph.sem("const_done")
    mask_const = ph.sem("mask_const")
    qx_done, kx_done, v1_done = ph.sem("qx_done"), ph.sem("kx_done"), ph.sem("v1_done")
    tr_done, tr_free = ph.sem("tr_done"), ph.sem("tr_free")
    sa_done, max_done = ph.sem("sa_done"), ph.sem("max_done")
    nm_hi, nm_done = ph.sem("nm_hi"), ph.sem("nm_done")
    sb_done, exp_done, av_done = ph.sem("sb_done"), ph.sem("exp_done"), ph.sem("av_done")
    ot_out, rden_done, ao_done = ph.sem("ot_out"), ph.sem("rden_done"), ph.sem("ao_done")

    NSTEP = sum(4 * g + 4 for g in range(NH))
    STEPS = [(g, kb) for g in range(NH) for kb in range(4 * g + 4)]
    NG = H // G
    NA = TT * G
    NB = NSTEP * G
    A_UNITS = [(t, a) for t in range(TT) for a in range(G)]
    LATE = [(t, a) for t, a in A_UNITS if t >= 2]
    B0 = 4 * G

    def slot_items(n=None):
        after = {v: [] for v in range(-1, NB)}
        after[-1] += [("k", 1, 0, 0), ("k", 1, 0, 1)]
        for v in range(NA // 2):
            after[v].append(("a", v))
            after[B0 + v * 28 // 16].append(("a", NA // 2 + v))
        after[NB - 3].append(("s",))
        after[2].append(("w", -1, NSTEP - 1))
        after[3].append(("o", -1, 1))
        for v, use in ((1, ("m", 0, 1, 0)), (4, ("m", 0, 1, 1)), (6, ("f", -1, 1)), (8, ("q", 1, 1, 0)),
                       (10, ("q", 1, 1, 1)), (12, ("k", 1, 1, 0)), (14, ("k", 1, 1, 1)), (24, ("f", 0, 0)),
                       (27, ("q", 2, 0, 0)), (29, ("q", 2, 0, 1)), (32, ("m", 1, 0, 0)), (35, ("m", 1, 0, 1))):
            after[v].append(use)
        after[21].append(("o", 0, 0))
        for s in range(NSTEP - 1):
            after[G * s + 2 * G - 1].append(("w", 0, s))
        items = list(after[-1])
        for v in range(NB):
            items += [("b", v)] + after[v]
        return kept(items, n)

    def group_of(item):
        return {"b": 0, "a": 1, "s": 1}[item[0]] if item[0] in "bas" else item[1]

    def kept(items, n):
        return [x for x in items if (sparse or x[0] != "k") and (n is None or 0 <= n + group_of(x) < NG)]

    def first_items():
        items = [("k", 1, 0, 0), ("q", 1, 0, 0), ("k", 1, 0, 1), ("q", 1, 0, 1)]
        later = [("q", 1, 1, 0), ("q", 1, 1, 1), ("k", 1, 1, 0), ("k", 1, 1, 1)]
        for v in range(NA):
            items.append(("a", v))
            if v % 3 == 2 and later:
                items.append(later.pop(0))
        items.append(("s",))
        return kept(items + [("q", 2, 0, 0), ("q", 2, 0, 1), ("m", 1, 0, 0), ("m", 1, 0, 1)], -1)

    last_items = [("w", -1, NSTEP - 1), ("o", -1, 1), ("f", -1, 1)]

    def is_use(x):
        return x[0] in "kqmf"

    def uses(items):
        return sum(is_use(x) for x in items)

    K_ONCE = 0 if sparse else 2 * NH
    U_FIRST, U_SLOT = K_ONCE + uses(first_items()), uses(slot_items())

    def use_base(n, edge):
        if edge and n <= 0:
            return U_FIRST if n == 0 else K_ONCE
        if edge and n > NG - 2:
            return U_FIRST + sum(uses(slot_items(m)) for m in range(n))
        return n * U_SLOT + (U_FIRST - 1)

    def at(items, base, item):
        return base + uses(items[:items.index(item) + 1])

    def over_slots(eng, slot):
        slot(-1, 1, first_items(), use_base(-1, True), True)
        for n in range(2):
            slot(n, n, slot_items(n), use_base(n, True), True)
        with eng.Fori(1, NG // 2 - 1) as i:
            for p in range(2):
                slot(2 * i + p, p, slot_items(), use_base(2 * i + p, False), False)
        for n in range(NG - 2, NG):
            slot(n, n % 2, slot_items(n), use_base(n, True), True)
        slot(NG, 0, last_items, use_base(NG, True), True)

    def known(n, edge, m):
        return edge and n == m

    C_ALL = 3 + 4 * KSET

    with nc.Block() as block:
        @block.gpsimd
        def _(pool):
            def prepare_q(m, p, base):
                if base is not None:
                    pool.wait_ge(tr_done, base)
                src = q_nat[:, :, bass.ds(m * (G * HD), G * HD)].rearrange("p t (s w) -> p t s w", w=HD)
                v = qx[p][:, :, :, :].rearrange("p t i (e w) -> p t (i e) w", w=SR)
                hi, lo, third = (v[:, :, :, HD * c:HD * (c + 1)] for c in range(3))
                nc.gpsimd.tensor_copy(hi.bitcast(F32R), src).then_inc(qx_done, 1)
                nc.gpsimd.tensor_copy(third, src).then_inc(qx_done, 1)
                pool.wait_ge(qx_done, 4 * m + 2)
                nc.gpsimd.tensor_tensor(lo.bitcast(F32R), third, hi, ALU.subtract).then_inc(qx_done, 1)
                pool.wait_ge(qx_done, 4 * m + 3)
                nc.gpsimd.tensor_tensor(third.bitcast(F32R), third, lo, ALU.subtract).then_inc(qx_done, 1)

            def prepare_k(m, base):
                if base is not None:
                    pool.wait_ge(tr_done, base)
                src = kv_nat[:, :, bass.ds(m * HD, HD)] if sparse else kv_nat[:, :, 0:HD]
                hi, second, lo = (kx[:, :, SR + HD * c:SR + HD * (c + 1)] for c in range(3))
                nc.gpsimd.tensor_copy(hi.bitcast(F32R), src).then_inc(kx_done, 1)
                nc.gpsimd.tensor_copy(second.bitcast(F32R), src).then_inc(kx_done, 1)
                nc.gpsimd.tensor_copy(lo, src).then_inc(kx_done, 1)
                pool.wait_ge(kx_done, 4 * m + 3)
                nc.gpsimd.tensor_tensor(lo.bitcast(F32R), lo, hi, ALU.subtract).then_inc(kx_done, 1)

            def prepare_v(m, p, wait):
                if wait:
                    pool.wait_ge(av_done, NSTEP * (m - 1))
                src = kv_nat[:, :, bass.ds(m * HD + kvw // 2, HD)] if sparse else kv_nat[:, :, HD:2 * HD]
                nc.gpsimd.tensor_copy(v1[p][:, :, 0:HD], src).then_inc(v1_done, 1)

            def masks(m, p, wait, u0=0, u1=len(LATE) + 1):
                base = len(LATE) * m
                for u in range(u0, u1):
                    if u == 0 and wait:
                        pool.wait_ge(sb_done, NB * (m - 1))
                    if u < len(LATE):
                        pool.wait_ge(cr_done, base + u + 1)
                    if u >= 2:
                        pool.wait_ge(mk_done, base + u - 1)
                    if u == 0:
                        nc.gpsimd.tensor_tensor(spare[:, :], mark[:, :], mark[:, :], ALU.subtract).then_inc(spared, 1)
                    else:
                        t, a = LATE[u - 1]
                        nch = 8 * t
                        pool.wait_ge(drop_done, base + u)
                        nc.gpsimd.tensor_tensor(
                            mk[p][a][t - 2][:, :].rearrange("p (c w) -> p c w", w=CHUNK),
                            drop[(u - 1) % 2][:, 8:nch].unsqueeze(2).to_broadcast((P, nch - 8, CHUNK)),
                            price[:, (TT - 1 - t) * P:].rearrange("p (c w) -> p c w", w=CHUNK),
                            ALU.mult).then_inc(mk_done, 1)
                    if u < len(LATE):
                        nch = 8 * LATE[u][0]
                        nc.gpsimd.tensor_scalar(drop[u % 2][:, 8:nch], cr[u % 4][:, 8:nch], MARK, None,
                                                ALU.is_lt).then_inc(drop_done, 1)

            if sparse:
                nc.gpsimd.memset(mark[:, :], MARK).then_inc(mask_const, 1)
                nc.gpsimd.memset(price[:, :], NEG).then_inc(mask_const, 1)
                pool.wait_ge(mask_const, 2)
                nc.gpsimd.affine_select(out=price[:, -P:], in_=price[:, -P:], compare_op=ALU.is_ge, fill=0.0,
                                        base=0, pattern=[[-1, P]], channel_multiplier=1).then_inc(mask_const, 1)
                pool.wait_ge(mask_const, 3)

            def slot(n, p, items, base, edge):
                here = [n + 1 < NG, n + 2 < NG] if edge else [True, True]
                if known(n, edge, -1):
                    pool.wait_ge(const_done, 1 + 2 * KSET)
                    prepare_v(0, 0, False)
                    pool.wait_ge(qx_done, 4)
                    prepare_q(1, 1, None)
                    if sparse:
                        pool.wait_ge(kx_done, 4)
                        prepare_k(1, at(items, base, ("k", 1, 1, 1)))
                        masks(0, 0, False)
                    return
                if here[1]:
                    prepare_q(n + 2, p, base)
                if sparse and here[0]:
                    prepare_v(n + 1, 1 - p, not known(n, edge, 0))
                    masks(n + 1, 1 - p, not known(n, edge, 0), 0, 2 * G)
                    if here[1]:
                        prepare_k(n + 2, at(items, base, ("k", 1, 1, 1)))
                    masks(n + 1, 1 - p, not known(n, edge, 0), 2 * G)
            over_slots(pool, slot)

        @block.tensor
        def _(pe):
            def use(u, first=False):
                if not first:
                    pe.wait_ge(tr_free, u)

            def turn_k(g, e):
                for t in range(TH):
                    mm = nc.tensor.transpose(tr[0:MR, t, :], kx[:, TH * g + t, SR * (1 - e):SR * (3 - e)], ident[:, :])
                mm.then_inc(tr_done, 1)

            def slot(n, p, items, base, edge):
                pos = base
                for x in items:
                    kind = x[0]
                    if is_use(x):
                        use(pos, known(n, edge, -1) and sparse and pos == 0)
                        pos = pos + 1
                    if kind == "k":
                        pe.wait_ge(kx_done, 4 * (n + 2))
                        turn_k(x[2], x[3])
                    elif kind == "q":
                        _, off, g, i = x
                        pe.wait_ge(qx_done, 4 * (n + off + 1))
                        for t in range(TH):
                            mm = nc.tensor.transpose(tr[0:MR, t, :], qx[(p + off) % 2][:, TH * g + t, i, :], ident[:, :])
                        mm.then_inc(tr_done, 1)
                    elif kind == "m":
                        _, off, g, i = x
                        pe.wait_ge(nm_done, NH * (n + off) + g + 1)
                        for t in range(TH):
                            mm = nc.tensor.transpose(
                                tr[0:4, t, :],
                                nm[(p + off) % 2][:, TH * g + t, 2 * i:2 * i + 2, :].rearrange("p a b -> p (a b)"),
                                ident[:, :])
                        mm.then_inc(tr_done, 1)
                    elif kind == "f":
                        _, off, g = x
                        pe.wait_ge(ot_out, NH * (n + off) + g + 1)
                        for t in range(TH):
                            mm = nc.tensor.transpose(tr[:, t, :], ot_sb[:, t * P:(t + 1) * P], ident[:, :])
                        mm.then_inc(tr_done, 1)
                    elif kind == "a":
                        v = x[1]
                        t, a = A_UNITS[v]
                        m, pm = n + 1, (p + 1) % 2
                        k = ks[pm if sparse else 0]
                        if v % (NA // 2) == 0:
                            own = [y for y in items if y[0] in "kq" and y[1] == 1 and y[2] == v // (NA // 2)]
                            pe.wait_ge(tr_free, at(items, base, own[-1]) if own else base)
                        if not (known(n, edge, -1) and v < 2):
                            pe.wait_ge(max_done, NA * m + v - 1)
                        q, out, w = qs[pm][a // 2][0:MR, t * P:(t + 1) * P], sa[a % 2], (t + 1) * P
                        for c0 in range(0, w, HALF):
                            c1 = min(c0 + HALF, w)
                            nc.tensor.matmul(out[:, c0:c1], q, k[a % 2][0:MR, c0:c1], start=True, stop=c1 < w,
                                             skip_group_check=True)
                        nc.tensor.matmul(out[:, w - P:w], ident_b[:, :], causal[:, :], start=False, stop=True,
                                         skip_group_check=True).then_inc(sa_done, 1)
                    elif kind == "b":
                        v = x[1]
                        s, a = v // G, v % G
                        g, kb = STEPS[s]
                        k = ks[p if sparse else 0]
                        if known(n, edge, 0) and v == 0:
                            pe.wait_ge(const_done, C_ALL)
                        if v == 0:
                            pe.wait_ge(tr_free, base)
                        if v == B0:
                            pe.wait_ge(tr_free, at(items, base, ("m", 0, 1, 1)))
                        if sparse and (g, kb, a) == (0, 1, 0):
                            pe.wait_ge(mk_done, len(LATE) * n + sum(t < TH for t, _ in LATE))
                        if sparse and v == B0:
                            pe.wait_ge(mk_done, len(LATE) * (n + 1))
                        if not (known(n, edge, 0) and v < 2):
                            pe.wait_ge(exp_done, NB * n + v - 1)
                        late = [t for t in range(TH * g, TH * (g + 1)) if sparse and t >= 2 and 1 <= kb <= t - 1]
                        adds = [(causal[:, :], kb)] if kb >= 4 * g else []
                        adds += [(mk[p][a][t - 2][:, (kb - 1) * P:kb * P], t) for t in late]
                        c0 = max(0, (kb - 4 * g) * P)
                        mm = nc.tensor.matmul(sb[a % 2][:, c0:HALF], k[a % 2][:, kb * P:(kb + 1) * P],
                                              qs[p][a // 2][:, HALF * g + c0:HALF * (g + 1)], start=True,
                                              stop=not adds, skip_group_check=True)
                        for y, (msk, t) in enumerate(adds):
                            c = t * P - HALF * g
                            mm = nc.tensor.matmul(sb[a % 2][:, c:c + P], msk, ident_b[:, :], start=False,
                                                  stop=y == len(adds) - 1, skip_group_check=True)
                        mm.then_inc(sb_done, 1)
                    elif kind == "w":
                        _, off, s = x
                        g, kb = STEPS[s]
                        m, pm = n + off, (p + off) % 2
                        c0 = max(0, (kb - 4 * g) * P)
                        pe.wait_ge(exp_done, NB * m + G * (s + 1))
                        if kb == 0 and not (known(n, edge, 0) and g == 0):
                            pe.wait_ge(ot_out, NH * m + g)
                        if s == 0:
                            pe.wait_ge(v1_done, m + 1 if sparse else 1)
                        for a in range(G):
                            mm = nc.tensor.matmul(ot[32 * a:32 * a + 32, c0:HALF],
                                                  v1[pm if sparse else 0][:, kb, :], pt[s % 2][a][:, c0:HALF],
                                                  start=kb == 0, stop=kb == 4 * g + 3, skip_group_check=True)
                        mm.then_inc(av_done, 1)

            if not sparse:
                pe.wait_ge(kx_done, 4)
                for g in range(NH):
                    for e in range(2):
                        use(2 * g + e, g + e == 0)
                        turn_k(g, e)
            over_slots(pe, slot)

        @block.scalar
        def _(act):
            def rows(dst, src, u):
                act.wait_ge(tr_done, u + 1)
                nc.scalar.activation(dst, src, ACT.Copy).then_inc(tr_free, 1)

            def half_of(stack, r0, r1, g):
                return stack[r0:r1, g * HALF:(g + 1) * HALF].rearrange("p (t w) -> p t w", w=P)

            def slot(n, p, items, base, edge):
                pos = base
                for x in items:
                    kind = x[0]
                    if kind == "k":
                        rows(half_of(ks[(p + 1) % 2][x[3]], 0, MR, x[2]), tr[0:MR, :, :], pos)
                    elif kind == "q":
                        rows(half_of(qs[(p + x[1]) % 2][x[3]], 0, MR, x[2]), tr[0:MR, :, :], pos)
                    elif kind == "m":
                        rows(half_of(qs[(p + x[1]) % 2][x[3]], MR, MR + 4, x[2]), tr[0:4, :, :], pos)
                    elif kind == "b":
                        v = x[1]
                        s, a = v // G, v % G
                        g, kb = STEPS[s]
                        c0 = max(0, (kb - 4 * g) * P)
                        act.wait_ge(sb_done, NB * n + v + 1)
                        if a == 0 and not (known(n, edge, 0) and s < 2):
                            act.wait_ge(av_done, NSTEP * n + s - 1)
                        nc.scalar.activation(pt[s % 2][a][:, c0:HALF], sb[a % 2][:, c0:HALF], ACT.Exp,
                                             scale=HD ** -0.5).then_inc(exp_done, 1)
                    if is_use(x):
                        pos = pos + 1

            if not sparse:
                for g in range(NH):
                    for e in range(2):
                        rows(half_of(ks[0][e], 0, MR, g), tr[0:MR, :, :], 2 * g + e)
            over_slots(act, slot)

        @block.vector
        def _(dve):
            nc.vector.memset(kx[:, :, :], 0.0).then_inc(const_done, 1)
            for v in v1:
                nc.vector.memset(v[:, :, :], 0.0).then_inc(const_done, 1)
            dve.wait_ge(const_done, 1 + KSET)
            hi, second, lo = (kx[:, :, SR + HD * c:SR + HD * (c + 1)] for c in range(3))
            src = kv_nat[:, :, 0:HD]
            nc.vector.tensor_copy(hi.bitcast(F32R), src).then_inc(kx_done, 1)
            nc.vector.tensor_copy(second.bitcast(F32R), src).then_inc(kx_done, 1)
            dve.wait_ge(kx_done, 2)
            nc.vector.tensor_tensor(lo.bitcast(F32R), src, hi, ALU.subtract).then_inc(kx_done, 2)
            src = q_nat[:, :, 0:G * HD].rearrange("p t (s w) -> p t s w", w=HD)
            v = qx[0][:, :, :, :].rearrange("p t i (e w) -> p t (i e) w", w=SR)
            hi, lo, third = (v[:, :, :, HD * c:HD * (c + 1)] for c in range(3))
            nc.vector.tensor_copy(hi.bitcast(F32R), src).then_inc(qx_done, 1)
            nc.vector.tensor_copy(third.bitcast(F32R), src).then_inc(qx_done, 1)
            dve.wait_ge(qx_done, 2)
            nc.vector.tensor_tensor(lo.bitcast(F32R), src, hi, ALU.subtract).then_inc(qx_done, 2)
            for v in v1:
                nc.vector.memset(v[:, :, HD:HD + 1], 1.0).then_inc(const_done, 1)
            for e in range(2):
                nc.vector.tensor_tensor(sel[:, e:e + 1], ident[:, MR + 2 * e:MR + 2 * e + 1],
                                        ident[:, MR + 2 * e + 1:MR + 2 * e + 2], ALU.add).then_inc(const_done, 1)
            dve.wait_ge(const_done, 3 + 2 * KSET)
            for pair in ks:
                for e, k in enumerate(pair):
                    nc.vector.tensor_copy(k[MR:MR + 4, :],
                                          sel[MR:MR + 4, e:e + 1].to_broadcast((4, T))).then_inc(const_done, 1)
            if sparse:
                dve.wait_ge(mask_const, 3)

            def late_of(v):
                return LATE.index(A_UNITS[v]) if 0 <= v < NA and A_UNITS[v] in LATE else None

            def chunk_maxima(m, start, v):
                t, a = A_UNITS[v]
                unit = NA * m + v
                if not (start and v == 0):
                    dve.wait_ge(max_done, unit)
                if not (start and v < 2):
                    dve.wait_ge(top_done, unit - 1)
                u = late_of(v - 2)
                if u is not None and not (start and u < 4):
                    dve.wait_ge(drop_done, len(LATE) * m + u - 3)
                if late_of(v - 4) is not None:
                    dve.wait_ge(cr_done, len(LATE) * m + late_of(v - 4) + 1)
                dve.wait_ge(sa_done, unit + 1)
                nc.vector.tensor_reduce(cm[v % 4][:, 0:8 * t + 8],
                                        sa[a % 2][:, 0:(t + 1) * P].rearrange("p (c w) -> p c w", w=CHUNK),
                                        AX.X, ALU.max).then_inc(max_done, 1)

            def largest(pm, v):
                t, a = A_UNITS[v]
                nc.vector.max(mx[pm][:, t, a, :], cm[v % 4][:, 0:8 * t + 8]).then_inc(top_done, 1)

            def match(pm, v):
                t, a = A_UNITS[v]
                if (t, a) in LATE:
                    nc.vector.match_replace(out=cr[late_of(v) % 4][:, 0:8 * t + 8],
                                            in_to_replace=mx[pm][:, t, a, :], in_values=cm[v % 4][:, 0:8 * t + 8],
                                            imm_value=MARK).then_inc(cr_done, 1)

            def settle(m, v):
                dve.wait_ge(max_done, NA * m + NA)
                dve.wait_ge(top_done, NA * m + v - 1)
                dve.wait_ge(drop_done, len(LATE) * m + late_of(v - 2) - 3)
                nc.vector.tensor_copy(idle[:, :], mark[:, :]).then_inc(settled, 1)

            def split_maxima(m, pm, g):
                top = mx[pm][:, TH * g:TH * (g + 1), :, 0]
                out = nm[pm][:, TH * g:TH * (g + 1), :, :]
                dve.wait_ge(top_done if sparse else max_done, NA * m + G * TH * (g + 1))
                nc.vector.tensor_scalar(out[:, :, :, 0].bitcast(F32R), top, -1.0, None, ALU.mult).then_inc(nm_hi, 1)
                dve.wait_ge(nm_hi, NH * m + g + 1)
                nc.vector.scalar_tensor_tensor(out[:, :, :, 1].bitcast(F32R), top, -1.0, out[:, :, :, 0],
                                               ALU.mult, ALU.subtract).then_inc(nm_done, 1)

            def slot(n, p, items, base, edge):
                m, pm = n + 1, (p + 1) % 2
                start = known(n, edge, -1)
                pos = base
                for x in items:
                    kind = x[0]
                    if kind == "a" and sparse:
                        v = x[1]
                        chunk_maxima(m, start, v)
                        if v >= 1:
                            largest(pm, v - 1)
                        if v >= 2:
                            match(pm, v - 2)
                        if v == NA // 2 + 1:
                            split_maxima(m, pm, 0)
                    elif kind == "a":
                        v = x[1]
                        t, a = A_UNITS[v]
                        dve.wait_ge(sa_done, NA * m + v + 1)
                        nc.vector.tensor_reduce(mx[pm][:, t, a, 0:1], sa[a % 2][:, 0:(t + 1) * P], AX.X,
                                                ALU.max).then_inc(max_done, 1)
                        if v == NA // 2 - 1:
                            split_maxima(m, pm, 0)
                    elif kind == "s":
                        if sparse:
                            settle(m, NA)
                            largest(pm, NA - 1)
                            match(pm, NA - 2)
                            settle(m, NA + 1)
                            match(pm, NA - 1)
                        split_maxima(m, pm, 1)
                    elif kind == "o":
                        _, off, g = x
                        dve.wait_ge(av_done, NSTEP * (n + off) + 4 + 8 * g)
                        nc.vector.tensor_copy(ot_sb[:, :], ot[:, :]).then_inc(ot_out, 1)
                    elif kind == "f":
                        _, off, g = x
                        dve.wait_ge(tr_done, pos + 1)
                        heads = tr[:, :, :].rearrange("p t (a w) -> p t a w", w=32)
                        nc.vector.reciprocal(rden[:, :, :], heads[:, :, :, HD]).then_inc(rden_done, 1)
                        dve.wait_ge(rden_done, NH * (n + off) + g + 1)
                        nc.vector.tensor_tensor(
                            ao[:, TH * g:TH * (g + 1),
                               bass.ds((n + off) * (G * HD), G * HD)].rearrange("p t (a w) -> p t a w", w=HD),
                            heads[:, :, :, 0:HD], rden[:, :, :].unsqueeze(3).to_broadcast((P, TH, G, HD)),
                            ALU.mult).then_inc(tr_free, 1)
                    if is_use(x):
                        pos = pos + 1
            over_slots(dve, slot)
    ph.close()


def store_phase(nc, x, out_dram):
    ph = Phase(nc, "store")
    stored = ph.sem("stored")
    with nc.Block() as block:
        @block.sync
        def _(sp):
            sp.dma_start(out_dram.rearrange("(t p) d -> p t d", p=P), x[:, :, :]).then_inc(stored, 16)
            sp.wait_ge(stored, 16)
    ph.close()


def attention(nc, name, x, ident, ident_b, causal, t, layer, kvw):
    with ExitStack() as keep:
        q_nat = keep.enter_context(nc.sbuf_tensor(f"{name}_q", [P, TT, D], F32))
        kv_nat = keep.enter_context(nc.sbuf_tensor(f"{name}_kv", [P, TT, kvw], F32))
        ao = keep.enter_context(nc.sbuf_tensor(f"{name}_ao", [P, TT, D], F32))
        project_phase(nc, f"{name}p", x, ident, q_nat, kv_nat, t[f"{layer}_wqkv"], t.get(f"{layer}_bqkv"),
                      t.get("rope"))
        attend_phase(nc, f"{name}s", ident, ident_b, causal, q_nat, kv_nat, ao, sparse=layer == "L1")
        output_phase(nc, f"{name}o", x, ident, ao, t[f"{layer}_wo"], t.get(f"{layer}_bo"))


def program(nc, t):
    with ExitStack() as keep:
        x = keep.enter_context(nc.sbuf_tensor("x", [P, TT, D], F32))
        ident = keep.enter_context(nc.sbuf_tensor("ident", [P, P], F32))
        ident_b = keep.enter_context(nc.sbuf_tensor("ident_b", [P, P], BF16))
        causal = keep.enter_context(nc.sbuf_tensor("causal", [P, P], BF16))
        load_phase(nc, x, ident, ident_b, causal, t["x"])
        ffn_phase(nc, "ffn0a", x, ident, t["L0_w13"], t["L0_w2"], t["L0_scale"])
        attention(nc, "att0", x, ident, ident_b, causal, t, "L0", 2 * HD)
        ffn_phase(nc, "ffn0b", x, ident, t["L0_w13"], t["L0_w2"], t["L0_scale"])
        ffn_phase(nc, "ffn1a", x, ident, t["L1_w13"], t["L1_w2"], t["L1_scale"])
        attention(nc, "att1", x, ident, ident_b, causal, t, "L1", 2 * HKV1 * HD)
        ffn_phase(nc, "ffn1b", x, ident, t["L1_w13"], t["L1_w2"], t["L1_scale"])
        store_phase(nc, x, t["out"])


def kernel(**inputs):
    import numpy as np
    import concourse.bacc as bacc
    from concourse.bass_utils import run_bass_kernel_spmd

    arrays = {"x": np.ascontiguousarray(inputs["L0_attn_x"].reshape(T, D))}
    for layer in ("L0", "L1"):
        def in_blocks(w):
            return w.reshape(NJ, P, KC, P).transpose(0, 3, 2, 1)
        w1, w3, w2 = (inputs[f"{layer}_ffn_w{n}"] for n in (1, 3, 2))
        s1, s3, s2 = (inputs[f"{layer}_ffn_w{n}_scale"] for n in (1, 3, 2))
        arrays[f"{layer}_w13"] = np.ascontiguousarray(np.concatenate([in_blocks(w1), in_blocks(w3)], axis=2))
        arrays[f"{layer}_w2"] = np.ascontiguousarray(w2.T.reshape(NJ, P, KC, P))
        arrays[f"{layer}_scale"] = np.ascontiguousarray(np.concatenate([s1, s3, s2.T], axis=1))[None]
    def in_chunks(w):
        return np.ascontiguousarray(w.T.reshape(KC, P, -1).transpose(1, 0, 2))
    arrays["L0_wqkv"] = in_chunks(np.concatenate([inputs[f"L0_attn_w{n}_w"] for n in "qkv"]))
    arrays["L0_bqkv"] = np.concatenate([inputs[f"L0_attn_w{n}_b"] for n in "qkv"])[None]
    arrays["L0_wo"] = in_chunks(inputs["L0_attn_wo_w"])
    arrays["L0_bo"] = np.ascontiguousarray(inputs["L0_attn_wo_b"][None])
    arrays["L1_wqkv"] = in_chunks(np.concatenate([inputs[f"L1_attn_w{n}"] for n in "qkv"]))
    arrays["L1_wo"] = in_chunks(inputs["L1_attn_wo"])
    freq = (np.float32(1.0) / np.float32(10000.0) ** (np.arange(0, HD, 2, dtype=np.float32) / np.float32(HD)))
    angle = np.arange(T, dtype=np.float32)[:, None] * freq[None, :].astype(np.float32)
    cos, sin = np.cos(angle), np.sin(angle)
    rope = np.stack([np.concatenate([cos, cos], 1), np.concatenate([-sin, sin], 1)], 1)
    arrays["rope"] = np.ascontiguousarray(rope.reshape(TT, P, 2, HD).transpose(1, 0, 2, 3).astype(np.float32))
    nc = bacc.Bacc("TRN2", target_bir_lowering=False, num_devices=1)
    aps = {n: nc.dram_tensor(f"in_{n}", a.shape, mybir.dt.from_np(a.dtype), kind="ExternalInput").ap()
           for n, a in arrays.items()}
    aps["out"] = nc.dram_tensor("result", (T, D), F32, kind="ExternalOutput").ap()
    program(nc, aps)
    r = run_bass_kernel_spmd(nc, [{f"in_{n}": a for n, a in arrays.items()}], core_ids=[0])
    return r.results[0]["result"].reshape(1, T, D)
```

```python
import concourse.bass as bass
from concourse import mybir
from contextlib import ExitStack

F32 = mybir.dt.float32
F32R = mybir.dt.float32r
I32 = mybir.dt.int32
BF16 = mybir.dt.bfloat16
ALU = mybir.AluOpType
ACT = mybir.ActivationFunctionType
AX = mybir.AxisListType

P = 128
T = 1024
D = 512
TT = T // P
KC = D // P
INTER = 1792
NJ = INTER // P
HALF = 512
NH = T // HALF
TH = HALF // P
EPS = 1e-5
H, HD = 32, 16
HKV1 = 8
G = 4
SR = 3 * HD
MR = 2 * SR
CHUNK = 16
NCH = T // CHUNK
MARK = 3e38
RSQRT_MAGIC = 1597463007.0


NEG = -1e36
READY = 2


class Region:

    def __init__(self, nc, name, start, end):
        self.nc, self.name, self.next, self.end = nc, name, start, end

    def __call__(self, name, shape, dt=F32):
        size = 2 if dt == BF16 else 4
        for n in shape[1:]:
            size *= n
        offset, self.next = self.next, self.next + (size + 31) // 32 * 32
        assert self.next <= self.end, (self.name, name, self.next, self.end)
        return self.nc.alloc_sbuf_tensor_at(f"{self.name}_{name}", shape, dt, offset=offset)


class Phase:

    def __init__(self, nc, name, start=None, end=None):
        self.nc, self.name, self.stack, self.sems = nc, name, ExitStack(), []
        self.region = Region(nc, name, start, end)

    def sb(self, name, shape, dt=F32):
        return self.region(name, shape, dt)

    def ps(self, name, shape, dt=F32):
        return self.stack.enter_context(self.nc.psum_tensor(f"{self.name}_{name}", shape, dt))

    def sem(self, name):
        self.sems.append(self.nc.alloc_semaphore(f"{self.name}_{name}"))
        return self.sems[-1]

    def close(self):
        self.nc.clear_and_free_semaphores(self.sems)
        self.nc.all_engine_barrier()
        self.stack.close()


class Common:

    END = 229344

    def __init__(self, nc):
        r = Region(nc, "common", 16512, self.END)
        self.x = r("x", [P, TT, D])
        self.ident = r("ident", [P, P])
        self.ident_b = r("ident_b", [P, P], BF16)
        self.causal = r("causal", [P, P], BF16)
        self.scale = {layer: r(f"scale_{layer}", [P, NJ, 12]) for layer in ("L0", "L1")}
        self.st = r("stats", [P, TH, 6])
        self.mv = r("moments", [P, TH, 2])
        self.rstd = r("rstd", [P, 3, TH])
        self.xn = r("xn", [P, 2, D])
        over_xt = r.next
        self.xt_hi = r("xt_hi", [P, KC, T], F32R)
        self.xt_lo = r("xt_lo", [P, KC, T], F32R)
        self.free = r.next
        self.w13_hi = [r(f"w13_hi{b}", [P, 8, P], F32R) for b in range(2)]
        self.w13_lo = [r(f"w13_lo{b}", [P, 8, P], F32R) for b in range(2)]
        self.raw13 = [r(f"raw13_{b}", [P, 8, P]) for b in range(2)]
        self.after_w13 = r.next
        stacks = Region(nc, "stacks", self.free, self.after_w13)
        self.qx0 = stacks("qx0", [P, TT, 2, 2 * SR])
        self.kx = stacks("kx", [P, TT, 3 * SR])
        self.v1 = [stacks(f"v1{p}", [P, TT, 32]) for p in range(2)]
        self.sel = stacks("sel", [P, 2])
        self.after_stacks = stacks.next
        over = Region(nc, "over_xt", over_xt, self.free)
        self.wo_raw = over("wo_raw", [P, KC, D])
        over.next = over_xt + 4 * KC * T
        self.ao = over("ao", [P, TT, D])
        kv_bytes = 4 * TT * 2 * HKV1 * HD
        self.q_at = self.END - kv_bytes - 4 * TT * D
        self.bias_at = self.q_at - 4 * D
        end = Region(nc, "end", self.q_at, self.END)
        self.q_nat = end("q", [P, TT, D])
        self.kv_nat = {"L1": end("kv1", [P, TT, 2 * HKV1 * HD])}
        end.next = self.q_at + 4 * TT * D
        self.kv_nat["L0"] = end("kv0", [P, TT, 2 * HD])
        end.next = self.bias_at
        self.bo = end("bo", [P, D])
        self.wo_hi = end("wo_hi", [P, KC, D], F32R)
        self.wo_lo = end("wo_lo", [P, KC, D], F32R)
        self.proj = {}
        for layer, nw in (("L0", D + 2 * HD), ("L1", D + 2 * HKV1 * HD)):
            raw = Region(nc, f"raw_{layer}", self.free, self.after_w13)("wqkv", [P, KC, nw])
            split = Region(nc, f"split_{layer}", self.after_w13, self.after_w13 + 4 * NJ * HALF)
            self.proj[layer] = (raw, split("wqkv_hi", [P, KC, nw], F32R), split("wqkv_lo", [P, KC, nw], F32R))


class Norm:

    def __init__(self, nc, ph, c, g, turn):
        self.nc, self.c, self.g, self.turn = nc, c, g, turn
        self.stats_done = ph.sem(f"norm{g}_stats")
        self.moments_done = ph.sem(f"norm{g}_moments")
        self.rstd_done = ph.sem(f"norm{g}_rstd")
        self.tile_done = ph.sem(f"norm{g}_tile")
        self.turned = ph.sem(f"norm{g}_turned")
        self.hi_done = ph.sem(f"norm{g}_hi")
        self.lo_done = ph.sem(f"norm{g}_lo")

    def tokens(self, t):
        return slice((TH * self.g + t) * P, (TH * self.g + t + 1) * P)

    def stats(self, dve, t):
        self.nc.vector.bn_stats(self.c.st[:, t, :], self.c.x[:, TH * self.g + t, :]).then_inc(self.stats_done, 1)

    def moments(self, dve):
        c, vector = self.c, self.nc.vector
        for t in range(TH):
            dve.wait_ge(self.stats_done, t + 1)
            vector.bn_aggr(c.mv[:, t, :], c.st[:, t, :]).then_inc(self.moments_done, 1)
        dve.wait_ge(self.moments_done, TH)
        y, var, tmp = (c.rstd[:, k, :] for k in range(3))
        vector.tensor_scalar(var, c.mv[:, :, 1], EPS, None, ALU.add).then_inc(self.rstd_done, 1)
        dve.wait_ge(self.rstd_done, 1)
        vector.tensor_scalar(tmp.bitcast(I32), var.bitcast(I32), 1, None,
                             ALU.logical_shift_right).then_inc(self.rstd_done, 1)
        dve.wait_ge(self.rstd_done, 2)
        vector.tensor_scalar(y.bitcast(I32), tmp.bitcast(I32), -1.0, RSQRT_MAGIC, ALU.mult,
                             ALU.add).then_inc(self.rstd_done, 1)

    def newton(self, dve, n):
        y, var, tmp = (self.c.rstd[:, k, :] for k in range(3))
        vector = self.nc.vector
        dve.wait_ge(self.rstd_done, 3 + 3 * n)
        vector.scalar_tensor_tensor(tmp, var, -0.5, y, ALU.mult, ALU.mult).then_inc(self.rstd_done, 1)
        dve.wait_ge(self.rstd_done, 4 + 3 * n)
        vector.tensor_tensor(tmp, tmp, y, ALU.mult).then_inc(self.rstd_done, 1)
        dve.wait_ge(self.rstd_done, 5 + 3 * n)
        vector.scalar_tensor_tensor(y, tmp, 1.5, y, ALU.add, ALU.mult).then_inc(self.rstd_done, 1)

    def scales(self, dve):
        for t in range(TH):
            self.stats(dve, t)
        self.moments(dve)
        for n in range(3):
            self.newton(dve, n)

    def tile(self, dve, t):
        c = self.c
        if t == 0:
            dve.wait_ge(self.rstd_done, 12)
        if t >= 2:
            dve.wait_ge(self.turned, t - 1)
        self.nc.vector.tensor_scalar(c.xn[:, t % 2, :], c.x[:, TH * self.g + t, :], c.mv[:, t, 0:1],
                                     c.rstd[:, 0, t:t + 1], ALU.subtract, ALU.mult).then_inc(self.tile_done, 1)

    def transpose(self, pe, t):
        pe.wait_ge(self.tile_done, t + 1)
        if t >= 2:
            pe.wait_ge(self.lo_done, t - 1)
        for k in range(KC):
            last = self.nc.tensor.transpose(self.turn[t % 2][:, k, :], self.c.xn[:, t % 2, k * P:(k + 1) * P],
                                            self.c.ident[:, :])
        last.then_inc(self.turned, 1)

    def upper(self, act, t):
        act.wait_ge(self.turned, t + 1)
        self.nc.scalar.activation(self.c.xt_hi[:, :, self.tokens(t)], self.turn[t % 2][:, :, :],
                                  ACT.Copy).then_inc(self.hi_done, 1)

    def lower(self, dve, t):
        dve.wait_ge(self.hi_done, t + 1)
        self.nc.vector.tensor_tensor(self.c.xt_lo[:, :, self.tokens(t)], self.turn[t % 2][:, :, :],
                                     self.c.xt_hi[:, :, self.tokens(t)].bitcast(F32),
                                     ALU.subtract).then_inc(self.lo_done, 1)


class FirstBlocks:

    def __init__(self, nc, ph, c, w13_dram, scale):
        self.nc, self.c, self.dram, self.scale = nc, c, w13_dram, scale
        self.arrived = [ph.sem(f"next_w13_in{b}") for b in range(READY)]
        self.scaled, self.hi_done, self.lo_done = (ph.sem(f"next_w13_{n}") for n in ("scaled", "hi", "lo"))

    def load(self, sp, b):
        sp.dma_start(self.c.raw13[b][:, :, :], self.dram[b, :, :, :]).then_inc(self.arrived[b], 16)

    def dequantise(self, pool, b):
        pool.wait_ge(self.arrived[b], 16)
        raw = self.c.raw13[b][:, :, :]
        self.nc.gpsimd.tensor_tensor(raw, raw, self.scale[:, b, 0:8].unsqueeze(2).to_broadcast((P, 8, P)),
                                     ALU.mult).then_inc(self.scaled, 1)

    def upper(self, act, b):
        act.wait_ge(self.scaled, b + 1)
        self.nc.scalar.activation(self.c.w13_hi[b][:, :, :], self.c.raw13[b][:, :, :],
                                  ACT.Copy).then_inc(self.hi_done, 1)

    def lower(self, dve, b):
        dve.wait_ge(self.hi_done, b + 1)
        self.nc.vector.tensor_tensor(self.c.w13_lo[b][:, :, :], self.c.raw13[b][:, :, :],
                                     self.c.w13_hi[b][:, :, :].bitcast(F32), ALU.subtract).then_inc(self.lo_done, 1)


class ProjectWeights:

    def __init__(self, nc, ph, dram, tensors):
        self.nc, self.dram, (self.raw, self.hi, self.lo) = nc, dram, tensors
        self.arrived, self.hi_done, self.lo_done = (ph.sem(f"wqkv_{n}") for n in ("in", "hi", "lo"))

    def load(self, sp):
        sp.dma_start(self.raw[:, :, :], self.dram).then_inc(self.arrived, 16)

    def upper(self, act, k):
        act.wait_ge(self.arrived, 16)
        self.nc.scalar.activation(self.hi[:, k, :], self.raw[:, k, :], ACT.Copy).then_inc(self.hi_done, 1)

    def lower(self, dve, k):
        dve.wait_ge(self.hi_done, k + 1)
        self.nc.vector.tensor_tensor(self.lo[:, k, :], self.raw[:, k, :], self.hi[:, k, :].bitcast(F32),
                                     ALU.subtract).then_inc(self.lo_done, 1)


def load_phase(nc, c, t):
    ph = Phase(nc, "load")
    turn = [ph.ps(f"turn{b}", [P, 4, P]) for b in range(2)]
    x_in = [ph.sem(f"x_in{t}") for t in range(TH + 1)]
    scale_in, scale1_in = ph.sem("scale_in"), ph.sem("scale1_in")
    made = ph.sem("made")
    first = FirstBlocks(nc, ph, c, t["L0_w13"], c.scale["L0"])
    norm = Norm(nc, ph, c, 0, turn)
    with nc.Block() as block:
        @block.sync
        def _(sp):
            x_dram = t["x"].rearrange("(t p) d -> p t d", p=P)
            for n in range(TH):
                sp.dma_start(c.x[:, n, :], x_dram[:, n, :]).then_inc(x_in[n], 16)
            sp.dma_start(c.scale["L0"][:, :, :], t["L0_scale"].to_broadcast((P, NJ, 12))).then_inc(scale_in, 16)
            for b in range(READY):
                first.load(sp, b)
            sp.dma_start(c.x[:, TH:, :], x_dram[:, TH:, :]).then_inc(x_in[TH], 16)
            sp.dma_start(c.scale["L1"][:, :, :], t["L1_scale"].to_broadcast((P, NJ, 12))).then_inc(scale1_in, 16)
            sp.wait_ge(x_in[TH], 16)
            sp.wait_ge(scale1_in, 16)

        @block.gpsimd
        def _(pool):
            nc.gpsimd.memset(c.ident[:, :], 0.0).then_inc(made, 1)
            nc.gpsimd.memset(c.ident_b[:, :], 0.0).then_inc(made, 1)
            nc.gpsimd.memset(c.causal[:, :], 0.0).then_inc(made, 1)
            pool.wait_ge(made, 3)
            for m in (c.ident, c.ident_b):
                nc.gpsimd.affine_select(out=m[:, :], in_=m[:, :], compare_op=ALU.not_equal, fill=1.0,
                                        base=0, pattern=[[-1, P]], channel_multiplier=1).then_inc(made, 1)
            nc.gpsimd.affine_select(out=c.causal[:, :], in_=c.causal[:, :], compare_op=ALU.is_ge, fill=NEG,
                                    base=0, pattern=[[-1, P]], channel_multiplier=1).then_inc(made, 1)
            pool.wait_ge(scale_in, 16)
            for b in range(READY):
                first.dequantise(pool, b)

        @block.vector
        def _(dve):
            for t in range(TH):
                dve.wait_ge(x_in[t], 16)
                norm.stats(dve, t)
            norm.moments(dve)
            for n in range(3):
                norm.newton(dve, n)
            norm.tile(dve, 0)
            norm.tile(dve, 1)
            first.lower(dve, 0)
            norm.lower(dve, 0)
            norm.tile(dve, 2)
            norm.lower(dve, 1)
            norm.tile(dve, 3)
            first.lower(dve, 1)
            norm.lower(dve, 2)
            norm.lower(dve, 3)

        @block.scalar
        def _(act):
            for b in range(READY):
                first.upper(act, b)
            for t in range(TH):
                norm.upper(act, t)

        @block.tensor
        def _(pe):
            pe.wait_ge(made, 4)
            for t in range(TH):
                norm.transpose(pe, t)
    ph.close()


def ffn_phase(nc, name, c, w13_dram, w2_dram, sc, next_ffn=None, next_projection=None,
              out_dram=None):
    ph = Phase(nc, name, c.after_w13, c.END)
    x, raw13, w13_hi, w13_lo, xt_hi, xt_lo = c.x, c.raw13, c.w13_hi, c.w13_lo, c.xt_hi, c.xt_lo
    h = ph.sb("h", [P, NH, NJ, HALF])
    w2_hi = ph.sb("w2_hi", [P, NJ, D], F32R)
    w2_lo = ph.sb("w2_lo", [P, NJ, D], F32R)
    raw2 = [ph.sb(f"raw2_{b}", [P, 4, P]) for b in range(2)]
    silu = [ph.sb(f"silu{b}", [P, HALF]) for b in range(2)]
    hs_hi = [ph.sb(f"hs_hi{b}", [P, HALF], F32R) for b in range(2)]
    hs_lo = [ph.sb(f"hs_lo{b}", [P, HALF], F32R) for b in range(2)]
    bank = [ph.ps(f"bank{b}", [P, 4, P]) for b in range(8)]
    turn = bank[4:6]
    flat = [b[:, :, :].rearrange("p a b -> p (a b)") for b in bank]
    gate, up = flat[0:2], flat[2:4]
    y = [flat[4:8], flat[0:4]]

    norm = Norm(nc, ph, c, 1, turn)
    following = next_ffn is not None or next_projection is not None
    norm_next = Norm(nc, ph, c, 0, turn) if following else None
    ffn_next = FirstBlocks(nc, ph, c, *next_ffn) if next_ffn is not None else None
    proj_next = ProjectWeights(nc, ph, *next_projection) if next_projection is not None else None
    w13_in = [ph.sem(f"w13_in{b}") for b in range(2)]
    w2_in = [ph.sem(f"w2_in{b}") for b in range(2)]
    w13_scaled, w2_scaled = ph.sem("w13_scaled"), ph.sem("w2_scaled")
    w13_hi_done, w2_hi_done = ph.sem("w13_hi_done"), ph.sem("w2_hi_done")
    w13_lo_done, w2_lo_done = ph.sem("w13_lo_done"), ph.sem("w2_lo_done")
    gate_done, up_done = ph.sem("gate_done"), ph.sem("up_done")
    silu_done, h_done = ph.sem("silu_done"), ph.sem("h_done")
    hs_hi_done, hs_lo_done, hs_used = ph.sem("hs_hi_done"), ph.sem("hs_lo_done"), ph.sem("hs_used")
    y_done, x_done, stored = ph.sem("y_done"), ph.sem("x_done"), ph.sem("stored")

    FIRST_UNITS = [(0, 0), (1, 0), (0, 1), (1, 1)]
    first_banks = [(gate[0], up[0]), (flat[6], flat[7]), (gate[1], up[1]), (flat[4], flat[5])]

    def middle_blocks(eng, step):
        with eng.Fori(1, NJ // 2 - 1) as i:
            for b in range(2):
                step(i, b, False)
        for b in range(2):
            step(NJ // 2 - 1, b, True)

    def second_begins(step):
        for b in range(2):
            step(0, 0, b, True, False)

    def second_goes_on(eng, step):
        middle_blocks(eng, lambda i, b, last: step(0, i, b, False, last))
        for j in range(NJ):
            step(1, j // 2, j % 2, j < 2, j >= NJ - 2)

    def part_free(eng, hf, i, b, first):
        if not first:
            eng.wait_ge(hs_used, (NJ - 1) * hf + 2 * i + b - 1)
        elif hf > 0:
            if b == 0:
                eng.wait_ge(hs_used, (NJ - 1) * hf)
            else:
                eng.wait_ge(y_done, TH * hf)

    with nc.Block() as block:
        @block.sync
        def _(sp):
            def load13(i, b):
                sp.dma_start(raw13[b][:, :, :], w13_dram[2 * i + b, :, :, :]).then_inc(w13_in[b], 16)

            def load2(i, b):
                sp.dma_start(raw2[b][:, :, :], w2_dram[2 * i + b, :, :, :]).then_inc(w2_in[b], 16)
            for b in range(2):
                load2(0, b)
            for b in range(2):
                load13(1, b)
            for b in range(2):
                sp.wait_ge(w2_lo_done, b + 1)
                load2(1, b)
            with sp.Fori(2, NJ // 2) as i:
                for b in range(2):
                    j = 2 * i + b
                    sp.wait_ge(w13_lo_done, j - 1 - READY)
                    load13(i, b)
                    sp.wait_ge(w2_lo_done, j - 1)
                    load2(i, b)
            if ffn_next is not None:
                for b in range(READY):
                    sp.wait_ge(w13_lo_done, NJ - 1 + b - READY)
                    ffn_next.load(sp, b)
            if proj_next is not None:
                sp.wait_ge(up_done, NH * NJ)
                proj_next.load(sp)
            if out_dram is not None:
                out = out_dram.rearrange("(t p) d -> p t d", p=P)
                parts = [slice(0, TH), slice(TH, TH + 2), slice(TH + 2, TT)]
                for tiles in parts:
                    sp.wait_ge(x_done, tiles.stop)
                    sp.dma_start(out[:, tiles, :], x[:, tiles, :]).then_inc(stored, 16)
                sp.wait_ge(stored, 16 * len(parts))

        @block.gpsimd
        def _(pool):
            def dequantise13(i, b):
                pool.wait_ge(w13_in[b], 16 * i)
                nc.gpsimd.tensor_tensor(raw13[b][:, :, :], raw13[b][:, :, :],
                                        sc[:, 2 * i + b, 0:8].unsqueeze(2).to_broadcast((P, 8, P)),
                                        ALU.mult).then_inc(w13_scaled, 1)

            def dequantise2(i, b):
                pool.wait_ge(w2_in[b], 16 * i + 16)
                nc.gpsimd.tensor_tensor(raw2[b][:, :, :], raw2[b][:, :, :],
                                        sc[:, 2 * i + b, 8:12].unsqueeze(2).to_broadcast((P, 4, P)),
                                        ALU.mult).then_inc(w2_scaled, 1)

            def both(i, b, last):
                dequantise13(i, b)
                dequantise2(i, b)
            for b in range(2):
                dequantise2(0, b)
            middle_blocks(pool, both)
            if ffn_next is not None:
                for b in range(READY):
                    ffn_next.dequantise(pool, b)

        @block.scalar
        def _(act):
            def upper13(j, b, early=False):
                act.wait_ge(w13_scaled, j + 1 - READY)
                act.wait_ge(up_done, 3 if early else 2 * j - 2)
                nc.scalar.activation(w13_hi[b][:, :, :], raw13[b][:, :, :], ACT.Copy).then_inc(w13_hi_done, 1)

            def upper2(j, b):
                act.wait_ge(w2_scaled, j + 1)
                nc.scalar.activation(w2_hi[:, j, :], raw2[b][:, :, :].rearrange("p a b -> p (a b)"),
                                     ACT.Copy).then_inc(w2_hi_done, 1)

            def silu_first(u):
                j, hf = FIRST_UNITS[u]
                act.wait_ge(gate_done, u + 1)
                if j == 1:
                    act.wait_ge(h_done, u)
                nc.scalar.activation(silu[hf][:, :], first_banks[u][0], ACT.Silu).then_inc(silu_done, 1)

            def inner(i, b, last):
                j = 2 * i + b
                if not (last and b == 1):
                    upper13(j + 1, 1 - b)
                upper2(j, b)
                for hf in range(NH):
                    if last and b == 1 and hf == 1:
                        act.wait_ge(h_done, 2)
                        second_begins(split)
                    act.wait_ge(gate_done, 2 * j + hf + 1)
                    act.wait_ge(h_done, 2 * j + hf - 1)
                    nc.scalar.activation(silu[hf][:, :], gate[hf], ACT.Silu).then_inc(silu_done, 1)

            def split(hf, i, b, first, last):
                part_free(act, hf, i, b, first)
                nc.scalar.activation(hs_hi[b][:, :], h[:, hf, 2 * i + b, :], ACT.Copy).then_inc(hs_hi_done, 1)
                if hf == 0 and last and ffn_next is not None:
                    if b == 0:
                        act.wait_ge(up_done, NH * NJ)
                    ffn_next.upper(act, b)
                if hf == 1:
                    j = 2 * i + b
                    if proj_next is not None and 2 <= j < 2 + KC:
                        if j == 2:
                            act.wait_ge(hs_lo_done, NJ)
                        proj_next.upper(act, j - 2)
                    if norm_next is not None and j in (8, 9, 11, 12):
                        norm_next.upper(act, (8, 9, 11, 12).index(j))

            silu_first(0)
            norm.upper(act, 0)
            norm.upper(act, 1)
            silu_first(1)
            norm.upper(act, 2)
            norm.upper(act, 3)
            upper2(0, 0)
            upper2(1, 1)
            silu_first(2)
            upper13(2, 0, early=True)
            silu_first(3)
            middle_blocks(act, inner)
            act.wait_ge(h_done, NH * NJ)
            second_goes_on(act, split)

        @block.vector
        def _(dve):
            def lower13(j, b):
                dve.wait_ge(w13_hi_done, j + 1 - READY)
                nc.vector.tensor_tensor(w13_lo[b][:, :, :], raw13[b][:, :, :], w13_hi[b][:, :, :].bitcast(F32),
                                        ALU.subtract).then_inc(w13_lo_done, 1)

            def lower2(j, b):
                dve.wait_ge(w2_hi_done, j + 1)
                nc.vector.tensor_tensor(w2_lo[:, j, :], raw2[b][:, :, :].rearrange("p a b -> p (a b)"),
                                        w2_hi[:, j, :].bitcast(F32), ALU.subtract).then_inc(w2_lo_done, 1)

            def h_first(u):
                j, hf = FIRST_UNITS[u]
                dve.wait_ge(up_done, u + 1)
                dve.wait_ge(silu_done, u + 1)
                nc.vector.tensor_tensor(h[:, hf, j, :], first_banks[u][1], silu[hf][:, :], ALU.mult).then_inc(h_done, 1)

            def inner(i, b, last):
                j = 2 * i + b
                if not (last and b == 1):
                    lower13(j + 1, 1 - b)
                lower2(j, b)
                for hf in range(NH):
                    if last and b == 1 and hf == 1:
                        dve.wait_ge(h_done, 2)
                        second_begins(split)
                    dve.wait_ge(up_done, 2 * j + hf + 1)
                    dve.wait_ge(silu_done, 2 * j + hf + 1)
                    nc.vector.tensor_tensor(h[:, hf, j, :], up[hf], silu[hf][:, :], ALU.mult).then_inc(h_done, 1)

            def add(hf):
                for t in range(TH):
                    dve.wait_ge(y_done, TH * hf + t + 1)
                    xs = x[:, TH * hf + t, :]
                    nc.vector.scalar_tensor_tensor(xs, y[hf][t], 0.5, xs, ALU.mult, ALU.add).then_inc(x_done, 1)

            def split(hf, i, b, first, last):
                n = hf * NJ + 2 * i + b
                part_free(dve, hf, i, b, first)
                dve.wait_ge(hs_hi_done, n + 1)
                nc.vector.tensor_tensor(hs_lo[b][:, :], h[:, hf, 2 * i + b, :],
                                        hs_hi[b][:, :].bitcast(F32), ALU.subtract).then_inc(hs_lo_done, 1)
                if hf == 0 and last and ffn_next is not None:
                    ffn_next.lower(dve, b)
                if hf == 1:
                    j = 2 * i + b
                    if j == 1:
                        add(0)
                    if proj_next is not None and j in (3, 5, 7, 10):
                        proj_next.lower(dve, (3, 5, 7, 10).index(j))
                    if norm_next is not None:
                        prepare_next(j)

            def prepare_next(j):
                if j == 2:
                    dve.wait_ge(x_done, TH)
                if j in (2, 3):
                    norm_next.stats(dve, 2 * j - 4)
                    norm_next.stats(dve, 2 * j - 3)
                if j == 4:
                    norm_next.moments(dve)
                    norm_next.newton(dve, 0)
                if j == 5:
                    norm_next.newton(dve, 1)
                    norm_next.newton(dve, 2)
                if j == 6:
                    norm_next.tile(dve, 0)
                    norm_next.tile(dve, 1)
                if j in (8, 9, 11, 12):
                    t = (8, 9, 11, 12).index(j)
                    norm_next.lower(dve, t)
                    if t < 2:
                        norm_next.tile(dve, t + 2)

            norm.scales(dve)
            norm.tile(dve, 0)
            norm.tile(dve, 1)
            h_first(0)
            norm.lower(dve, 0)
            norm.tile(dve, 2)
            norm.lower(dve, 1)
            norm.tile(dve, 3)
            norm.lower(dve, 2)
            norm.lower(dve, 3)
            h_first(1)
            lower2(0, 0)
            lower2(1, 1)
            h_first(2)
            lower13(2, 0)
            h_first(3)
            middle_blocks(dve, inner)
            dve.wait_ge(h_done, NH * NJ)
            second_goes_on(dve, split)
            add(1)

        @block.tensor
        def _(pe):
            def products(b, hf, banks, which=(0, 1)):
                cols = slice(hf * HALF, (hf + 1) * HALF)
                for w in which:
                    done = (gate_done, up_done)[w]
                    for k in range(KC):
                        w_hi, w_lo = w13_hi[b][:, 4 * w + k, :], w13_lo[b][:, 4 * w + k, :]
                        nc.tensor.matmul(banks[w], w_hi, xt_hi[:, k, cols], start=k == 0, stop=False)
                        nc.tensor.matmul(banks[w], w_hi, xt_lo[:, k, cols], start=False, stop=False)
                        mm = nc.tensor.matmul(banks[w], w_lo, xt_hi[:, k, cols], start=False, stop=k == KC - 1)
                    mm.then_inc(done, 1)

            def inner(i, b, last):
                j = 2 * i + b
                pe.wait_ge(w13_lo_done, j + 1 - READY)
                for hf in range(NH):
                    pe.wait_ge(h_done, 2 * j + hf - 1)
                    products(b, hf, (gate[hf], up[hf]))

            def outer(hf, i, b, first, last):
                n = hf * NJ + 2 * i + b
                j = 2 * i + b
                pe.wait_ge(hs_lo_done, n + 1)
                begin, end = first and b == 0, last and b == 1
                for t in range(TH):
                    tok = slice(t * P, (t + 1) * P)
                    nc.tensor.matmul(y[hf][t], hs_hi[b][:, tok], w2_hi[:, j, :], start=begin, stop=False)
                    nc.tensor.matmul(y[hf][t], hs_hi[b][:, tok], w2_lo[:, j, :], start=False, stop=False)
                    mm = nc.tensor.matmul(y[hf][t], hs_lo[b][:, tok], w2_hi[:, j, :], start=False, stop=end)
                    if end:
                        mm.then_inc(y_done, 1)
                if not end:
                    mm.then_inc(hs_used, 1)
                if hf == 1 and norm_next is not None and j in (6, 7, 9, 10):
                    norm_next.transpose(pe, (6, 7, 9, 10).index(j))

            products(0, 0, first_banks[0])
            norm.transpose(pe, 0)
            norm.transpose(pe, 1)
            products(1, 0, first_banks[1], which=(0,))
            norm.transpose(pe, 2)
            norm.transpose(pe, 3)
            products(1, 0, first_banks[1], which=(1,))
            pe.wait_ge(norm.lo_done, TH)
            products(0, 1, first_banks[2])
            products(1, 1, first_banks[3])
            middle_blocks(pe, inner)
            pe.wait_ge(w2_lo_done, NJ)
            second_begins(outer)
            pe.wait_ge(h_done, NH * NJ)
            second_goes_on(pe, outer)
    ph.close()


class TurnSems:

    def __init__(self, ph):
        self.turned = ph.sem("turned")
        self.hi = ph.sem("turned_hi")
        self.lo = ph.sem("turned_lo")


def project_phase(nc, name, c, layer, bias_dram, rope_dram):
    q_nat, kv_nat, xt_hi, xt_lo = c.q_nat, c.kv_nat[layer], c.xt_hi, c.xt_lo
    _, w_hi, w_lo = c.proj[layer]
    kvw = kv_nat.shape[2]
    nw = D + kvw
    ph = Phase(nc, name, c.after_w13 + 4 * NJ * HALF, c.q_at)
    bank = [ph.ps(f"bank{b}", [P, 4, P]) for b in range(6)]
    flat = [b[:, :, :].rearrange("p a b -> p (a b)") for b in bank]
    turn, q_ps, kv_ps = bank[0:2], flat[2:4], flat[4:6]
    cut = nw // 2 if bias_dram is not None else D
    norm = Norm(nc, ph, c, 1, turn)
    extra_in = ph.sem("extra_in")
    q_done, kv_done, taken = ph.sem("q_done"), ph.sem("kv_done"), ph.sem("taken")
    zeros, ones, stack_hi, stack_done = ph.sem("zeros"), ph.sem("ones"), ph.sem("stack_hi"), ph.sem("stack_done")
    if bias_dram is not None:
        bias = ph.sb("bias", [P, nw])
    else:
        rope = ph.sb("rope", [P, TT, 2, HD])
        swap = ph.sb("swap", [P, H + HKV1, HD])
        rot_done, half_done = ph.sem("rot_done"), ph.sem("half_done")

    with nc.Block() as block:
        @block.sync
        def _(sp):
            if bias_dram is not None:
                sp.dma_start(bias[:, :], bias_dram.to_broadcast((P, nw))).then_inc(extra_in, 16)
            else:
                sp.dma_start(rope[:, :, :, :], rope_dram).then_inc(extra_in, 16)

        @block.gpsimd
        def _(pool):
            nc.gpsimd.memset(c.kx[:, :, :], 0.0).then_inc(zeros, 1)
            for v in c.v1:
                nc.gpsimd.memset(v[:, :, :], 0.0).then_inc(zeros, 1)
            for e in range(2):
                nc.gpsimd.tensor_tensor(c.sel[:, e:e + 1], c.ident[:, MR + 2 * e:MR + 2 * e + 1],
                                        c.ident[:, MR + 2 * e + 1:MR + 2 * e + 2], ALU.add).then_inc(ones, 1)
            pool.wait_ge(zeros, 3)
            for v in c.v1:
                nc.gpsimd.memset(v[:, :, HD:HD + 1], 1.0).then_inc(ones, 1)
            v_from = kvw // 2 if layer == "L1" else HD
            for t in range(TT):
                if bias_dram is not None:
                    pool.wait_ge(taken, 3 * (t + 1))
                else:
                    pool.wait_ge(taken, t + 1)
                    pool.wait_ge(rot_done, 2 * (t + 1))
                q = q_nat[:, t, 0:G * HD].rearrange("p (s w) -> p s w", w=HD)
                qv = c.qx0[:, t, :, :].rearrange("p i (e w) -> p (i e) w", w=SR)
                q_hi, q_lo, q_third = (qv[:, :, HD * n:HD * (n + 1)] for n in range(3))
                k = kv_nat[:, t, 0:HD]
                k_hi, k_second, k_lo = (c.kx[:, t, SR + HD * n:SR + HD * (n + 1)] for n in range(3))
                for out, value in ((q_hi, q), (q_third, q), (k_hi, k), (k_second, k)):
                    nc.gpsimd.tensor_copy(out.bitcast(F32R), value).then_inc(stack_hi, 1)
                nc.gpsimd.tensor_copy(c.v1[0][:, t, 0:HD], kv_nat[:, t, v_from:v_from + HD]).then_inc(stack_done, 1)
                pool.wait_ge(stack_hi, 4 * (t + 1))
                nc.gpsimd.tensor_tensor(q_lo.bitcast(F32R), q, q_hi, ALU.subtract).then_inc(stack_done, 1)
                nc.gpsimd.tensor_tensor(k_lo.bitcast(F32R), k, k_hi, ALU.subtract).then_inc(stack_done, 1)

        @block.scalar
        def _(act):
            for t in range(TH):
                norm.upper(act, t)

        @block.vector
        def _(dve):
            def take(t):
                if t == 0:
                    dve.wait_ge(extra_in, 16)
                dve.wait_ge(q_done, t + 1)
                dve.wait_ge(kv_done, t + 1)
                if bias_dram is not None:
                    for out, ps, a, b in ((q_nat[:, t, 0:cut], q_ps[t % 2][:, 0:cut], 0, cut),
                                          (q_nat[:, t, cut:D], kv_ps[t % 2][:, 0:D - cut], cut, D),
                                          (kv_nat[:, t, :], kv_ps[t % 2][:, D - cut:nw - cut], D, nw)):
                        nc.vector.tensor_tensor(out, ps, bias[:, a:b], ALU.add).then_inc(taken, 1)
                    return
                kw = kvw // 2
                qh = q_ps[t % 2].rearrange("p (h d) -> p h d", d=HD)
                kh = kv_ps[t % 2][:, 0:kw].rearrange("p (h d) -> p h d", d=HD)
                qo = q_nat[:, t, :].rearrange("p (h d) -> p h d", d=HD)
                ko = kv_nat[:, t, 0:kw].rearrange("p (h d) -> p h d", d=HD)
                half = HD // 2
                if t >= 1:
                    dve.wait_ge(rot_done, 2 * t)
                for src, out, lo, n in ((qh, qo, 0, H), (kh, ko, H, HKV1)):
                    def table(which, a, b):
                        return rope[:, t, which, a:b].unsqueeze(1).to_broadcast((P, n, b - a))
                    nc.vector.tensor_tensor(out, src, table(0, 0, HD), ALU.mult).then_inc(half_done, 1)
                    for a in (0, half):
                        b = half - a
                        nc.vector.tensor_tensor(swap[:, lo:lo + n, a:a + half], src[:, :, b:b + half],
                                                table(1, a, a + half), ALU.mult).then_inc(half_done, 1)
                nc.vector.tensor_copy(kv_nat[:, t, kw:kvw], kv_ps[t % 2][:, kw:kvw]).then_inc(taken, 1)
                dve.wait_ge(half_done, 6 * (t + 1))
                nc.vector.tensor_tensor(qo, qo, swap[:, 0:H, :], ALU.add).then_inc(rot_done, 1)
                nc.vector.tensor_tensor(ko, ko, swap[:, H:, :], ALU.add).then_inc(rot_done, 1)

            norm.scales(dve)
            norm.tile(dve, 0)
            norm.tile(dve, 1)
            take(0)
            norm.lower(dve, 0)
            norm.tile(dve, 2)
            norm.lower(dve, 1)
            norm.tile(dve, 3)
            take(1)
            norm.lower(dve, 2)
            norm.lower(dve, 3)
            for t in range(2, TT):
                take(t)

        @block.tensor
        def _(pe):
            taken_per_tile = 3 if bias_dram is not None else 1

            def project(t):
                tok = slice(t * P, (t + 1) * P)
                if t >= TH:
                    pe.wait_ge(norm.lo_done, t - TH + 1)
                if t >= 2:
                    pe.wait_ge(taken, taken_per_tile * (t - 1))
                for out, cols, done in ((q_ps[t % 2][:, 0:cut], slice(0, cut), q_done),
                                        (kv_ps[t % 2][:, 0:nw - cut], slice(cut, nw), kv_done)):
                    for c in range(KC):
                        nc.tensor.matmul(out, xt_hi[:, c, tok], w_hi[:, c, cols], start=c == 0, stop=False)
                        nc.tensor.matmul(out, xt_hi[:, c, tok], w_lo[:, c, cols], start=False, stop=False)
                        mm = nc.tensor.matmul(out, xt_lo[:, c, tok], w_hi[:, c, cols], start=False,
                                              stop=c == KC - 1)
                    mm.then_inc(done, 1)

            project(0)
            project(1)
            norm.transpose(pe, 0)
            norm.transpose(pe, 1)
            project(2)
            norm.transpose(pe, 2)
            norm.transpose(pe, 3)
            for t in range(3, TT):
                project(t)
    ph.close()


def output_phase(nc, name, c, w13_dram, scale):
    ph = Phase(nc, name, c.after_w13, c.bias_at)
    x, ao, w_hi, w_lo = c.x, c.ao, c.wo_hi, c.wo_lo
    at_hi = ph.sb("at_hi", [P, KC, T], F32R)
    at_lo = ph.sb("at_lo", [P, KC, T], F32R)
    bank = [ph.ps(f"bank{b}", [P, 4, P]) for b in range(6)]
    turn = bank[0:2]
    out = [b[:, :, :].rearrange("p a b -> p (a b)") for b in bank[2:4]]
    s = TurnSems(ph)
    norm = Norm(nc, ph, c, 0, bank[4:6])
    first = FirstBlocks(nc, ph, c, w13_dram, scale)
    y_done, x_done = ph.sem("y_done"), ph.sem("x_done")

    with nc.Block() as block:
        @block.sync
        def _(sp):
            for b in range(READY):
                first.load(sp, b)

        @block.gpsimd
        def _(pool):
            for b in range(READY):
                first.dequantise(pool, b)

        @block.scalar
        def _(act):
            for t in range(TT):
                act.wait_ge(s.turned, t + 1)
                nc.scalar.activation(at_hi[:, :, t * P:(t + 1) * P], turn[t % 2][:, :, :],
                                     ACT.Copy).then_inc(s.hi, 1)
                if t in (3, 4):
                    first.upper(act, t - 3)
            for t in range(TH):
                norm.upper(act, t)

        @block.vector
        def _(dve):
            def lower(t):
                dve.wait_ge(s.hi, t + 1)
                nc.vector.tensor_tensor(at_lo[:, :, t * P:(t + 1) * P], turn[t % 2][:, :, :],
                                        at_hi[:, :, t * P:(t + 1) * P].bitcast(F32),
                                        ALU.subtract).then_inc(s.lo, 1)

            def add(t):
                dve.wait_ge(y_done, t + 1)
                nc.vector.tensor_tensor(x[:, t, :], x[:, t, :], out[t % 2], ALU.add).then_inc(x_done, 1)

            lower(0)
            lower(1)
            for t in range(TT):
                add(t)
                if t + 2 < TT:
                    lower(t + 2)
                if t in (1, 2):
                    first.lower(dve, t - 1)
                if t < TH:
                    dve.wait_ge(x_done, t + 1)
                    norm.stats(dve, t)
                if t == 3:
                    norm.moments(dve)
                    for n in range(3):
                        norm.newton(dve, n)
                    norm.tile(dve, 0)
                    norm.tile(dve, 1)
                if t in (5, 6):
                    norm.lower(dve, t - 5)
                    norm.tile(dve, t - 3)
            norm.lower(dve, 2)
            norm.lower(dve, 3)

        @block.tensor
        def _(pe):
            def turn_tile(t):
                if t >= 2:
                    pe.wait_ge(s.lo, t - 1)
                for k in range(KC):
                    last = nc.tensor.transpose(turn[t % 2][:, k, :], ao[:, t, k * P:(k + 1) * P], c.ident[:, :])
                last.then_inc(s.turned, 1)
            turn_tile(0)
            turn_tile(1)
            for t in range(TT):
                if t >= 2:
                    pe.wait_ge(x_done, t - 1)
                pe.wait_ge(s.lo, t + 1)
                tok = slice(t * P, (t + 1) * P)
                for k in range(KC):
                    nc.tensor.matmul(out[t % 2], at_hi[:, k, tok], w_hi[:, k, :], start=k == 0, stop=False)
                    nc.tensor.matmul(out[t % 2], at_hi[:, k, tok], w_lo[:, k, :], start=False, stop=False)
                    mm = nc.tensor.matmul(out[t % 2], at_lo[:, k, tok], w_hi[:, k, :], start=False,
                                          stop=k == KC - 1)
                mm.then_inc(y_done, 1)
                if t + 2 < TT:
                    turn_tile(t + 2)
                if t >= 5:
                    norm.transpose(pe, t - 5)
            norm.transpose(pe, 3)
    ph.close()


PLACES = {
    "L0": dict(early=(0, 0, 1, 2, 3, 4, 4, 5, 6, 7, 8, 8, 9, 10, 11, 12),
               late=(17, 18, 20, 21, 23, 25, 26, 28, 29, 30, 32, 34, 36, 38, 39, 41),
               turns=(1, 4, 6, 8, 10, 12, 14, 24, 27, 29, 32, 38, 39, 42), before=(3, 3),
               out=20, product=0, last=45,
               first_turns=(1, 4, 7, 10, 17, 18, 22, 26, 28, 30), first_b=20, pace=3),
    "L1": dict(early=(0, 0, 1, 2, 3, 4, 5, 6, 7, 8, 9, 10, 11, 12, 12, 13),
               late=(17, 18, 20, 22, 23, 25, 27, 29, 31, 32, 33, 35, 37, 38, 40, 42),
               turns=(1, 4, 6, 8, 10, 12, 14, 24, 27, 29, 32, 35, 39, 42), before=(0, 0),
               out=20, product=0, last=46,
               first_turns=(1, 4, 7, 10, 17, 18, 22, 26, 28, 30), first_b=20, pace=3),
}


def attend_phase(nc, name, c, layer, wo_dram, bo_dram):
    ph = Phase(nc, name, c.after_stacks, c.bias_at)
    RING = 8
    ident, ident_b, causal, q_nat, kv_nat, ao = c.ident, c.ident_b, c.causal, c.q_nat, c.kv_nat[layer], c.ao
    sparse = layer == "L1"
    wo_in, bo_in, biased = ph.sem("wo_in"), ph.sem("bo_in"), ph.sem("biased")
    wo_hi_done, wo_lo_done = ph.sem("wo_hi_done"), ph.sem("wo_lo_done")
    kvw = kv_nat.shape[2]
    KSET = 2 if sparse else 1
    kx, v1 = c.kx, c.v1
    qx = [c.qx0, ph.sb("qx1", [P, TT, 2, 2 * SR])]
    qs = [[ph.sb(f"qs{p}{i}", [MR + 4, T], F32R) for i in range(2)] for p in range(2)]
    ks = [[ph.sb(f"ks{p}{e}", [MR + 4, T], F32R) for e in range(2)] for p in range(KSET)]
    mx = [ph.sb(f"mx{p}", [P, TT, G, 8]) for p in range(2)]
    nm = [ph.sb(f"nm{p}", [P, TT, G, 2]) for p in range(2)]
    pt = [[ph.sb(f"pt{s}{a}", [P, HALF]) for a in range(G)] for s in range(2)]
    ot_sb = ph.sb("ot_sb", [P, HALF])
    rden = ph.sb("rden", [P, TH, G])
    if sparse:
        cm = [ph.sb(f"cm{r}", [P, NCH]) for r in range(4)]
        cr = [ph.sb(f"cr{r}", [P, NCH]) for r in range(RING)]
        drop = [ph.sb(f"drop{r}", [P, NCH], BF16) for r in range(2)]
        mark = ph.sb("mark", [P, 1])
        idle = ph.sb("idle", [P, 1])
        settled = ph.sem("settled")
        spare = ph.sb("spare", [P, 1])
        spared = ph.sem("spared")
        price = ph.sb("price", [P, (TT - 2) * P], BF16)
        mk = [[[ph.sb(f"mk{p}{a}{t}", [P, (t - 1) * P], BF16) for t in range(2, TT)] for a in range(G)]
              for p in range(2)]
        top_done, cr_done = ph.sem("top_done"), ph.sem("cr_done")
        drop_done, mk_done = ph.sem("drop_done"), ph.sem("mk_done")

    sa = [ph.ps(f"sa{r}", [P, T]) for r in range(2)]
    sb = [ph.ps(f"sb{r}", [P, HALF]) for r in range(2)]
    ot = ph.ps("ot", [P, HALF])
    tr = ph.ps("tr", [P, TH, P])

    const_done = ph.sem("const_done")
    mask_const = ph.sem("mask_const")
    qx_done, kx_done, v1_done = ph.sem("qx_done"), ph.sem("kx_done"), ph.sem("v1_done")
    tr_done, tr_free = ph.sem("tr_done"), ph.sem("tr_free")
    sa_done, max_done = ph.sem("sa_done"), ph.sem("max_done")
    nm_hi, nm_done = ph.sem("nm_hi"), ph.sem("nm_done")
    sb_done, exp_done, av_done = ph.sem("sb_done"), ph.sem("exp_done"), ph.sem("av_done")
    ot_out, rden_done = ph.sem("ot_out"), ph.sem("rden_done")

    NSTEP = sum(4 * g + 4 for g in range(NH))
    STEPS = [(g, kb) for g in range(NH) for kb in range(4 * g + 4)]
    NG = H // G
    NA = TT * G
    NB = NSTEP * G
    A_UNITS = [(t, a) for t in range(TT) for a in range(G)]
    LATE = [(t, a) for t, a in A_UNITS if t >= 2]
    B0 = 4 * G

    place = PLACES[layer]

    def slot_items(n=None):
        after = {v: [] for v in range(NB)}
        for v in range(NA // 2):
            after[place["early"][v]].append(("a", v))
            after[place["late"][v]].append(("a", NA // 2 + v))
        after[place["last"]].append(("s",))
        after[place["before"][0]].append(("w", -1, NSTEP - 1))
        after[place["before"][1]].append(("o", -1, 1))
        for v, use in zip(place["turns"], (("m", 0, 1, 0), ("m", 0, 1, 1), ("f", -1, 1), ("q", 1, 1, 0),
                                           ("q", 1, 1, 1), ("k", 1, 1, 0), ("k", 1, 1, 1), ("f", 0, 0),
                                           ("q", 2, 0, 0), ("q", 2, 0, 1), ("m", 1, 0, 0), ("m", 1, 0, 1),
                                           ("k", 2, 0, 0), ("k", 2, 0, 1))):
            after[v].append(use)
        after[place["out"]].append(("o", 0, 0))
        for s in range(NSTEP - 1):
            after[G * s + 2 * G - 1 + place["product"]].append(("w", 0, s))
        items = []
        for v in range(NB):
            items += [("b", 0, v)] + after[v]
        if n == 0:
            items = [x for x in items if not begun(x)]
        return kept(items, n)

    def begun(x):
        return x[0] == "b" and x[2] < B0 or x[0] == "w" and x[1] == 0 and G * x[2] + 2 * G <= B0

    def group_of(item):
        return 1 if item[0] in "as" else item[1]

    def kept(items, n):
        return [x for x in items if (sparse or x[0] != "k") and (n is None or 0 <= n + group_of(x) < NG)]

    def first_items():
        items = [("k", 1, 0, 0), ("q", 1, 0, 0), ("k", 1, 0, 1), ("q", 1, 0, 1)]
        uses_at = dict(zip(place["first_turns"], (("q", 1, 1, 0), ("q", 1, 1, 1), ("k", 1, 1, 0), ("k", 1, 1, 1),
                                                  ("m", 1, 0, 0), ("m", 1, 0, 1), ("q", 2, 0, 0), ("q", 2, 0, 1),
                                                  ("k", 2, 0, 0), ("k", 2, 0, 1))))
        units = iter(range(B0))

        def some_b(count):
            for _, v in zip(range(count), units):
                items.append(("b", 1, v))
                s, a = divmod(v - 2 * G + 1, G)
                if s >= 0 and a == 0:
                    items.append(("w", 1, s))
        for v in range(NA):
            items.append(("a", v))
            if v in uses_at:
                items.append(uses_at[v])
            if v >= place["first_b"]:
                some_b(2 if v % place["pace"] == place["pace"] - 1 else 1)
        items.append(("s",))
        some_b(B0)
        return kept(items, -1)

    last_items = [("w", -1, NSTEP - 1), ("o", -1, 1), ("f", -1, 1)]

    def is_use(x):
        return x[0] in "kqmf"

    def uses(items):
        return sum(is_use(x) for x in items)

    EARLY_TURNS = 4 + (0 if sparse else 2 * NH - 2)
    early_banks = [tr[:, :, :]] + [b[:, :].rearrange("p (t w) -> p t w", w=P) for b in [ot] + sb]

    def turn_bank(u, edge):
        return early_banks[u % 4] if edge and u < EARLY_TURNS else tr

    K_ONCE = 0 if sparse else 2 * NH
    U_FIRST, U_SLOT = K_ONCE + uses(first_items()), uses(slot_items())

    def use_base(n, edge):
        if edge and n <= 0:
            return U_FIRST if n == 0 else K_ONCE
        if edge and n > NG - 2:
            return U_FIRST + sum(uses(slot_items(m)) for m in range(n))
        return n * U_SLOT + (U_FIRST - 1)

    def at(items, base, item):
        return base + uses(items[:items.index(item) + 1])

    def over_slots(eng, slot):
        slot(-1, 1, first_items(), use_base(-1, True), True)
        for n in range(2):
            slot(n, n, slot_items(n), use_base(n, True), True)
        with eng.Fori(1, NG // 2 - 1) as i:
            for p in range(2):
                slot(2 * i + p, p, slot_items(), use_base(2 * i + p, False), False)
        for n in range(NG - 2, NG):
            slot(n, n % 2, slot_items(n), use_base(n, True), True)
        slot(NG, 0, last_items, use_base(NG, True), True)

    def known(n, edge, m):
        return edge and n == m

    def narrow(n, edge, v):
        return edge and n <= 0 and v < NA // 2

    def scores_of(n, edge, v):
        c = HALF * (v // 2 % 2) if narrow(n, edge, v) else 0
        return sa[v % 2][:, c:c + (TH * P if v < NA // 2 else T)]

    def wide(n, edge, v):
        return v < B0 and not known(n, edge, 0) or known(n, edge, NG - 1)

    def bank_of(n, edge, v):
        return (sb + [s[:, HALF:T] for s in sa])[v % 4] if wide(n, edge, v) else sb[v % 2][:, :]

    def last_user(n, edge, v):
        if v in (2, 3) and wide(n, edge, v):
            return None
        return v - 4 if v >= 4 and (wide(n, edge, v) or B0 <= v < B0 + 2 and wide(n, edge, 0)) else v - 2

    C_ALL = 2 * KSET

    with nc.Block() as block:
        @block.sync
        def _(sp):
            sp.dma_start(c.wo_raw[:, :, :], wo_dram).then_inc(wo_in, 16)
            if bo_dram is not None:
                sp.dma_start(c.bo[:, :], bo_dram.to_broadcast((P, D))).then_inc(bo_in, 16)

        @block.gpsimd
        def _(pool):
            def prepare_q(m, p, base):
                if base is not None:
                    pool.wait_ge(tr_done, base)
                src = q_nat[:, :, bass.ds(m * (G * HD), G * HD)].rearrange("p t (s w) -> p t s w", w=HD)
                v = qx[p][:, :, :, :].rearrange("p t i (e w) -> p t (i e) w", w=SR)
                hi, lo, third = (v[:, :, :, HD * c:HD * (c + 1)] for c in range(3))
                nc.gpsimd.tensor_copy(hi.bitcast(F32R), src).then_inc(qx_done, 1)
                nc.gpsimd.tensor_copy(third, src).then_inc(qx_done, 1)
                pool.wait_ge(qx_done, 4 * (m - 1) + 2)
                nc.gpsimd.tensor_tensor(lo.bitcast(F32R), third, hi, ALU.subtract).then_inc(qx_done, 1)
                pool.wait_ge(qx_done, 4 * (m - 1) + 3)
                nc.gpsimd.tensor_tensor(third.bitcast(F32R), third, lo, ALU.subtract).then_inc(qx_done, 1)

            def prepare_k(m, base):
                if base is not None:
                    pool.wait_ge(tr_done, base)
                src = kv_nat[:, :, bass.ds(m * HD, HD)]
                hi, second, lo = (kx[:, :, SR + HD * c:SR + HD * (c + 1)] for c in range(3))
                nc.gpsimd.tensor_copy(hi.bitcast(F32R), src).then_inc(kx_done, 1)
                nc.gpsimd.tensor_copy(second.bitcast(F32R), src).then_inc(kx_done, 1)
                nc.gpsimd.tensor_copy(lo, src).then_inc(kx_done, 1)
                pool.wait_ge(kx_done, 4 * (m - 1) + 3)
                nc.gpsimd.tensor_tensor(lo.bitcast(F32R), lo, hi, ALU.subtract).then_inc(kx_done, 1)

            def prepare_v(m, p, wait):
                if wait:
                    pool.wait_ge(av_done, NSTEP * (m - 1))
                src = kv_nat[:, :, bass.ds(m * HD + kvw // 2, HD)]
                nc.gpsimd.tensor_copy(v1[p][:, :, 0:HD], src).then_inc(v1_done, 1)

            def masks(m, p, wait, u0=0, u1=len(LATE) + 1):
                base = len(LATE) * m
                for u in range(u0, u1):
                    if u == 0 and wait:
                        pool.wait_ge(sb_done, NB * (m - 1))
                    if u < len(LATE):
                        pool.wait_ge(cr_done, base + u + 1)
                    if u >= 2:
                        pool.wait_ge(mk_done, base + u - 1)
                    if u == 0:
                        nc.gpsimd.tensor_tensor(spare[:, :], mark[:, :], mark[:, :], ALU.subtract).then_inc(spared, 1)
                    else:
                        t, a = LATE[u - 1]
                        nch = 8 * t
                        pool.wait_ge(drop_done, base + u)
                        nc.gpsimd.tensor_tensor(
                            mk[p][a][t - 2][:, :].rearrange("p (c w) -> p c w", w=CHUNK),
                            drop[(u - 1) % 2][:, 8:nch].unsqueeze(2).to_broadcast((P, nch - 8, CHUNK)),
                            price[:, (TT - 1 - t) * P:].rearrange("p (c w) -> p c w", w=CHUNK),
                            ALU.mult).then_inc(mk_done, 1)
                    if u < len(LATE):
                        nch = 8 * LATE[u][0]
                        nc.gpsimd.tensor_scalar(drop[u % 2][:, 8:nch], cr[u % RING][:, 8:nch], MARK, None,
                                                ALU.is_lt).then_inc(drop_done, 1)

            if sparse:
                nc.gpsimd.memset(mark[:, :], MARK).then_inc(mask_const, 1)
                nc.gpsimd.memset(price[:, :], NEG).then_inc(mask_const, 1)
                pool.wait_ge(mask_const, 2)
                nc.gpsimd.affine_select(out=price[:, -P:], in_=price[:, -P:], compare_op=ALU.is_ge, fill=0.0,
                                        base=0, pattern=[[-1, P]], channel_multiplier=1).then_inc(mask_const, 1)
                pool.wait_ge(mask_const, 3)

            def slot(n, p, items, base, edge):
                here = [n + 1 < NG, n + 2 < NG] if edge else [True, True]
                if known(n, edge, -1):
                    prepare_q(1, 1, None)
                    if sparse:
                        masks(0, 0, False, 0, 2 * G)
                        prepare_k(1, at(items, base, ("k", 1, 1, 1)))
                        masks(0, 0, False, 2 * G)
                    return
                first = known(n, edge, 0)
                if here[1] and not (sparse and first):
                    prepare_q(n + 2, p, base)
                if sparse and here[0]:
                    prepare_v(n + 1, 1 - p, not first)
                    masks(n + 1, 1 - p, not first, 0, 2 * G)
                    if first:
                        prepare_q(n + 2, p, base)
                    if here[1]:
                        prepare_k(n + 2, at(items, base, ("k", 1, 1, 1)))
                    masks(n + 1, 1 - p, not first, 2 * G)
            over_slots(pool, slot)
            if bo_dram is not None:
                pool.wait_ge(bo_in, 16)
                for t in range(TT):
                    nc.gpsimd.tensor_tensor(c.x[:, t, :], c.x[:, t, :], c.bo[:, :], ALU.add).then_inc(biased, 1)

        @block.tensor
        def _(pe):
            def use(u, edge):
                if edge and u < EARLY_TURNS:
                    if u >= 4:
                        pe.wait_ge(tr_free, u - 3)
                else:
                    pe.wait_ge(tr_free, u)
                return turn_bank(u, edge)

            def turn_k(tr, g, e):
                for t in range(TH):
                    mm = nc.tensor.transpose(tr[0:MR, t, :], kx[:, TH * g + t, SR * (1 - e):SR * (3 - e)], ident[:, :])
                mm.then_inc(tr_done, 1)

            def slot(n, p, items, base, edge):
                pos = base
                for x in items:
                    kind = x[0]
                    if is_use(x):
                        tr = use(pos, edge)
                        pos = pos + 1
                    if kind == "k":
                        if not known(n + x[1], edge, 0):
                            pe.wait_ge(kx_done, 4 * (n + x[1]))
                        turn_k(tr, x[2], x[3])
                    elif kind == "q":
                        _, off, g, i = x
                        if not known(n + off, edge, 0):
                            pe.wait_ge(qx_done, 4 * (n + off))
                        for t in range(TH):
                            mm = nc.tensor.transpose(tr[0:MR, t, :], qx[(p + off) % 2][:, TH * g + t, i, :], ident[:, :])
                        mm.then_inc(tr_done, 1)
                    elif kind == "m":
                        _, off, g, i = x
                        pe.wait_ge(nm_done, NH * (n + off) + g + 1)
                        for t in range(TH):
                            mm = nc.tensor.transpose(
                                tr[0:4, t, :],
                                nm[(p + off) % 2][:, TH * g + t, 2 * i:2 * i + 2, :].rearrange("p a b -> p (a b)"),
                                ident[:, :])
                        mm.then_inc(tr_done, 1)
                    elif kind == "f":
                        _, off, g = x
                        pe.wait_ge(ot_out, NH * (n + off) + g + 1)
                        for t in range(TH):
                            mm = nc.tensor.transpose(tr[:, t, :], ot_sb[:, t * P:(t + 1) * P], ident[:, :])
                        mm.then_inc(tr_done, 1)
                    elif kind == "a":
                        v = x[1]
                        t, a = A_UNITS[v]
                        m, pm = n + 1, (p + 1) % 2
                        k = ks[pm if sparse else 0]
                        if v % (NA // 2) == 0:
                            own = [y for y in items if y[0] in "kq" and y[1] == 1 and y[2] == v // (NA // 2)]
                            pe.wait_ge(tr_free, at(items, base, own[-1]) if own else base)
                        if not narrow(n, edge, v):
                            pe.wait_ge(max_done, NA * m + v - 1)
                        elif v >= 4:
                            pe.wait_ge(max_done, NA * m + v - 3)
                        elif not known(n, edge, -1):
                            pe.wait_ge(max_done, NA * m + v % 2 - 1)
                        if v in (NA // 2, NA // 2 + 1) and not known(n, edge, -1):
                            pe.wait_ge(exp_done, NB * n + B0 - 1 + a % 2)
                        q, w = qs[pm][a // 2][0:MR, t * P:(t + 1) * P], (t + 1) * P
                        out = scores_of(n, edge, v)
                        for c0 in range(0, w, HALF):
                            c1 = min(c0 + HALF, w)
                            nc.tensor.matmul(out[:, c0:c1], q, k[a % 2][0:MR, c0:c1], start=True, stop=c1 < w,
                                             skip_group_check=True)
                        nc.tensor.matmul(out[:, w - P:w], ident_b[:, :], causal[:, :], start=False, stop=True,
                                         skip_group_check=True).then_inc(sa_done, 1)
                    elif kind == "b":
                        _, off, v = x
                        m, pm = n + off, (p + off) % 2
                        s, a = v // G, v % G
                        g, kb = STEPS[s]
                        k = ks[pm if sparse else 0]
                        if known(m, edge, 0) and v == 0:
                            pe.wait_ge(const_done, C_ALL)
                        if v == 0:
                            pe.wait_ge(tr_free, at(items, base, ("m", 1, 0, 1)) if off == 1 else base)
                        if v == B0:
                            pe.wait_ge(tr_free, at(items, base, ("m", 0, 1, 1)))
                        if sparse and (g, kb, a) == (0, 1, 0):
                            pe.wait_ge(mk_done, len(LATE) * m + sum(t < TH for t, _ in LATE))
                        if sparse and v == B0:
                            pe.wait_ge(mk_done, len(LATE) * (m + 1))
                        if v in (2, 3) and wide(m, edge, v):
                            pe.wait_ge(max_done, NA * m + NA + v - 3)
                        elif not (known(m, edge, 0) and v < 2):
                            pe.wait_ge(exp_done, NB * m + last_user(m, edge, v) + 1)
                        late = [t for t in range(TH * g, TH * (g + 1)) if sparse and t >= 2 and 1 <= kb <= t - 1]
                        adds = [(causal[:, :], kb)] if kb >= 4 * g else []
                        adds += [(mk[pm][a][t - 2][:, (kb - 1) * P:kb * P], t) for t in late]
                        c0 = max(0, (kb - 4 * g) * P)
                        out = bank_of(m, edge, v)
                        mm = nc.tensor.matmul(out[:, c0:HALF], k[a % 2][:, kb * P:(kb + 1) * P],
                                              qs[pm][a // 2][:, HALF * g + c0:HALF * (g + 1)], start=True,
                                              stop=not adds, skip_group_check=True)
                        for y, (msk, t) in enumerate(adds):
                            c = t * P - HALF * g
                            mm = nc.tensor.matmul(out[:, c:c + P], msk, ident_b[:, :], start=False,
                                                  stop=y == len(adds) - 1, skip_group_check=True)
                        mm.then_inc(sb_done, 1)
                    elif kind == "w":
                        _, off, s = x
                        g, kb = STEPS[s]
                        m, pm = n + off, (p + off) % 2
                        c0 = max(0, (kb - 4 * g) * P)
                        pe.wait_ge(exp_done, NB * m + G * (s + 1))
                        if kb == 0 and not (known(m, edge, 0) and g == 0):
                            pe.wait_ge(ot_out, NH * m + g)
                        if s == 0 and sparse and not known(m, edge, 0):
                            pe.wait_ge(v1_done, m)
                        for a in range(G):
                            mm = nc.tensor.matmul(ot[32 * a:32 * a + 32, c0:HALF],
                                                  v1[pm if sparse else 0][:, kb, :], pt[s % 2][a][:, c0:HALF],
                                                  start=kb == 0, stop=kb == 4 * g + 3, skip_group_check=True)
                        mm.then_inc(av_done, 1)

            if not sparse:
                for g in range(NH):
                    for e in range(2):
                        turn_k(use(2 * g + e, True), g, e)
            over_slots(pe, slot)

        @block.scalar
        def _(act):
            def rows(dst, src, u):
                act.wait_ge(tr_done, u + 1)
                nc.scalar.activation(dst, src, ACT.Copy).then_inc(tr_free, 1)

            def half_of(stack, r0, r1, g):
                return stack[r0:r1, g * HALF:(g + 1) * HALF].rearrange("p (t w) -> p t w", w=P)

            def slot(n, p, items, base, edge):
                pos = base
                for x in items:
                    kind = x[0]
                    tr = turn_bank(pos, edge)
                    if known(n, edge, NG - 1) and x == ("b", 0, NB // 2):
                        act.wait_ge(wo_in, 16)
                        act.wait_ge(qx_done, 4 * (NG - 1))
                        nc.scalar.activation(c.wo_hi[:, :, :], c.wo_raw[:, :, :], ACT.Copy).then_inc(wo_hi_done, 1)
                    if kind == "k":
                        rows(half_of(ks[(p + x[1]) % 2][x[3]], 0, MR, x[2]), tr[0:MR, :, :], pos)
                    elif kind == "q":
                        rows(half_of(qs[(p + x[1]) % 2][x[3]], 0, MR, x[2]), tr[0:MR, :, :], pos)
                    elif kind == "m":
                        rows(half_of(qs[(p + x[1]) % 2][x[3]], MR, MR + 4, x[2]), tr[0:4, :, :], pos)
                    elif kind == "b":
                        _, off, v = x
                        m = n + off
                        s, a = v // G, v % G
                        g, kb = STEPS[s]
                        c0 = max(0, (kb - 4 * g) * P)
                        act.wait_ge(sb_done, NB * m + v + 1)
                        if a == 0 and not (known(m, edge, 0) and s < 2):
                            act.wait_ge(av_done, NSTEP * m + s - 1)
                        nc.scalar.activation(pt[s % 2][a][:, c0:HALF], bank_of(m, edge, v)[:, c0:HALF], ACT.Exp,
                                             scale=HD ** -0.5).then_inc(exp_done, 1)
                    if is_use(x):
                        pos = pos + 1

            if not sparse:
                for g in range(NH):
                    for e in range(2):
                        rows(half_of(ks[0][e], 0, MR, g), turn_bank(2 * g + e, True)[0:MR, :, :], 2 * g + e)
            over_slots(act, slot)

        @block.vector
        def _(dve):
            for pair in ks:
                for e, k in enumerate(pair):
                    nc.vector.tensor_copy(k[MR:MR + 4, :],
                                          c.sel[MR:MR + 4, e:e + 1].to_broadcast((4, T))).then_inc(const_done, 1)
            if sparse:
                dve.wait_ge(mask_const, 3)

            def late_of(v):
                return LATE.index(A_UNITS[v]) if 0 <= v < NA and A_UNITS[v] in LATE else None

            def chunk_maxima(m, start, scores, v):
                t, a = A_UNITS[v]
                unit = NA * m + v
                if not (start and v == 0):
                    dve.wait_ge(max_done, unit)
                if not (start and v < 2):
                    dve.wait_ge(top_done, unit - 1)
                u = late_of(v - 2)
                if u is not None and not (start and u < RING):
                    dve.wait_ge(drop_done, len(LATE) * m + u + 1 - RING)
                if late_of(v - 4) is not None:
                    dve.wait_ge(cr_done, len(LATE) * m + late_of(v - 4) + 1)
                dve.wait_ge(sa_done, unit + 1)
                nc.vector.tensor_reduce(cm[v % 4][:, 0:8 * t + 8],
                                        scores[:, 0:(t + 1) * P].rearrange("p (c w) -> p c w", w=CHUNK),
                                        AX.X, ALU.max).then_inc(max_done, 1)

            def largest(pm, v):
                t, a = A_UNITS[v]
                nc.vector.max(mx[pm][:, t, a, :], cm[v % 4][:, 0:8 * t + 8]).then_inc(top_done, 1)

            def match(pm, v):
                t, a = A_UNITS[v]
                if (t, a) in LATE:
                    nc.vector.match_replace(out=cr[late_of(v) % RING][:, 0:8 * t + 8],
                                            in_to_replace=mx[pm][:, t, a, :], in_values=cm[v % 4][:, 0:8 * t + 8],
                                            imm_value=MARK).then_inc(cr_done, 1)

            def settle(m, v):
                dve.wait_ge(max_done, NA * m + NA)
                dve.wait_ge(top_done, NA * m + v - 1)
                dve.wait_ge(drop_done, len(LATE) * m + late_of(v - 2) + 1 - RING)
                nc.vector.tensor_copy(idle[:, :], mark[:, :]).then_inc(settled, 1)

            def split_maxima(m, pm, g):
                top = mx[pm][:, TH * g:TH * (g + 1), :, 0]
                out = nm[pm][:, TH * g:TH * (g + 1), :, :]
                dve.wait_ge(top_done if sparse else max_done, NA * m + G * TH * (g + 1))
                nc.vector.tensor_scalar(out[:, :, :, 0].bitcast(F32R), top, -1.0, None, ALU.mult).then_inc(nm_hi, 1)
                dve.wait_ge(nm_hi, NH * m + g + 1)
                nc.vector.scalar_tensor_tensor(out[:, :, :, 1].bitcast(F32R), top, -1.0, out[:, :, :, 0],
                                               ALU.mult, ALU.subtract).then_inc(nm_done, 1)

            def slot(n, p, items, base, edge):
                m, pm = n + 1, (p + 1) % 2
                start = known(n, edge, -1)
                pos = base
                for x in items:
                    kind = x[0]
                    if known(n, edge, NG - 1) and x == ("b", 0, NB // 2 + 4):
                        dve.wait_ge(wo_hi_done, 1)
                        nc.vector.tensor_tensor(c.wo_lo[:, :, :], c.wo_raw[:, :, :], c.wo_hi[:, :, :].bitcast(F32),
                                                ALU.subtract).then_inc(wo_lo_done, 1)
                    if kind == "a" and sparse:
                        v = x[1]
                        chunk_maxima(m, start, scores_of(n, edge, v), v)
                        if v >= 1:
                            largest(pm, v - 1)
                        if v >= 2:
                            match(pm, v - 2)
                        if v == NA // 2 + 1:
                            split_maxima(m, pm, 0)
                    elif kind == "a":
                        v = x[1]
                        t, a = A_UNITS[v]
                        dve.wait_ge(sa_done, NA * m + v + 1)
                        nc.vector.tensor_reduce(mx[pm][:, t, a, 0:1], scores_of(n, edge, v)[:, 0:(t + 1) * P], AX.X,
                                                ALU.max).then_inc(max_done, 1)
                        if v == NA // 2 - 1:
                            split_maxima(m, pm, 0)
                    elif kind == "s":
                        if sparse:
                            settle(m, NA)
                            largest(pm, NA - 1)
                            match(pm, NA - 2)
                            settle(m, NA + 1)
                            match(pm, NA - 1)
                        split_maxima(m, pm, 1)
                    elif kind == "o":
                        _, off, g = x
                        dve.wait_ge(av_done, NSTEP * (n + off) + 4 + 8 * g)
                        nc.vector.tensor_copy(ot_sb[:, :], ot[:, :]).then_inc(ot_out, 1)
                    elif kind == "f":
                        _, off, g = x
                        dve.wait_ge(tr_done, pos + 1)
                        heads = tr[:, :, :].rearrange("p t (a w) -> p t a w", w=32)
                        nc.vector.reciprocal(rden[:, :, :], heads[:, :, :, HD]).then_inc(rden_done, 1)
                        dve.wait_ge(rden_done, NH * (n + off) + g + 1)
                        nc.vector.tensor_tensor(
                            ao[:, TH * g:TH * (g + 1),
                               bass.ds((n + off) * (G * HD), G * HD)].rearrange("p t (a w) -> p t a w", w=HD),
                            heads[:, :, :, 0:HD], rden[:, :, :].unsqueeze(3).to_broadcast((P, TH, G, HD)),
                            ALU.mult).then_inc(tr_free, 1)
                    if is_use(x):
                        pos = pos + 1
            over_slots(dve, slot)
    ph.close()


def attention(nc, name, c, t, layer):
    project_phase(nc, f"{name}p", c, layer, t.get(f"{layer}_bqkv"), t["rope"])
    attend_phase(nc, f"{name}s", c, layer, t[f"{layer}_wo"], t.get(f"{layer}_bo"))
    output_phase(nc, f"{name}o", c, t[f"{layer}_w13"], c.scale[layer])


def program(nc, t):
    c = Common(nc)
    load_phase(nc, c, t)
    for n, layer in enumerate(("L0", "L1")):
        weights = (t[f"{layer}_w13"], t[f"{layer}_w2"], c.scale[layer])
        ffn_phase(nc, f"ffn{n}a", c, *weights, next_projection=(t[f"{layer}_wqkv"], c.proj[layer]))
        attention(nc, f"att{n}", c, t, layer)
        ffn_phase(nc, f"ffn{n}b", c, *weights, next_ffn=(t["L1_w13"], c.scale["L1"]) if n == 0 else None,
                  out_dram=t["out"] if n == 1 else None)


def kernel(**inputs):
    import numpy as np
    import concourse.bacc as bacc
    from concourse.bass_utils import run_bass_kernel_spmd

    arrays = {"x": np.ascontiguousarray(inputs["L0_attn_x"].reshape(T, D))}
    for layer in ("L0", "L1"):
        def in_blocks(w):
            return w.reshape(NJ, P, KC, P).transpose(0, 3, 2, 1)
        w1, w3, w2 = (inputs[f"{layer}_ffn_w{n}"] for n in (1, 3, 2))
        s1, s3, s2 = (inputs[f"{layer}_ffn_w{n}_scale"] for n in (1, 3, 2))
        arrays[f"{layer}_w13"] = np.ascontiguousarray(np.concatenate([in_blocks(w1), in_blocks(w3)], axis=2))
        arrays[f"{layer}_w2"] = np.ascontiguousarray(w2.T.reshape(NJ, P, KC, P))
        arrays[f"{layer}_scale"] = np.ascontiguousarray(np.concatenate([s1, s3, s2.T], axis=1))[None]
    def in_chunks(w):
        return np.ascontiguousarray(w.T.reshape(KC, P, -1).transpose(1, 0, 2))
    arrays["L0_wqkv"] = in_chunks(np.concatenate([inputs[f"L0_attn_w{n}_w"] for n in "qkv"]))
    arrays["L0_bqkv"] = np.concatenate([inputs[f"L0_attn_w{n}_b"] for n in "qkv"])[None]
    arrays["L0_wo"] = in_chunks(inputs["L0_attn_wo_w"])
    arrays["L0_bo"] = np.ascontiguousarray(inputs["L0_attn_wo_b"][None])
    arrays["L1_wqkv"] = in_chunks(np.concatenate([inputs[f"L1_attn_w{n}"] for n in "qkv"]))
    arrays["L1_wo"] = in_chunks(inputs["L1_attn_wo"])
    freq = (np.float32(1.0) / np.float32(10000.0) ** (np.arange(0, HD, 2, dtype=np.float32) / np.float32(HD)))
    angle = np.arange(T, dtype=np.float32)[:, None] * freq[None, :].astype(np.float32)
    cos, sin = np.cos(angle), np.sin(angle)
    rope = np.stack([np.concatenate([cos, cos], 1), np.concatenate([-sin, sin], 1)], 1)
    arrays["rope"] = np.ascontiguousarray(rope.reshape(TT, P, 2, HD).transpose(1, 0, 2, 3).astype(np.float32))
    nc = bacc.Bacc("TRN2", target_bir_lowering=False, num_devices=1)
    aps = {n: nc.dram_tensor(f"in_{n}", a.shape, mybir.dt.from_np(a.dtype), kind="ExternalInput").ap()
           for n, a in arrays.items()}
    aps["out"] = nc.dram_tensor("result", (T, D), F32, kind="ExternalOutput").ap()
    program(nc, aps)
    r = run_bass_kernel_spmd(nc, [{f"in_{n}": a for n, a in arrays.items()}], core_ids=[0])
    return r.results[0]["result"].reshape(1, T, D)
```
